# Optimizing a Trainium2 kernel written in Bass

```python
import numpy as np
import jax
import jax.numpy as jnp

def _softmax(x, axis=-1):
    return jax.nn.softmax(x, axis=axis)

def _gelu(x):
    return jax.nn.gelu(x, approximate=True)

def _silu(x):
    return jax.nn.silu(x)

def _sigmoid(x):
    return jax.nn.sigmoid(x)

def _layernorm(x, axis=-1, eps=1e-05):
    m = jnp.mean(x, axis=axis, keepdims=True)
    v = jnp.var(x, axis=axis, keepdims=True)
    return (x - m) / jnp.sqrt(v + eps)

def _scatter_add(tgt, idx, src, axis=0):
    return tgt.at[idx].add(src)

def _segment_sum(src, seg, n):
    return jax.ops.segment_sum(src, seg, n)
kernel_name = 'mk_gnn_ffn_d1_gnn_r8_70698d'

def setup_inputs(seed: int=0):
    np.random.seed(seed)
    _w = jnp.asarray

    def _rec_inputs():
        import jax
        import jax.numpy as jnp
        _gk = jax.random.key(seed)
        x = -8.776e-05 + 1 * jax.random.normal(jax.random.fold_in(_gk, 1), (6250, 256), jnp.float32)
        src = jax.random.randint(jax.random.fold_in(_gk, 2), (100000,), 0, 6250, jnp.int32)
        dst = jnp.minimum((6250 * jax.random.uniform(jax.random.fold_in(_gk, 3), (100000,)) ** 2.0).astype(jnp.int32), 49999)
        _o = jnp.argsort(dst, stable=True)
        src = src[_o]
        dst = dst[_o]
        edge_attr_64 = 0.000151818 + 1.00006 * jax.random.normal(jax.random.fold_in(_gk, 11), (100000, 64), jnp.float32)
        edge_weight = jax.random.uniform(jax.random.fold_in(_gk, 13), (100000,), jnp.float32, 0.0, 4.99999)
        return (x, src, dst, edge_attr_64, edge_weight)
    x, src, dst, edge_attr_64, edge_weight = _rec_inputs()

    def _L0_gnn_setup():
        import jax, jax.numpy as jnp
        import numpy as np
        H = 256
        R = 64
        N = 2500
        E = 40000
        CUTOFF_LO = 0.0
        CUTOFF_UP = 5.0
        LN_EPS = 1e-05

        def _layernorm(x, g, b):
            mu = jnp.mean(x, axis=-1, keepdims=True)
            var = jnp.var(x, axis=-1, keepdims=True)
            return (x - mu) * jax.lax.rsqrt(var + LN_EPS) * g + b

        def _cosine_cutoff(r):
            c = 0.5 * (jnp.cos(r * (jnp.pi / CUTOFF_UP)) + 1.0)
            return c * (r < CUTOFF_UP).astype(r.dtype)
        key = jax.random.key(seed)
        ks = jax.random.split(key, 16)

        def xavier(k, shape):
            fan_in, fan_out = (shape[1], shape[0])
            lim = np.sqrt(6.0 / (fan_in + fan_out))
            return jax.random.uniform(k, shape, jnp.float32, -lim, lim)
        x = jax.random.normal(ks[0], (N, H), jnp.float32)
        edge_index = jax.random.randint(ks[1], (2, E), 0, N, jnp.int64)
        edge_weight = jax.random.uniform(ks[2], (E,), jnp.float32, 0.0, CUTOFF_UP)
        edge_attr = jax.random.normal(ks[3], (E, R), jnp.float32)
        return {'x': x, 'edge_index': edge_index, 'edge_weight': edge_weight, 'edge_attr': edge_attr, 'ln_g': jnp.ones((H,), jnp.float32), 'ln_b': jnp.zeros((H,), jnp.float32), 'Wq': xavier(ks[4], (H, H)), 'bq': jnp.zeros((H,), jnp.float32), 'Wk': xavier(ks[5], (H, H)), 'bk': jnp.zeros((H,), jnp.float32), 'Wv': xavier(ks[6], (H, H)), 'bv': jnp.zeros((H,), jnp.float32), 'Wo': xavier(ks[7], (H, H)), 'bo': jnp.zeros((H,), jnp.float32), 'Wdk': xavier(ks[8], (H, R)), 'bdk': jnp.zeros((H,), jnp.float32), 'Wdv': xavier(ks[9], (H, R)), 'bdv': jnp.zeros((H,), jnp.float32)}
    _L0_gnn_all = _L0_gnn_setup()
    _L0_gnn_in = {k: v for k, v in _L0_gnn_all.items() if k in ('ln_g', 'ln_b', 'Wq', 'bq', 'Wk', 'bk', 'Wv', 'bv', 'Wo', 'bo', 'Wdk', 'bdk', 'Wdv', 'bdv')}
    del _L0_gnn_all

    def _L0_ffn_setup():
        import jax, jax.numpy as jnp
        import numpy as np
        TOP_K = 2
        LN_EPS = 1e-05
        key = jax.random.key(seed)
        ks = jax.random.split(key, 8)
        B, S, D, E, H = (16, 1024, 256, 8, 1024)
        x = jax.random.normal(ks[0], (B, S, D), dtype=jnp.float32)
        Wr = jax.random.normal(ks[1], (D, E), dtype=jnp.float32) * 0.1
        br = jnp.zeros((E,), dtype=jnp.float32)
        ln_g = jnp.ones((E, D), dtype=jnp.float32)
        ln_b = jnp.zeros((E, D), dtype=jnp.float32)
        W1 = jax.random.normal(ks[2], (E, D, H), dtype=jnp.float32) * (1.0 / np.sqrt(D))
        b1 = jnp.zeros((E, H), dtype=jnp.float32)
        W2 = jax.random.normal(ks[3], (E, H, D), dtype=jnp.float32) * (1.0 / np.sqrt(H))
        b2 = jnp.zeros((E, D), dtype=jnp.float32)
        return {'x': x, 'Wr': Wr, 'br': br, 'ln_g': ln_g, 'ln_b': ln_b, 'W1': W1, 'b1': b1, 'W2': W2, 'b2': b2}
    _L0_ffn_all = _L0_ffn_setup()
    _L0_ffn_in = {k: v for k, v in _L0_ffn_all.items() if k in ('Wr', 'br', 'ln_g', 'ln_b', 'W1', 'b1', 'W2', 'b2')}
    del _L0_ffn_all
    return {'x': x, 'src': src, 'dst': dst, 'edge_attr_64': edge_attr_64, 'edge_weight': edge_weight, 'L0_gnn_ln_g': _L0_gnn_in['ln_g'], 'L0_gnn_ln_b': _L0_gnn_in['ln_b'], 'L0_gnn_Wq': _L0_gnn_in['Wq'], 'L0_gnn_bq': _L0_gnn_in['bq'], 'L0_gnn_Wk': _L0_gnn_in['Wk'], 'L0_gnn_bk': _L0_gnn_in['bk'], 'L0_gnn_Wv': _L0_gnn_in['Wv'], 'L0_gnn_bv': _L0_gnn_in['bv'], 'L0_gnn_Wo': _L0_gnn_in['Wo'], 'L0_gnn_bo': _L0_gnn_in['bo'], 'L0_gnn_Wdk': _L0_gnn_in['Wdk'], 'L0_gnn_bdk': _L0_gnn_in['bdk'], 'L0_gnn_Wdv': _L0_gnn_in['Wdv'], 'L0_gnn_bdv': _L0_gnn_in['bdv'], 'L0_ffn_Wr': _L0_ffn_in['Wr'], 'L0_ffn_br': _L0_ffn_in['br'], 'L0_ffn_ln_g': _L0_ffn_in['ln_g'], 'L0_ffn_ln_b': _L0_ffn_in['ln_b'], 'L0_ffn_W1': _L0_ffn_in['W1'], 'L0_ffn_b1': _L0_ffn_in['b1'], 'L0_ffn_W2': _L0_ffn_in['W2'], 'L0_ffn_b2': _L0_ffn_in['b2']}

def reference(x, src, dst, edge_attr_64, edge_weight, L0_gnn_ln_g, L0_gnn_ln_b, L0_gnn_Wq, L0_gnn_bq, L0_gnn_Wk, L0_gnn_bk, L0_gnn_Wv, L0_gnn_bv, L0_gnn_Wo, L0_gnn_bo, L0_gnn_Wdk, L0_gnn_bdk, L0_gnn_Wdv, L0_gnn_bdv, L0_ffn_Wr, L0_ffn_br, L0_ffn_ln_g, L0_ffn_ln_b, L0_ffn_W1, L0_ffn_b1, L0_ffn_W2, L0_ffn_b2):
    import jax
    import jax.numpy as jnp

    def _L0_gnn_ref(x, edge_index, edge_weight, edge_attr, ln_g, ln_b, Wq, bq, Wk, bk, Wv, bv, Wo, bo, Wdk, bdk, Wdv, bdv):
        import jax, jax.numpy as jnp
        import numpy as np
        H = 256
        R = 64
        N = 2500
        E = 40000
        CUTOFF_LO = 0.0
        CUTOFF_UP = 5.0
        LN_EPS = 1e-05

        def _layernorm(x, g, b):
            mu = jnp.mean(x, axis=-1, keepdims=True)
            var = jnp.var(x, axis=-1, keepdims=True)
            return (x - mu) * jax.lax.rsqrt(var + LN_EPS) * g + b

        def _cosine_cutoff(r):
            c = 0.5 * (jnp.cos(r * (jnp.pi / CUTOFF_UP)) + 1.0)
            return c * (r < CUTOFF_UP).astype(r.dtype)
        src = edge_index[0]
        dst = edge_index[1]
        x_norm = _layernorm(x, ln_g, ln_b)
        q = x_norm @ Wq.T + bq
        k = x_norm @ Wk.T + bk
        v = x_norm @ Wv.T + bv
        dk = jax.nn.silu(edge_attr @ Wdk.T + bdk)
        dv = jax.nn.silu(edge_attr @ Wdv.T + bdv)
        q_i = q[dst]
        k_j = k[src]
        v_j = v[src]
        attn = jnp.sum(q_i * k_j * dk, axis=1)
        attn = jax.nn.silu(attn) * _cosine_cutoff(edge_weight)
        msg = v_j * dv * attn[:, None]
        agg = jax.ops.segment_sum(msg, dst, num_segments=x.shape[0])
        out = agg @ Wo.T + bo
        return x + out

    def _L0_ffn_ref(x, Wr, br, ln_g, ln_b, W1, b1, W2, b2):
        import jax, jax.numpy as jnp
        import numpy as np
        TOP_K = 2
        LN_EPS = 1e-05
        B, S, D = x.shape
        N = B * S
        xt = x.reshape(N, D)
        logits = xt @ Wr + br
        probs = jax.nn.softmax(logits, axis=-1)
        top_p, top_idx = jax.lax.top_k(probs, TOP_K)
        weights = top_p / top_p.sum(axis=-1, keepdims=True)
        mu = xt.mean(axis=-1, keepdims=True)
        var = ((xt - mu) ** 2).mean(axis=-1, keepdims=True)
        xn = (xt - mu) * jax.lax.rsqrt(var + LN_EPS)
        xe = xn[None, :, :] * ln_g[:, None, :] + ln_b[:, None, :]
        h = jax.nn.gelu(jnp.einsum('end,edh->enh', xe, W1) + b1[:, None, :], approximate=False)
        y = jnp.einsum('enh,ehd->end', h, W2) + b2[:, None, :]
        y_tok = jnp.transpose(y, (1, 0, 2))
        sel = jnp.take_along_axis(y_tok, top_idx[:, :, None], axis=1)
        out = (weights[:, :, None] * sel).sum(axis=1)
        return out.reshape(B, S, D)
    edge_index = jnp.stack([src, dst])
    x = x + _L0_gnn_ref(_layernorm(x, axis=-1), edge_index, edge_weight, edge_attr_64, L0_gnn_ln_g, L0_gnn_ln_b, L0_gnn_Wq, L0_gnn_bq, L0_gnn_Wk, L0_gnn_bk, L0_gnn_Wv, L0_gnn_bv, L0_gnn_Wo, L0_gnn_bo, L0_gnn_Wdk, L0_gnn_bdk, L0_gnn_Wdv, L0_gnn_bdv)
    x = x + _L0_ffn_ref(_layernorm(x, axis=-1)[None], L0_ffn_Wr, L0_ffn_br, L0_ffn_ln_g, L0_ffn_ln_b, L0_ffn_W1, L0_ffn_b1, L0_ffn_W2, L0_ffn_b2)[0]
    return x

_drawn_inputs = setup_inputs


def setup_inputs(seed=0):
    import zlib

    import numpy as np

    out = dict(_drawn_inputs(seed))
    spreads = {'L0_gnn_ln_g': (1.0, 0.2),
     'L0_gnn_ln_b': (0.0, 0.1),
     'L0_gnn_bq': (0.0, 0.1),
     'L0_gnn_bk': (0.0, 0.1),
     'L0_gnn_bv': (0.0, 0.1),
     'L0_gnn_bo': (0.0, 0.295),
     'L0_gnn_bdk': (0.0, 0.1),
     'L0_gnn_bdv': (0.0, 0.1),
     'L0_ffn_br': (0.0, 0.283),
     'L0_ffn_ln_g': (1.0, 0.6),
     'L0_ffn_ln_b': (0.0, 0.661),
     'L0_ffn_b1': (0.0, 0.651),
     'L0_ffn_b2': (0.0, 0.457)}
    factors = {}
    for name, (base, spread) in spreads.items():
        noise = np.random.default_rng([zlib.crc32(name.encode()), seed]).standard_normal(out[name].shape)
        drawn = base * np.exp(spread * noise) if base else spread * noise
        out[name] = jnp.asarray(drawn.astype(out[name].dtype))
    for name, factor in factors.items():
        out[name] = (out[name] * factor).astype(out[name].dtype)
    return out
```

```python
import math
from contextlib import ExitStack

import concourse.bass as bass
from concourse import mybir

P = 128
N = 6250
E = 100000
D = 256
R = 64
NE = 8
HID = 1024
DC = D // P
KC = HID // P
NT = -(-N // P)
ET = -(-E // P)
EPS = 1e-5
CUT = 5.0

U = 12
PAIRS = U // 2
ITEMS_IT = 2 * U
CH = 120
HALVES_CH = CH // U
MAX_CH = -(-(ET * NT) // CH)
MAX_ITEMS = MAX_CH * CH
MAX_IT = MAX_ITEMS // ITEMS_IT
FULL = ET // P
REST = ET - FULL * P
STS = (2 * NT * P + NE * (P - 1)) // P

F32 = mybir.dt.float32
I32 = mybir.dt.int32
BF16 = mybir.dt.bfloat16
ALU = mybir.AluOpType
ACT = mybir.ActivationFunctionType
AX = mybir.AxisListType.X


def ds(start, size):
    return bass.ds(start, size)


def over_tiles(eng, count, body):
    for t in range(2):
        body(t, t, 0, False)
    with eng.Fori(1, count // 2) as i:
        for s in range(2):
            body(2 * i + s, s, i, False)
    if count % 2:
        body(count - 1, 0, count // 2, True)


def slot_free(eng, sem, n, per=1):
    if not (isinstance(n, int) and n == 0):
        eng.wait_ge(sem, n * per)


class Chain:

    def __init__(self, eng, sem):
        self.eng, self.sem, self.n = eng, sem, 0

    def __call__(self, ins):
        self.n += 1
        ins.then_inc(self.sem, 1)
        self.eng.wait_ge(self.sem, self.n)


def build_program(nc, a, out):
    ctx = ExitStack()
    with ctx:
        def dram(name, shape, dt=F32):
            return nc.dram_tensor(name, shape, dt, kind="Internal").ap()

        kv_table = dram("kv_table", [NT * P, 2 * D])
        res_table = dram("res_table", [NT * P, D])
        range_rows = dram("range_rows", [2, (FULL + 1) * P])
        meta_cols = dram("meta_cols", [MAX_ITEMS // U, P, 3 * U])
        rel_rows = dram("rel_rows", [MAX_ITEMS, P], BF16)
        item_tab = dram("item_tab", [2, MAX_ITEMS], I32)
        slot_x = dram("slot_x", [STS * P, D])
        slot_y = dram("slot_y", [STS * P, D])

        in_use = []

        def named(name):
            in_use.append(nc.alloc_semaphore(name))
            return in_use[-1]

        def next_phase():
            nc.clear_and_free_semaphores(in_use)
            in_use.clear()
            nc.all_engine_barrier()

        def outer(name, shape, dt=F32):
            return ctx.enter_context(nc.sbuf_tensor(name, shape, dt))

        FRONT = NE * KC * D - NT * D + D
        region = outer("region", [P, FRONT + 2 * NT * D])
        ident = outer("ident", [P, P])
        iota_free = outer("iota_free", [P, P])
        iota_part = outer("iota_part", [P, 1])
        ones = outer("ones", [P, P])
        n_run = outer("n_run", [P, 2], I32)
        stats = outer("stats", [P, NT, 6])
        ln_s = outer("ln_s", [P, 8, NT])
        slot_i = outer("slot_i", [P, NT, 2], I32)
        w_top = outer("w_top", [P, NT, 2])
        expert_i = outer("expert_i", [1, STS], I32)
        agg = region[:, FRONT:FRONT + NT * D]
        qx = region[:, FRONT + NT * D:]
        w2 = region[:, 0:NE * KC * D]

        mean, var, rstd, rstd2, bias_r, bias_s, tmp_a, tmp_b = (ln_s[:, k, :] for k in range(8))

        def norm_scales(dve, act_sem, chain, sqrt_sem, step):
            def refine(dst, v):
                chain(dve.reciprocal(dst, tmp_b))
                chain(dve.tensor_tensor(tmp_b, dst, dst, ALU.mult))
                chain(dve.tensor_tensor(tmp_b, tmp_b, tmp_a, ALU.mult))
                chain(dve.tensor_scalar(tmp_b, tmp_b, -0.5, 1.5, ALU.mult, ALU.add))
                chain(dve.tensor_tensor(dst, dst, tmp_b, ALU.mult))

            ev, od = stats[:, :, 1], stats[:, :, 4]
            chain(dve.tensor_tensor(mean, ev, od, ALU.add))
            chain(dve.tensor_scalar(mean, mean, 0.5, None, ALU.mult))
            chain(dve.tensor_tensor(tmp_a, ev, od, ALU.subtract))
            chain(dve.tensor_scalar(tmp_a, tmp_a, 0.5, None, ALU.mult))
            chain(dve.tensor_tensor(tmp_a, tmp_a, tmp_a, ALU.mult))
            chain(dve.tensor_tensor(var, stats[:, :, 2], stats[:, :, 5], ALU.add))
            chain(dve.scalar_tensor_tensor(out=var, in0=var, scalar=1.0 / D, in1=tmp_a, op0=ALU.mult, op1=ALU.add))
            dve.tensor_scalar(tmp_a, var, EPS, None, ALU.add).then_inc(sqrt_sem, 1)
            dve.wait_ge(act_sem, step + 1)
            refine(rstd, tmp_a)
            chain(dve.tensor_tensor(tmp_a, rstd, rstd, ALU.mult))
            chain(dve.tensor_tensor(tmp_a, tmp_a, var, ALU.mult))
            dve.tensor_scalar(tmp_a, tmp_a, EPS, None, ALU.add).then_inc(sqrt_sem, 1)
            dve.wait_ge(act_sem, step + 2)
            refine(rstd2, tmp_a)
            chain(dve.tensor_tensor(rstd2, rstd2, rstd, ALU.mult))
            chain(dve.scalar_tensor_tensor(out=bias_r, in0=mean, scalar=-1.0, in1=rstd, op0=ALU.mult, op1=ALU.mult))
            chain(dve.scalar_tensor_tensor(out=bias_s, in0=mean, scalar=-1.0, in1=rstd2, op0=ALU.mult, op1=ALU.mult))

        def norm_roots(act, act_sem, sqrt_sem):
            for k in range(2):
                act.wait_ge(sqrt_sem, k + 1)
                act.activation(tmp_b, tmp_a, ACT.Sqrt).then_inc(act_sem, 1)

        with ExitStack() as s1:
            def sb(name, shape, dt=F32):
                return s1.enter_context(nc.sbuf_tensor(name, shape, dt))

            def ps(name, shape):
                return s1.enter_context(nc.psum_tensor(name, shape, F32))

            def sem(name):
                return named(name)

            xt = agg.rearrange("p (t d) -> p t d", d=D)
            qt = qx.rearrange("p (t d) -> p t d", d=D)
            wqkv = sb("wqkv", [P, DC, 3 * D])
            g_col = sb("g_col", [P, DC])
            b_col = sb("b_col", [P, DC])
            b_rep = sb("b_rep", [P, DC, P])
            bias_in = sb("bias_in", [1, 3 * D])
            bias_all = sb("bias_all", [P, 3 * D])
            normed = sb("normed", [P, 2, D])
            normed_t = sb("normed_t", [P, 2, D])
            kv_out = sb("kv_out", [P, 2, 2 * D])
            tp = ps("tp", [P, 2, 512])
            proj = ps("proj", [P, 2, 1024])

            s_x = [sem(f"s_x{k}") for k in range(7)]
            s_w = sem("s_w")
            s_bin = sem("s_bin")
            s_const = sem("s_const")
            s_chain = sem("s_chain")
            s_stats = sem("s_stats")
            s_var = sem("s_var")
            s_root = sem("s_root")
            s_scales = sem("s_scales")
            s_fold = sem("s_fold")
            s_bias_mm = sem("s_bias_mm")
            s_bias = sem("s_bias")
            normed_made = [sem(f"normed_made{k}") for k in range(2)]
            res_made = sem("res_made")
            transposed = [sem(f"transposed{k}") for k in range(2)]
            copied = [sem(f"copied{k}") for k in range(2)]
            projected = [sem(f"projected{k}") for k in range(2)]
            evacuated = [sem(f"evacuated{k}") for k in range(2)]
            kv_stored = [sem(f"kv_stored{k}") for k in range(2)]
            gate = sem("gate1")
            s_res = sem("s_res")
            block = s1.enter_context(nc.Block())

            G = NT // 7
            x_rows = a["x"].rearrange("(t p) d -> p t d", p=P)

            @block.sync
            def _(sp):
                for k in range(7):
                    sp.dma_start(xt[:, k * G:(k + 1) * G, :], x_rows[:, k * G:(k + 1) * G, :]).then_inc(s_x[k], 16)
                sp.dma_start(wqkv[:, :, :], a["wqkv_t"].rearrange("(c p) n -> p c n", p=P)).then_inc(s_w, 16)
                sp.dma_start(g_col[:, :], a["gnn_g"]).then_inc(s_w, 16)
                sp.dma_start(b_col[:, :], a["gnn_b"]).then_inc(s_w, 16)
                sp.dma_start(bias_in[:, :], a["bqkv"]).then_inc(s_bin, 16)

                def store(t, s, n, last):
                    sp.wait_ge(evacuated[s], 2 * (n + 1))
                    sp.dma_start(kv_table[ds(t * P, P), :], kv_out[:, s, :]).then_inc(kv_stored[s], 16)

                over_tiles(sp, NT, store)
                sp.wait_ge(res_made, NT)
                sp.dma_start(res_table.rearrange("(t p) d -> p t d", p=P), xt[:, :, :]).then_inc(s_res, 16)
                sp.wait_ge(s_res, 16)
                sp.wait_ge(kv_stored[0], 16 * (NT // 2 + 1))
                sp.wait_ge(kv_stored[1], 16 * (NT // 2))

            @block.gpsimd
            def _(pool):
                c = Chain(pool, s_const)
                c(pool.memset(ones[:, :], 1.0))
                c(pool.affine_select(out=ident[:, :], in_=ones[:, :], compare_op=ALU.is_equal, fill=0.0, base=0,
                                     pattern=[[-1, P]], channel_multiplier=1))
                c(pool.iota(iota_free[:, :], pattern=[[1, P]], base=0, channel_multiplier=0,
                            allow_small_or_imprecise_dtypes=True))
                c(pool.iota(iota_part[:, :], pattern=[[0, 1]], base=0, channel_multiplier=1,
                            allow_small_or_imprecise_dtypes=True))

            @block.scalar
            def _(act):
                norm_roots(act, s_root, s_var)
                act.wait_ge(s_scales, 1)

                def normalise(t, s, n, last):
                    slot_free(act, transposed[s], n)
                    act.sem_inc(gate, 1)
                    act.activation(normed[:, s, :], agg[:, ds(t * D, D)], ACT.Identity, scale=rstd2[:, ds(t, 1)],
                                   bias=bias_s[:, ds(t, 1)]).then_inc(normed_made[s], 1)
                    act.activation(agg[:, ds(t * D, D)], agg[:, ds(t * D, D)], ACT.Identity,
                                   scale=tmp_a[:, ds(t, 1)], bias=bias_r[:, ds(t, 1)]).then_inc(res_made, 1)

                over_tiles(act, NT, normalise)

            @block.vector
            def _(dve):
                c = Chain(dve, s_chain)
                for k in range(7):
                    dve.wait_ge(s_x[k], 16)
                    with dve.Fori(k * G, (k + 1) * G) as t:
                        dve.bn_stats(stats[:, ds(t, 1), :].rearrange("p a b -> p (a b)"), agg[:, ds(t * D, D)]) \
                            .then_inc(s_stats, 1)
                dve.wait_ge(s_stats, NT)
                norm_scales(dve, s_root, c, s_var, 0)
                dve.tensor_scalar(tmp_a, rstd, 1.0, None, ALU.add).then_inc(s_scales, 1)
                dve.wait_ge(s_w, 48)
                dve.wait_ge(s_const, 4)
                for k in range(DC):
                    dve.tensor_scalar(b_rep[:, k, :], ones[:, :], b_col[:, k:k + 1], None, ALU.mult).then_inc(s_fold, 1)
                dve.wait_ge(s_bias_mm, 1)
                for k in range(DC):
                    dve.tensor_scalar(wqkv[:, k, :], wqkv[:, k, :], g_col[:, k:k + 1], None, ALU.mult).then_inc(s_fold, 1)
                dve.tensor_copy(bias_all[:, :], proj[:, 0, 0:3 * D]).then_inc(s_bias, 1)
                dve.wait_ge(s_bias, 1)

                def copy(s, n):
                    slot_free(dve, projected[s], n)
                    dve.wait_ge(transposed[s], n + 1)
                    dve.tensor_copy(normed_t[:, s, :], tp[:, s, 0:D]).then_inc(copied[s], 1)

                def evacuate(t, s, n, last):
                    if not last:
                        copy(1 - s, n + s)
                    slot_free(dve, kv_stored[s], n, 16)
                    dve.wait_ge(projected[s], n + 1)
                    dve.tensor_tensor(kv_out[:, s, :], proj[:, s, 0:2 * D], bias_all[:, 0:2 * D], ALU.add) \
                        .then_inc(evacuated[s], 1)
                    dve.tensor_tensor(qx[:, ds(t * D, D)], proj[:, s, 2 * D:3 * D], bias_all[:, 2 * D:3 * D],
                                      ALU.add).then_inc(evacuated[s], 1)

                copy(0, 0)
                over_tiles(dve, NT, evacuate)

            @block.tensor
            def _(pe):
                pe.wait_ge(s_fold, DC)
                pe.wait_ge(s_w, 48)
                pe.wait_ge(s_bin, 16)
                for lo, hi in ((0, 512), (512, 3 * D)):
                    for k in range(DC):
                        pe.matmul(proj[:, 0, lo:hi], b_rep[:, k, :], wqkv[:, k, lo:hi], start=(k == 0), stop=False)
                    mm = pe.matmul(proj[:, 0, lo:hi], ones[0:1, :], bias_in[:, lo:hi], start=False, stop=True)
                mm.then_inc(s_bias_mm, 1)
                pe.wait_ge(s_fold, 2 * DC)
                pe.wait_ge(s_bias, 1)

                def transposes(s, n):
                    slot_free(pe, copied[s], n)
                    pe.wait_ge(normed_made[s], n + 1)
                    for k in range(DC):
                        mm = pe.transpose(tp[:, s, k * P:(k + 1) * P], normed[:, s, k * P:(k + 1) * P], ident[:, :])
                    mm.then_inc(transposed[s], 1)

                def products(t, s, n, last):
                    if not last:
                        transposes(1 - s, n + s)
                    slot_free(pe, evacuated[s], n, 2)
                    pe.wait_ge(copied[s], n + 1)
                    for lo, hi in ((0, 512), (512, 3 * D)):
                        for k in range(DC):
                            mm = pe.matmul(proj[:, s, lo:hi], normed_t[:, s, k * P:(k + 1) * P], wqkv[:, k, lo:hi],
                                           start=(k == 0), stop=(k == DC - 1))
                    mm.then_inc(projected[s], 1)

                transposes(0, 0)
                over_tiles(pe, NT, products)

        next_phase()

        with ExitStack() as s2:
            def sb(name, shape, dt=F32):
                return s2.enter_context(nc.sbuf_tensor(name, shape, dt))

            def sem(name):
                return named(name)

            dst_rows = sb("dst_rows", [P, FULL + 1, P], I32)
            least = sb("least", [P, 2, FULL + 1])
            block_i = sb("block_i", [P, 2, FULL + 1], I32)
            block_f = sb("block_f", [P, 2, FULL + 1])
            ranges = sb("ranges", [P, 2, ET])
            upto = sb("upto", [P, ET])
            count = sb("count", [P, ET])
            offset = sb("offset", [P, ET])
            ones_row = sb("ones_row", [P, ET])
            iota_row = sb("iota_row", [P, MAX_IT])
            junk = sb("junk", [P, MAX_IT])
            n_f = sb("n_f", [P, 2])
            zero = sb("zero", [P, 7 * D])
            j_col = sb("j_col", [P, 1])
            t_col = sb("t_col", [P, 1])
            o_col = sb("o_col", [P, 1])
            b_col2 = sb("b_col2", [P, 2])
            tab_i = sb("tab_i", [P, 2], I32)
            src_g = sb("src_g", [P, P], I32)
            dst_g = sb("dst_g", [P, P], I32)
            ew_g = sb("ew_g", [P, P])
            ew_turn = sb("ew_turn", [P, P])
            ew_whole = sb("ew_whole", [P, P], I32)
            half_pi = sb("half_pi", [P, 1])
            metas = sb("metas", [P, 3, P])
            rel_b = sb("rel_b", [P, P], BF16)
            meta_out = sb("meta_out", [P, HALVES_CH, 3, U])
            meta_ps = s2.enter_context(nc.psum_tensor("meta_ps", [P, 3, 512], F32))

            s_dst = sem("s_dst")
            s_c2 = sem("s_c2")
            s_pc2 = sem("s_pc2")
            s_blocks = sem("s_blocks")
            s_rng_st = sem("s_rng_st")
            s_rng = sem("s_rng")
            s_iota = sem("s_iota")
            s_zero = sem("s_zero")
            s_zfill = sem("s_zfill")
            s_count = sem("s_count")
            s_link = sem("s_link")
            tiles_known = sem("tiles_known")
            gathered = sem("gathered")
            turn_ready = sem("turn_ready")
            abs_made = sem("abs_made")
            sin_made = sem("sin_made")
            metas_made = sem("metas_made")
            metas_turned = sem("metas_turned")
            meta_copied = sem("meta_copied")
            chunk_stored = sem("chunk_stored")
            chunk_free = sem("chunk_free")
            gate_p = sem("gate_p2")
            gate_a = sem("gate_a2")
            block = s2.enter_context(nc.Block())

            @block.sync
            def _(sp):
                sp.sem_inc(chunk_free, 1)
                sp.dma_start(dst_rows[:, 0:FULL, :],
                             a["dst"][0:FULL * P, :].rearrange("(c p) e -> p c e", p=P)).then_inc(s_dst, 16)
                sp.dma_start(dst_rows[0:REST, FULL, :], a["dst"][FULL * P:ET, :]).then_inc(s_dst, 16)
                sp.wait_ge(s_blocks, 1)
                for k in range(2):
                    with nc.allow_non_contiguous_dma(reason="a column of seven numbers a partition"):
                        sp.dma_start(range_rows[k].rearrange("(c p) -> p c", p=P), block_f[:, k, :]) \
                            .then_inc(s_rng_st, 16)
                sp.wait_ge(s_rng_st, 32)
                sp.dma_start(ranges[:, :, :], range_rows[:, 0:ET].unsqueeze(0).to_broadcast([P, 2, ET])) \
                    .then_inc(s_rng, 16)
                sp.wait_ge(s_count, 1)
                chunks = sp.value_load(n_run[0:1, 1:2], min_val=1, max_val=MAX_CH)
                with sp.Fori(0, chunks) as c:
                    sp.wait_ge(meta_copied, c + 1)
                    sp.dma_start(meta_cols[ds(c * HALVES_CH, HALVES_CH)].rearrange("h p m -> p h m"),
                                 meta_out[:, :, :, :].rearrange("p h k u -> p h (k u)")).then_inc(chunk_stored, 16)
                    sp.dma_start(rel_rows[ds(c * CH, CH), :], rel_b[0:CH, :]).then_inc(chunk_stored, 16)
                    with nc.allow_non_contiguous_dma(reason="one number a partition"):
                        for k in range(2):
                            sp.dma_start(item_tab[k, ds(c * CH, CH)].unsqueeze(1), tab_i[0:CH, k:k + 1]) \
                                .then_inc(chunk_stored, 16)
                    sp.wait_ge(chunk_stored, 64 * c + 64)
                    sp.sem_inc(chunk_free, 1)

            @block.gpsimd
            def _(pool):
                c = Chain(pool, s_pc2)
                pool.iota(iota_row[:, :], pattern=[[1, MAX_IT]], base=0, channel_multiplier=0,
                          allow_small_or_imprecise_dtypes=True).then_inc(s_iota, 1)
                pool.iota(j_col[:, :], pattern=[[0, 1]], base=-CH, channel_multiplier=1,
                          allow_small_or_imprecise_dtypes=True).then_inc(s_iota, 1)
                pool.memset(zero[:, :], 0.0).then_inc(s_zero, 1)
                c(pool.memset(agg, 0.0))
                pool.wait_ge(s_count, 1)
                chunks = pool.value_load(n_run[0:1, 1:2], min_val=1, max_val=MAX_CH)
                with pool.Fori(0, chunks) as k:
                    pool.wait_ge(tiles_known, k + 1)
                    pool.sem_inc(gate_p, 1)
                    for row, name in ((src_g, "src"), (dst_g, "dst"), (ew_g, "edge_weight")):
                        pool.indirect_dma_start(row[0:CH, :], None, a[name],
                                                bass.IndirectOffsetOnAxis(ap=tab_i[0:CH, 0:1], axis=0)) \
                            .then_inc(gathered, 16)

            @block.vector
            def _(dve):
                c = Chain(dve, s_c2)
                c(dve.memset(least[:, :, :], 0.0))
                dve.memset(ones_row[:, :], 1.0).then_inc(s_c2, 1)
                dve.memset(half_pi[:, :], math.pi / 2).then_inc(s_c2, 1)
                c.n += 2
                dve.wait_ge(s_dst, 32)
                for k, op in ((0, ALU.min), (1, ALU.max)):
                    c(dve.tensor_reduce(least[:, k, 0:FULL], dst_rows[:, 0:FULL, :], AX, op))
                    c(dve.tensor_reduce(least[0:REST, k, FULL:FULL + 1], dst_rows[0:REST, FULL, :], AX, op))
                c(dve.tensor_copy(block_i[:, :, :], least[:, :, :]))
                c(dve.tensor_scalar(block_i[:, :, :], block_i[:, :, :], 7, None, ALU.arith_shift_right))
                c(dve.tensor_copy(block_f[:, :, :], block_i[:, :, :]))
                dve.sem_inc(s_blocks, 1)
                dve.wait_ge(s_rng, 16)
                dve.wait_ge(s_iota, 2)
                c(dve.tensor_tensor(count[:, :], ranges[:, 1, :], ranges[:, 0, :], ALU.subtract))
                c(dve.tensor_scalar(count[:, :], count[:, :], 1.0, None, ALU.add))
                c(dve.tensor_tensor_scan(upto[:, :], ones_row[:, :], count[:, :], 0.0, ALU.mult, ALU.add))
                c(dve.tensor_tensor(offset[:, :], ranges[:, 0, :], upto[:, :], ALU.subtract))
                c(dve.tensor_tensor(offset[:, :], offset[:, :], count[:, :], ALU.add))
                for k, n, per, most in ((0, upto[:, ET - 1:ET], ITEMS_IT, MAX_IT),
                                        (1, n_f[:, 0:1], CH // ITEMS_IT, MAX_CH)):
                    c(dve.tensor_scalar(count[:, 0:1], n, 1.0 / per, None, ALU.mult))
                    c(dve.tensor_scalar(junk[:, 0:most], iota_row[:, 0:most], count[:, 0:1], None, ALU.is_lt,
                                        ALU.add, accum_out=n_f[:, k:k + 1]))
                c(dve.tensor_copy(n_run[:, :], n_f[:, :]))
                dve.sem_inc(s_count, 1)
                chunks = dve.value_load(n_run[0:1, 1:2], min_val=1, max_val=MAX_CH)
                LINKS = 13
                with dve.Fori(0, chunks) as k:
                    done = 0

                    def link(ins):
                        nonlocal done
                        done += 1
                        ins.then_inc(s_link, 1)
                        dve.wait_ge(s_link, k * LINKS + done)

                    dve.wait_ge(chunk_free, k + 1)
                    link(dve.tensor_scalar(j_col[:, :], j_col[:, :], float(CH), None, ALU.add))
                    link(dve.tensor_scalar(junk[:, 0:ET - 1], upto[:, 0:ET - 1], j_col[:, 0:1], None, ALU.is_le,
                                           ALU.add, accum_out=t_col[:, :]))
                    link(dve.scalar_tensor_tensor(out=junk[:, 0:ET], in0=iota_row[:, 0:ET], scalar=t_col[:, 0:1],
                                                  in1=offset[:, :], op0=ALU.is_equal, op1=ALU.mult,
                                                  accum_out=o_col[:, :]))
                    link(dve.tensor_tensor(o_col[:, :], o_col[:, :], j_col[:, :], ALU.add))
                    link(dve.tensor_scalar(b_col2[:, 0:1], o_col[:, :], float(NT - 1), None, ALU.min))
                    dve.tensor_copy(tab_i[:, 0:1], t_col[:, :]).then_inc(tiles_known, 1)
                    link(dve.tensor_scalar(b_col2[:, 1:2], o_col[:, :], float(P), None, ALU.mult))
                    link(dve.tensor_copy(tab_i[:, 1:2], b_col2[:, 0:1]))
                    dve.wait_ge(gathered, 48 * k + 48)
                    link(dve.tensor_scalar(ew_turn[0:CH, :], ew_g[0:CH, :], 0.5 / CUT, None, ALU.mult))
                    link(dve.tensor_copy(ew_whole[0:CH, :], ew_turn[0:CH, :]))
                    dve.tensor_tensor(ew_turn[0:CH, :], ew_turn[0:CH, :], ew_whole[0:CH, :], ALU.subtract) \
                        .then_inc(turn_ready, 1)
                    dve.tensor_copy(metas[0:CH, 0, :], src_g[0:CH, :]).then_inc(metas_made, 1)
                    link(dve.tensor_scalar(metas[0:CH, 1, :], dst_g[0:CH, :], b_col2[0:CH, 1:2], -1.0,
                                           ALU.subtract, ALU.max))
                    link(dve.tensor_scalar(metas[0:CH, 1, :], metas[0:CH, 1, :], float(P), None, ALU.min))
                    dve.tensor_copy(rel_b[0:CH, :], metas[0:CH, 1, :]).then_inc(metas_made, 1)
                    dve.wait_ge(sin_made, k + 1)
                    link(dve.tensor_scalar(ew_turn[0:CH, :], ew_turn[0:CH, :], 0.5, 0.5, ALU.mult, ALU.add))
                    link(dve.scalar_tensor_tensor(out=metas[0:CH, 2, :], in0=ew_g[0:CH, :], scalar=CUT,
                                                  in1=ew_turn[0:CH, :], op0=ALU.is_lt, op1=ALU.mult))
                    dve.sem_inc(metas_made, 1)
                    assert done == LINKS
                    dve.wait_ge(metas_turned, k + 1)
                    for m in range(3):
                        ins = dve.tensor_copy(meta_out[:, :, m, :],
                                              meta_ps[:, m, 0:CH].rearrange("p (h u) -> p h u", u=U))
                    ins.then_inc(meta_copied, 1)

            @block.scalar
            def _(act):
                act.wait_ge(s_zero, 1)
                for k in range(-(-STS // 7)):
                    n = min(7, STS - 7 * k)
                    act.dma_start(slot_x[7 * k * P:(7 * k + n) * P, :].rearrange("(p r) d -> p (r d)", p=P),
                                  zero[:, 0:n * D]).then_inc(s_zfill, 16)
                act.wait_ge(s_count, 1)
                chunks = act.value_load(n_run[0:1, 1:2], min_val=1, max_val=MAX_CH)
                with act.Fori(0, chunks) as k:
                    act.wait_ge(turn_ready, k + 1)
                    act.sem_inc(gate_a, 1)
                    act.activation(ew_turn[0:CH, :], ew_turn[0:CH, :], ACT.Abs).then_inc(abs_made, 1)
                    act.wait_ge(abs_made, k + 1)
                    act.sem_inc(gate_a, 1)
                    act.activation(ew_turn[0:CH, :], ew_turn[0:CH, :], ACT.Sin, scale=-2.0 * math.pi,
                                   bias=half_pi[0:CH, 0:1]).then_inc(sin_made, 1)
                act.wait_ge(s_zfill, 16 * -(-STS // 7))

            @block.tensor
            def _(pe):
                pe.wait_ge(s_count, 1)
                chunks = pe.value_load(n_run[0:1, 1:2], min_val=1, max_val=MAX_CH)
                with pe.Fori(0, chunks) as k:
                    pe.wait_ge(metas_made, 3 * k + 3)
                    for m in range(3):
                        mm = pe.transpose(meta_ps[:, m, 0:CH], metas[0:CH, m, :], ident[0:CH, 0:CH])
                    mm.then_inc(metas_turned, 1)

        next_phase()

        with ExitStack() as s3:
            def sb(name, shape, dt=F32):
                return s3.enter_context(nc.sbuf_tensor(name, shape, dt))

            def ps(name, shape):
                return s3.enter_context(nc.psum_tensor(name, shape, F32))

            def sem(name):
                return named(name)

            wd = sb("wd", [R + 1, 2 * D])
            kv_in = sb("kv_in", [P, U, 2 * D])
            ea_in = sb("ea_in", [R + 1, U, P])
            meta_in = sb("meta_in", [P, 2, 3, U])
            rel_in = sb("rel_in", [P, 2, U * P], BF16)
            tab_in = sb("tab_in", [1, 2, 2 * U], I32)
            src_i = sb("src_i", [P, 2, U], I32)
            onehot_t = sb("onehot_t", [P, 3, 4 * P])
            onehot = sb("onehot", [P, 3, 2, P])
            kd = sb("kd", [P, 2, 2, D])
            msg = sb("msg", [P, 3, 2, D])
            logit = sb("logit", [P, 3, 2])
            gated = sb("gated", [P, 3, 2])
            attn = sb("attn", [P, 3, 2])
            neg_part = sb("neg_part", [P, 1])
            dkv = ps("dkv", [P, 3, 2, 2 * D])
            q_ps = ps("q_ps", [P, 2, D])
            agg_ps = ps("agg_ps", [P, 2, D])

            s_wd = sem("s_wd")
            s_rows = sem("s_rows")
            s_npart = sem("s_npart")
            kv_landed = [sem(f"kv_landed{u}") for u in range(U)]
            ea_landed = [sem(f"ea_landed{u}") for u in range(U)]
            meta_landed = [sem(f"meta_landed{h}") for h in range(2)]
            rel_landed = [sem(f"rel_landed{h}") for h in range(2)]
            tab_landed = [sem(f"tab_landed{h}") for h in range(2)]
            src_ready = sem("src_ready")
            gate_pool = sem("gate_pool3")
            gate_act = sem("gate_act3")
            gate_sp = sem("gate_sp3")
            gate_pe = sem("gate_pe3")

            def each(name):
                return [sem(f"{name}{p}") for p in range(3)]

            dkv_made = each("dkv_made")
            dkv_silu = each("dkv_silu")
            turned = each("turned")
            onehot_t_made = each("onehot_t_made")
            q_made = each("q_made")
            kd_made = each("kd_made")
            onehot_made = each("onehot_made")
            logit_made = each("logit_made")
            logit_silu = each("logit_silu")
            attn_made = each("attn_made")
            msg_made = each("msg_made")
            sum_made = each("sum_made")
            added_even = each("added_even")
            added_odd = each("added_odd")
            block = s3.enter_context(nc.Block())

            def before(h, half, p, lag):
                return (h, half, p - lag) if p >= lag else (1 - h, half - 1, p - lag + PAIRS)

            def landed(h, half):
                return 16 if isinstance(half, int) else 8 * (half - h) + 16

            def exists(half):
                return not (isinstance(half, int) and half < 0)

            def done(eng, sems, at):
                h, half, p = at
                if exists(half):
                    eng.wait_ge(sems[p % 3], 2 * half + p // 3 + 1)

            def half_steps(eng, body, drain=None):
                for h in range(2):
                    body(h, h)
                n_it = eng.value_load(n_run[0:1, 0:1], min_val=2, max_val=MAX_IT)
                with eng.Fori(1, n_it) as i:
                    for h in range(2):
                        body(h, 2 * i + h)
                if drain:
                    drain(0, 2 * n_it)

            @block.sync
            def _(sp):
                sp.dma_start(wd[:, :], a["wd_t"]).then_inc(s_wd, 16)
                sp.wait_ge(s_rows, 1)

                def half_step(h, half):
                    done(sp, added_odd, (h, half - 2, PAIRS - 1))
                    sp.dma_start(tab_in[:, h, :].rearrange("p (k u) -> p k u", k=2),
                                 item_tab[:, ds(half * U, U)].unsqueeze(0)).then_inc(tab_landed[h], 16)
                    sp.dma_start(meta_in[:, h, :, :].rearrange("p k u -> p (k u)"),
                                 meta_cols[ds(half, 1)].rearrange("a p m -> (a p) m")).then_inc(meta_landed[h], 16)
                    sp.dma_start(rel_in[:, h, :], rel_rows[ds(half * U, U), :].rearrange("u e -> (u e)")
                                 .unsqueeze(0).to_broadcast([P, U * P])).then_inc(rel_landed[h], 16)
                    n = landed(h, half)
                    sp.wait_ge(tab_landed[h], n)
                    sp.sem_inc(gate_sp, 1)
                    for u in range(U):
                        t = sp.value_load(tab_in[0:1, h, u:u + 1], min_val=0, max_val=ET - 1)
                        done(sp, dkv_made, (1 - h, half - 1, u // 2))
                        sp.dma_start(ea_in[0:R, u, :], a["edge_attr_t"][ds(t, 1)].rearrange("a r e -> (a r) e")) \
                            .then_inc(ea_landed[u], 16)

                half_steps(sp, half_step)

            @block.gpsimd
            def _(pool):
                pool.tensor_scalar(neg_part[:, :], iota_part[:, :], -1.0, None, ALU.mult).then_inc(s_npart, 1)

                def half_step(h, half):
                    pool.wait_ge(meta_landed[h], landed(h, half))
                    pool.sem_inc(gate_pool, 1)
                    pool.tensor_copy(src_i[:, h, :], meta_in[:, h, 0, :]).then_inc(src_ready, 1)
                    pool.wait_ge(src_ready, half + 1)
                    pool.sem_inc(gate_pool, 1)
                    for u in range(U):
                        if u % 2 == 0:
                            done(pool, msg_made, (1 - h, half - 1, u // 2))
                            pool.sem_inc(gate_pool, 1)
                        pool.indirect_dma_start(kv_in[:, u, :], None, kv_table,
                                                bass.IndirectOffsetOnAxis(ap=src_i[:, h, u:u + 1], axis=0)) \
                            .then_inc(kv_landed[u], 16)

                half_steps(pool, half_step)

            @block.scalar
            def _(act):
                act.wait_ge(s_npart, 1)

                def attention(at):
                    h, half, p = at
                    if exists(half):
                        done(act, logit_made, at)
                        act.sem_inc(gate_act, 1)
                        act.activation(gated[:, p % 3, :], logit[:, p % 3, :], ACT.Silu).then_inc(logit_silu[p % 3], 1)

                def half_step(h, half):
                    for p in range(PAIRS):
                        if p % 2 == 0:
                            g = p // 2
                            if p == 0:
                                act.wait_ge(rel_landed[h], landed(h, half))
                            done(act, q_made, (1 - h, half - 1, p + 1))
                            act.sem_inc(gate_act, 1)
                            act.activation(onehot_t[:, g, :], rel_in[:, h, g * 4 * P:(g + 1) * 4 * P], ACT.Abs,
                                           bias=neg_part[:, 0:1]).then_inc(turned[g], 1)
                        done(act, dkv_made, (h, half, p))
                        act.sem_inc(gate_act, 1)
                        act.activation(dkv[:, p % 3, :, :], dkv[:, p % 3, :, :], ACT.Silu).then_inc(dkv_silu[p % 3], 1)
                        if p % 2 == 0:
                            act.wait_ge(turned[g], half + 1)
                            act.sem_inc(gate_act, 1)
                            act.activation(onehot_t[:, g, :], onehot_t[:, g, :], ACT.Relu, bias=1.0,
                                           scale=-1.0).then_inc(onehot_t_made[g], 1)
                        attention(before(h, half, p, 1))

                half_steps(act, half_step, lambda h, half: attention(before(h, half, 0, 1)))

            @block.tensor
            def _(pe):
                pe.wait_ge(s_wd, 16)
                pe.wait_ge(s_rows, 1)

                def sums(at):
                    h, half, p = at
                    if exists(half):
                        done(pe, msg_made, at)
                        done(pe, added_odd, before(h, half, p, 1))
                        for k in range(2):
                            mm = pe.matmul(agg_ps[:, k, :], onehot[:, p % 3, k, :], msg[:, p % 3, k, :],
                                           start=True, stop=True)
                        mm.then_inc(sum_made[p % 3], 1)

                def half_step(h, half):
                    for p in range(PAIRS):
                        done(pe, msg_made, before(h, half, p, 3))
                        for k in range(2):
                            u = 2 * p + k
                            pe.wait_ge(ea_landed[u], 16 * half + 16)
                            mm = pe.matmul(dkv[:, p % 3, k, :], ea_in[:, u, :], wd[:, :], start=True, stop=True)
                        mm.then_inc(dkv_made[p % 3], 1)
                        if p == 0:
                            pe.wait_ge(tab_landed[h], landed(h, half))
                        pe.wait_ge(onehot_t_made[p // 2], half + 1)
                        done(pe, logit_made, before(h, half, p, 1))
                        pe.sem_inc(gate_pe, 1)
                        for k in range(2):
                            u = 2 * p + k
                            b = pe.value_load(tab_in[0:1, h, U + u:U + u + 1], min_val=0, max_val=NT - 1)
                            mm = pe.matmul(q_ps[:, k, :], onehot_t[:, p // 2, (u % 4) * P:(u % 4 + 1) * P],
                                           qx[:, ds(b * D, D)], start=True, stop=True)
                        mm.then_inc(q_made[p % 3], 1)
                        sums(before(h, half, p, 2))

                def drain(h, half):
                    sums(before(h, half, 0, 2))
                    sums(before(h, half, 0, 1))

                half_steps(pe, half_step, drain)

            @block.vector
            def _(dve):
                dve.memset(ea_in[R:R + 1, :, :], 1.0).then_inc(s_rows, 1)

                def logits(h, half, p):
                    done(dve, dkv_silu, (h, half, p))
                    for k in range(2):
                        dve.wait_ge(kv_landed[2 * p + k], 16 * half + 16)
                    dve.tensor_tensor(kd[:, p % 2, :, :], kv_in[:, 2 * p:2 * p + 2, 0:D], dkv[:, p % 3, :, 0:D],
                                      ALU.mult).then_inc(kd_made[p % 3], 1)
                    if p == 0:
                        dve.wait_ge(meta_landed[h], landed(h, half))
                    done(dve, sum_made, before(h, half, p, 3))
                    for k in range(2):
                        u = 2 * p + k
                        ins = dve.tensor_scalar(onehot[:, p % 3, k, :], iota_free[:, :], meta_in[:, h, 1, u:u + 1],
                                                None, ALU.is_equal)
                    ins.then_inc(onehot_made[p % 3], 1)
                    done(dve, q_made, (h, half, p))
                    done(dve, kd_made, (h, half, p))
                    for k in range(2):
                        ins = dve.tensor_tensor_reduce(kd[:, p % 2, k, :], kd[:, p % 2, k, :], q_ps[:, k, :], 1.0, 0.0,
                                                       ALU.mult, ALU.add, logit[:, p % 3, k:k + 1])
                    ins.then_inc(logit_made[p % 3], 1)

                def cutoff(at):
                    h, half, p = at
                    if exists(half):
                        done(dve, logit_silu, at)
                        dve.tensor_tensor(attn[:, p % 3, :], gated[:, p % 3, :],
                                          meta_in[:, h, 2, 2 * p:2 * p + 2], ALU.mult).then_inc(attn_made[p % 3], 1)

                def messages(at):
                    h, half, p = at
                    if exists(half):
                        done(dve, attn_made, at)
                        for k in range(2):
                            ins = dve.scalar_tensor_tensor(
                                out=msg[:, p % 3, k, :], in0=kv_in[:, 2 * p + k, D:2 * D],
                                scalar=attn[:, p % 3, k:k + 1], in1=dkv[:, p % 3, k, D:2 * D],
                                op0=ALU.mult, op1=ALU.mult)
                        ins.then_inc(msg_made[p % 3], 1)

                def add(at, k):
                    h, half, p = at
                    if exists(half):
                        b = dve.value_load(tab_in[0:1, h, U + 2 * p + k:U + 2 * p + k + 1], min_val=0, max_val=NT - 1)
                        if k == 0:
                            done(dve, sum_made, at)
                            done(dve, added_odd, before(h, half, p, 1))
                        else:
                            done(dve, added_even, at)
                        dve.tensor_tensor(agg[:, ds(b * D, D)], agg[:, ds(b * D, D)], agg_ps[:, k, :], ALU.add) \
                            .then_inc((added_even, added_odd)[k][p % 3], 1)

                def half_step(h, half):
                    for p in range(PAIRS):
                        logits(h, half, p)
                        cutoff(before(h, half, p, 1))
                        add(before(h, half, p, 2), 0)
                        messages(before(h, half, p, 1))
                        add(before(h, half, p, 2), 1)

                def drain(h, half):
                    cutoff(before(h, half, 0, 1))
                    add(before(h, half, 0, 2), 0)
                    messages(before(h, half, 0, 1))
                    add(before(h, half, 0, 2), 1)
                    add(before(h, half, 0, 1), 0)
                    add(before(h, half, 0, 1), 1)

                half_steps(dve, half_step, drain)

        def late(name, shape, dt=F32):
            return ctx.enter_context(nc.sbuf_tensor(name, shape, dt))

        w1 = late("w1_all", [P, NE * DC * HID])
        BR = 3 * NE
        bias1 = late("bias1", [P, HID], BF16)
        bias2 = late("bias2", [P, D], BF16)
        pick = late("pick_sb", [P, NE * P], BF16)

        next_phase()

        with ExitStack() as s4:
            def sb(name, shape, dt=F32):
                return s4.enter_context(nc.sbuf_tensor(name, shape, dt))

            def ps(name, shape):
                return s4.enter_context(nc.psum_tensor(name, shape, F32))

            wo = sb("wo", [P, DC, D])
            bo = sb("bo_sb", [1, D])
            offs = sb("offs", [P, NE, DC])
            offs_rep = sb("offs_rep", [P, NE, DC, BR])
            b1_in = sb("b1_in", [BR, HID])
            b2_in = sb("b2_in", [BR, D])
            mask = sb("mask", [BR, 3])
            pick_in = sb("pick_in", [BR, NE * P])
            part_b = sb("part_b", [BR, HID], BF16)
            agg_in = sb("agg_in", [P, 2, D])
            agg_t = sb("agg_t", [P, 2, D])
            tp = ps("tp4", [P, 2, 512])
            prod = ps("prod", [P, 2, 512])
            b1_ps = ps("b1_ps", [BR, HID])
            res_landed = [named(f"res_landed{k}") for k in range(7)]
            wo_landed = named("wo_landed")
            small_landed = named("small_landed")
            w1_landed = named("w1_landed")
            rep_made = named("rep_made")
            bias_mm = named("bias_mm4")
            turned4 = [named(f"turned4_{k}") for k in range(2)]
            copied4 = [named(f"copied4_{k}") for k in range(2)]
            prod_made = [named(f"prod_made{k}") for k in range(2)]
            x2_made = [named(f"x2_made{k}") for k in range(2)]
            stats_made = named("stats_made4")
            staged = [named(f"staged{k}") for k in range(2)]
            gate4 = named("gate4")
            s_c4 = named("s_c4")
            s_var4 = named("s_var4")
            s_root4 = named("s_root4")
            block = s4.enter_context(nc.Block())
            G = NT // 7

            @block.sync
            def _(sp):
                sp.dma_start(wo[:, :, :], a["wo_t"].rearrange("(c p) n -> p c n", p=P)).then_inc(wo_landed, 16)
                sp.dma_start(bo[:, :], a["bo"]).then_inc(wo_landed, 16)
                for k in range(7):
                    sp.dma_start(qx[:, k * G * D:(k + 1) * G * D].rearrange("p (t d) -> p t d", d=D),
                                 res_table[k * G * P:(k + 1) * G * P, :].rearrange("(t p) d -> p t d", p=P)) \
                        .then_inc(res_landed[k], 16)
                for tile, name in ((offs[:, :, :], "ffn_b"), (b1_in[:, :], "b1"), (b2_in[:, :], "b2"),
                                   (mask[:, :], "part_mask"), (pick_in[:, :], "pick")):
                    sp.dma_start(tile, a[name]).then_inc(small_landed, 16)
                for e in range(NE):
                    sp.dma_start(w1[:, e * DC * HID:(e + 1) * DC * HID].rearrange("p (c h) -> p c h", c=DC),
                                 a["w1"][e].rearrange("(c p) h -> p c h", p=P)).then_inc(w1_landed, 16)
                sp.wait_ge(w1_landed, 16 * NE)

            @block.scalar
            def _(act):
                def stage(t, s, n, last):
                    slot_free(act, turned4[s], n)
                    act.sem_inc(gate4, 1)
                    act.activation(agg_in[:, s, :], agg[:, ds(t * D, D)], ACT.Copy).then_inc(staged[s], 1)

                over_tiles(act, NT, stage)
                norm_roots(act, s_root4, s_var4)

            @block.tensor
            def _(pe):
                pe.wait_ge(wo_landed, 32)

                def transposes(s, n):
                    slot_free(pe, copied4[s], n)
                    pe.wait_ge(staged[s], n + 1)
                    for k in range(DC):
                        mm = pe.transpose(tp[:, s, k * P:(k + 1) * P], agg_in[:, s, k * P:(k + 1) * P], ident[:, :])
                    mm.then_inc(turned4[s], 1)

                def product(t, s, n, last):
                    if not last:
                        transposes(1 - s, n + s)
                    slot_free(pe, x2_made[s], n)
                    pe.wait_ge(copied4[s], n + 1)
                    for k in range(DC):
                        pe.matmul(prod[:, s, 0:D], agg_t[:, s, k * P:(k + 1) * P], wo[:, k, :], start=(k == 0),
                                  stop=False)
                    pe.matmul(prod[:, s, 0:D], ones[0:1, :], bo[:, :], start=False, stop=True) \
                        .then_inc(prod_made[s], 1)

                transposes(0, 0)
                over_tiles(pe, NT, product)
                pe.wait_ge(rep_made, 1)
                pe.wait_ge(w1_landed, 16 * NE)
                for e in range(NE):
                    for c in range(DC):
                        for lo in range(0, HID, 512):
                            mm = pe.matmul(b1_ps[:, lo:lo + 512], offs_rep[:, e, c, :],
                                           w1[:, (e * DC + c) * HID + lo:(e * DC + c) * HID + lo + 512],
                                           start=(e == 0 and c == 0), stop=(e == NE - 1 and c == DC - 1))
                mm.then_inc(bias_mm, 1)

            @block.vector
            def _(dve):
                c = Chain(dve, s_c4)

                def copy(s, n):
                    slot_free(dve, prod_made[s], n)
                    dve.wait_ge(turned4[s], n + 1)
                    dve.tensor_copy(agg_t[:, s, :], tp[:, s, 0:D]).then_inc(copied4[s], 1)

                def add(t, s, n, last):
                    if not last:
                        copy(1 - s, n + s)
                    dve.wait_ge(prod_made[s], n + 1)
                    dve.tensor_tensor(qx[:, ds(t * D, D)], qx[:, ds(t * D, D)], prod[:, s, 0:D], ALU.add) \
                        .then_inc(x2_made[s], 1)
                    dve.wait_ge(x2_made[s], n + 1)
                    dve.bn_stats(stats[:, ds(t, 1), :].rearrange("p a b -> p (a b)"), qx[:, ds(t * D, D)]) \
                        .then_inc(stats_made, 1)

                for k in range(7):
                    dve.wait_ge(res_landed[k], 16)
                copy(0, 0)
                over_tiles(dve, NT, add)
                dve.wait_ge(stats_made, NT)
                norm_scales(dve, s_root4, c, s_var4, 0)
                dve.wait_ge(small_landed, 16 * 5)
                c(dve.memset(offs_rep[:, :, :, :], 0.0))
                for e in range(NE):
                    ins = dve.tensor_copy(offs_rep[:, e, :, 3 * e:3 * e + 3],
                                          offs[:, e, :].unsqueeze(2).to_broadcast([P, DC, 3]))
                ins.then_inc(rep_made, 1)
                c(dve.memset(pick[:, :], 0.0))
                c(dve.memset(bias1[:, :], 0.0))
                c(dve.memset(bias2[:, :], 0.0))
                c(dve.tensor_copy(pick[0:BR, :], pick_in[:, :]))
                dve.wait_ge(bias_mm, 1)
                c(dve.tensor_tensor(b1_in[:, :], b1_in[:, :], b1_ps[:, :], ALU.add))
                for full, out_b, n in ((b1_in, bias1, HID), (b2_in, bias2, D)):
                    c(dve.tensor_copy(part_b[:, 0:n], full[:, :]))
                    c(dve.tensor_scalar(out_b[0:BR, :], part_b[:, 0:n], mask[:, 0:1], None, ALU.mult))
                    for m in range(1, 3):
                        c(dve.tensor_tensor(full[:, :], full[:, :], part_b[:, 0:n], ALU.subtract))
                        c(dve.tensor_copy(part_b[:, 0:n], full[:, :]))
                        c(dve.scalar_tensor_tensor(out=out_b[0:BR, :], in0=part_b[:, 0:n], scalar=mask[:, m:m + 1],
                                                   in1=out_b[0:BR, :], op0=ALU.mult, op1=ALU.add))

        next_phase()

        with ExitStack() as s5:
            def sb(name, shape, dt=F32):
                return s5.enter_context(nc.sbuf_tensor(name, shape, dt))

            def ps(name, shape):
                return s5.enter_context(nc.psum_tensor(name, shape, F32))

            wr = sb("wr_sb", [P, DC, NE])
            br = sb("br_sb", [1, NE])
            gains = sb("gains", [P, NE, DC])
            z = sb("z", [P, 2, D])
            z_t = sb("z_t", [P, 2, D])
            tri = sb("tri", [P, P])
            down = sb("down", [P, NE])
            rows = sb("rows", [P, NT])
            tiles = sb("tiles", [P, STS])
            lg = sb("lg", [P, NT, NE])
            hot1 = sb("hot1", [P, NT, NE])
            hot2 = sb("hot2", [P, NT, NE])
            work = sb("work", [P, NT, NE])
            cum = sb("cum", [P, NE, NT])
            cmp = sb("cmp", [P, NE, NT])
            over = sb("over", [1, STS, NE - 1])
            m1 = sb("m1", [P, NT])
            m2 = sb("m2", [P, NT])
            d12 = sb("d12", [P, NT])
            n_tiles = sb("n_tiles", [P, NE])
            end = sb("end", [P, NE])
            base = sb("base", [P, NE])
            slot_f = sb("slot_f", [P, NT, 2])
            expert_f = sb("expert_f", [1, STS])
            tp = ps("tp5", [P, 2, 512])
            lg_ps = ps("lg_ps", [P, 512])
            rank = ps("rank", [P, 512])
            total = ps("total", [P, 512])
            wr_landed = named("wr_landed")
            gains_landed = named("gains_landed")
            w2_landed = named("w2_landed")
            w1_scaled = named("w1_scaled")
            z_made = [named(f"z_made{k}") for k in range(2)]
            turned5 = [named(f"turned5_{k}") for k in range(2)]
            copied5 = [named(f"copied5_{k}") for k in range(2)]
            lg_made = [named(f"lg_made{k}") for k in range(2)]
            gate5 = named("gate5")
            gap_made = named("gap_made")
            exp_made = named("exp_made")
            hot_made = named("hot_made")
            ranks_made = named("ranks_made")
            const5 = named("const5")
            s_c5 = named("s_c5")
            block = s5.enter_context(nc.Block())

            @block.sync
            def _(sp):
                sp.dma_start(wr[:, :, :], a["wr"].rearrange("(c p) e -> p c e", p=P)).then_inc(wr_landed, 16)
                sp.dma_start(br[:, :], a["br"]).then_inc(wr_landed, 16)
                sp.dma_start(gains[:, :, :], a["ffn_g"]).then_inc(gains_landed, 16)
                for e in range(NE):
                    sp.dma_start(w2[:, e * KC * D:(e + 1) * KC * D].rearrange("p (k d) -> p k d", k=KC),
                                 a["w2"][e].rearrange("(k p) d -> p k d", p=P)).then_inc(w2_landed, 16)
                sp.wait_ge(w2_landed, 16 * NE)

            @block.gpsimd
            def _(pool):
                c = Chain(pool, const5)
                c(pool.affine_select(out=tri[:, :], in_=ones[:, :], compare_op=ALU.is_gt, fill=0.0, base=0,
                                     pattern=[[1, P]], channel_multiplier=-1))
                c(pool.iota(down[:, :], pattern=[[-1, NE]], base=NE, channel_multiplier=0,
                            allow_small_or_imprecise_dtypes=True))
                c(pool.iota(rows[:, :], pattern=[[P, NT]], base=0, channel_multiplier=0,
                            allow_small_or_imprecise_dtypes=True))
                c(pool.iota(tiles[:, :], pattern=[[1, STS]], base=0, channel_multiplier=0,
                            allow_small_or_imprecise_dtypes=True))
                pool.wait_ge(gains_landed, 16)
                for e in range(NE):
                    for k in range(DC):
                        w = w1[:, (e * DC + k) * HID:(e * DC + k + 1) * HID]
                        pool.tensor_scalar(w, w, gains[:, e, k:k + 1], None, ALU.mult).then_inc(w1_scaled, 1)

            @block.scalar
            def _(act):
                def norm(t, s, n, last):
                    slot_free(act, turned5[s], n)
                    act.sem_inc(gate5, 1)
                    act.activation(z[:, s, :], qx[:, ds(t * D, D)], ACT.Identity, scale=rstd[:, ds(t, 1)],
                                   bias=bias_r[:, ds(t, 1)]).then_inc(z_made[s], 1)

                over_tiles(act, NT, norm)
                act.wait_ge(gap_made, 1)
                act.activation(m2[:, :], m2[:, :], ACT.Exp).then_inc(exp_made, 1)

            @block.tensor
            def _(pe):
                pe.wait_ge(wr_landed, 32)

                def transposes(s, n):
                    slot_free(pe, copied5[s], n)
                    pe.wait_ge(z_made[s], n + 1)
                    for k in range(DC):
                        mm = pe.transpose(tp[:, s, k * P:(k + 1) * P], z[:, s, k * P:(k + 1) * P], ident[:, :])
                    mm.then_inc(turned5[s], 1)

                def logits(t, s, n, last):
                    if not last:
                        transposes(1 - s, n + s)
                    pe.wait_ge(copied5[s], n + 1)
                    o = lg_ps[:, ds(t * NE, NE)]
                    for k in range(DC):
                        pe.matmul(o, z_t[:, s, k * P:(k + 1) * P], wr[:, k, :], start=(k == 0), stop=False)
                    pe.matmul(o, ones[0:1, :], br[:, :], start=False, stop=True).then_inc(lg_made[s], 1)

                transposes(0, 0)
                over_tiles(pe, NT, logits)
                pe.wait_ge(hot_made, 1)
                pe.wait_ge(const5, 4)
                both = work[:, :, :].rearrange("p t e -> p (t e)")
                pe.matmul(rank[:, 0:NT * NE], tri[:, :], both, start=True, stop=True)
                pe.matmul(total[:, 0:NT * NE], ones[:, :], both, start=True, stop=True).then_inc(ranks_made, 1)

            @block.vector
            def _(dve):
                c = Chain(dve, s_c5)

                def copy(t, s, n, last):
                    slot_free(dve, lg_made[s], n)
                    dve.wait_ge(turned5[s], n + 1)
                    dve.tensor_copy(z_t[:, s, :], tp[:, s, 0:D]).then_inc(copied5[s], 1)

                over_tiles(dve, NT, copy)
                dve.wait_ge(lg_made[0], NT // 2 + 1)
                dve.wait_ge(lg_made[1], NT // 2)
                dve.wait_ge(const5, 4)
                c(dve.tensor_copy(lg[:, :, :].rearrange("p t e -> p (t e)"), lg_ps[:, 0:NT * NE]))
                down_b = down[:, :].unsqueeze(1).to_broadcast([P, NT, NE])

                def wide(v):
                    return v[:, :].unsqueeze(2).to_broadcast([P, NT, NE])

                def best(m, hot):
                    c(dve.tensor_reduce(m[:, :], lg[:, :, :], AX, ALU.max))
                    c(dve.tensor_tensor(work[:, :, :], lg[:, :, :], wide(m), ALU.is_ge))
                    c(dve.tensor_tensor(work[:, :, :], work[:, :, :], down_b, ALU.mult))
                    c(dve.tensor_reduce(d12[:, :], work[:, :, :], AX, ALU.max))
                    c(dve.tensor_tensor(hot[:, :, :], down_b, wide(d12), ALU.is_equal))

                best(m1, hot1)
                c(dve.scalar_tensor_tensor(out=lg[:, :, :], in0=hot1[:, :, :], scalar=-3.0e38, in1=lg[:, :, :],
                                           op0=ALU.mult, op1=ALU.add))
                best(m2, hot2)
                c(dve.tensor_tensor(work[:, :, :], hot1[:, :, :], hot2[:, :, :], ALU.add))
                dve.sem_inc(hot_made, 1)
                c(dve.tensor_tensor(m2[:, :], m2[:, :], m1[:, :], ALU.subtract))
                dve.sem_inc(gap_made, 1)
                dve.wait_ge(exp_made, 1)
                c(dve.tensor_scalar(m1[:, :], m2[:, :], 1.0, None, ALU.add))
                c(dve.reciprocal(w_top[:, :, 0], m1[:, :]))
                c(dve.tensor_tensor(w_top[:, :, 1], m2[:, :], w_top[:, :, 0], ALU.mult))
                dve.wait_ge(ranks_made, 1)
                tot = total[:, 0:NT * NE].rearrange("p (t e) -> p t e", e=NE)
                for e in range(NE):
                    c(dve.tensor_tensor_scan(cum[:, e, :], ones[:, 0:NT], tot[:, :, e], 0.0, ALU.mult, ALU.add))
                c(dve.tensor_tensor(cmp[:, :, :], cum[:, :, NT - 1:NT].to_broadcast([P, NE, NT]),
                                    rows[:, :].unsqueeze(1).to_broadcast([P, NE, NT]), ALU.is_gt))
                c(dve.tensor_reduce(n_tiles[:, :], cmp[:, :, :], AX, ALU.add))
                c(dve.tensor_tensor_scan(end[:, :], ones[:, 0:NE], n_tiles[:, :], 0.0, ALU.mult, ALU.add))
                c(dve.tensor_tensor(base[:, :], end[:, :], n_tiles[:, :], ALU.subtract))
                c(dve.tensor_scalar(base[:, :], base[:, :], float(P), None, ALU.mult))
                c(dve.tensor_tensor(work[:, :, :], cum[:, :, :].rearrange("p e t -> p t e"), tot, ALU.subtract))
                c(dve.tensor_tensor(work[:, :, :], work[:, :, :],
                                    rank[:, 0:NT * NE].rearrange("p (t e) -> p t e", e=NE), ALU.add))
                c(dve.tensor_tensor(work[:, :, :], work[:, :, :],
                                    base[:, :].unsqueeze(1).to_broadcast([P, NT, NE]), ALU.add))
                for k, hot in enumerate((hot1, hot2)):
                    c(dve.tensor_tensor(hot[:, :, :], hot[:, :, :], work[:, :, :], ALU.mult))
                    c(dve.tensor_reduce(slot_f[:, :, k], hot[:, :, :], AX, ALU.add))
                c(dve.tensor_copy(slot_i[:, :, :], slot_f[:, :, :]))
                c(dve.tensor_tensor(over[:, :, :], tiles[0:1, :].unsqueeze(2).to_broadcast([1, STS, NE - 1]),
                                    end[0:1, 0:NE - 1].unsqueeze(1).to_broadcast([1, STS, NE - 1]), ALU.is_ge))
                c(dve.tensor_reduce(expert_f[:, :], over[:, :, :], AX, ALU.add))
                c(dve.tensor_copy(expert_i[:, :], expert_f[:, :]))

        next_phase()

        with ExitStack() as s6:
            xn = s6.enter_context(nc.sbuf_tensor("xn", [P, 2, D], F32))
            slot_s = s6.enter_context(nc.sbuf_tensor("slot_s", [P, 2, 2], I32))
            xn_made = [named(f"xn_made{k}") for k in range(2)]
            slot_copied = named("slot_copied")
            scattered = [named(f"scattered{k}") for k in range(2)]
            gate6a = named("gate6a")
            gate6p = named("gate6p")
            block = s6.enter_context(nc.Block())

            @block.scalar
            def _(act):
                def norm(t, s, n, last):
                    slot_free(act, scattered[s], n, 32)
                    act.sem_inc(gate6a, 1)
                    act.activation(xn[:, s, :], qx[:, ds(t * D, D)], ACT.Identity, scale=rstd2[:, ds(t, 1)],
                                   bias=bias_s[:, ds(t, 1)]).then_inc(xn_made[s], 1)

                over_tiles(act, NT, norm)

            @block.gpsimd
            def _(pool):
                def scatter(t, s, n, last):
                    slot_free(pool, scattered[s], n, 32)
                    pool.sem_inc(gate6p, 1)
                    pool.tensor_copy(slot_s[:, s, :], slot_i[:, ds(t, 1), :].rearrange("p a k -> p (a k)")) \
                        .then_inc(slot_copied, 1)
                    pool.wait_ge(slot_copied, t + 1)
                    pool.wait_ge(xn_made[s], n + 1)
                    pool.sem_inc(gate6p, 1)
                    for k in range(2):
                        pool.indirect_dma_start(slot_x, bass.IndirectOffsetOnAxis(ap=slot_s[:, s, k:k + 1], axis=0),
                                                xn[:, s, :], None).then_inc(scattered[s], 16)

                over_tiles(pool, NT, scatter)
                pool.wait_ge(scattered[0], 32 * (NT // 2 + 1))
                pool.wait_ge(scattered[1], 32 * (NT // 2))

        next_phase()

        with ExitStack() as s7:
            def sb(name, shape, dt=F32):
                return s7.enter_context(nc.sbuf_tensor(name, shape, dt))

            def ps(name, shape):
                return s7.enter_context(nc.psum_tensor(name, shape, F32))

            xs = sb("xs", [P, 2, D])
            xs_t = sb("xs_t", [P, 2, D])
            h = sb("h", [P, 2, HID])
            h_t = sb("h_t", [P, HID])
            y = sb("y", [P, 2, D])
            tp = ps("tp7", [P, 512])
            h_ps = ps("h_ps", [P, 2, HID])
            ht_ps = ps("ht_ps", [P, HID])
            y_ps = ps("y_ps", [P, 512])
            xs_landed = [named(f"xs_landed{k}") for k in range(2)]
            xs_turned = [named(f"xs_turned{k}") for k in range(2)]
            xs_copied = [named(f"xs_copied{k}") for k in range(2)]
            h_made = [named(f"h_made{k}") for k in range(2)]
            h_gelu = [named(f"h_gelu{k}") for k in range(2)]
            h_turned = [named(f"h_turned{k}") for k in range(2)]
            h_copied = [named(f"h_copied{k}") for k in range(2)]
            y_made = [named(f"y_made{k}") for k in range(2)]
            y_taken = [named(f"y_taken{k}") for k in range(2)]
            y_stored = [named(f"y_stored{k}") for k in range(2)]
            gate7 = named("gate7")
            gate7p = named("gate7p")
            gate7s = named("gate7s")
            block = s7.enter_context(nc.Block())

            @block.sync
            def _(sp):
                def load(q, s, n, last):
                    slot_free(sp, xs_turned[s], n)
                    sp.dma_start(xs[:, s, :], slot_x[ds(q * P, P), :]).then_inc(xs_landed[s], 16)

                over_tiles(sp, STS, load)

            @block.tensor
            def _(pe):
                def turn_x(s, n):
                    pe.wait_ge(xs_landed[s], 16 * n + 16)
                    if not (isinstance(n, int) and n == 0 and s == 0):
                        pe.wait_ge(xs_copied[1 - s], n + s)
                    for k in range(DC):
                        mm = pe.transpose(tp[:, k * P:(k + 1) * P], xs[:, s, k * P:(k + 1) * P], ident[:, :])
                    mm.then_inc(xs_turned[s], 1)

                def turn_h(s, n):
                    pe.wait_ge(h_gelu[s], n + 1)
                    for g in range(2):
                        if not (isinstance(n, int) and n == 0 and s == 0):
                            pe.wait_ge(h_copied[g], 2 * n + s)
                        for k in range(KC // 2 * g, KC // 2 * (g + 1)):
                            mm = pe.transpose(ht_ps[:, k * P:(k + 1) * P], h[:, s, k * P:(k + 1) * P], ident[:, :])
                        mm.then_inc(h_turned[g], 1)

                def expert(q):
                    pe.sem_inc(gate7p, 1)
                    return pe.value_load(expert_i[0:1, ds(q, 1)], min_val=0, max_val=NE - 1)

                def layer1(q, s, n):
                    pe.wait_ge(xs_copied[s], n + 1)
                    slot_free(pe, h_gelu[s], n)
                    e = expert(q)
                    for lo in range(0, HID, 512):
                        for k in range(DC):
                            pe.matmul(h_ps[:, s, lo:lo + 512], xs_t[:, s, k * P:(k + 1) * P],
                                      w1[:, ds(e * (DC * HID) + (k * HID + lo), 512)], start=(k == 0), stop=False)
                        mm = pe.matmul(h_ps[:, s, lo:lo + 512], pick[:, ds(e * P, P)], bias1[:, lo:lo + 512],
                                       start=False, stop=True)
                    mm.then_inc(h_made[s], 1)

                def layer2(q, s, n):
                    e = expert(q)
                    if not (isinstance(n, int) and n == 0 and s == 0):
                        pe.wait_ge(y_taken[1 - s], n + s)
                    pe.matmul(y_ps[:, 0:D], pick[:, ds(e * P, P)], bias2[:, :], start=True, stop=False)
                    for k in range(KC):
                        if k % (KC // 2) == 0:
                            pe.wait_ge(h_copied[k // (KC // 2)], 2 * n + s + 1)
                        mm = pe.matmul(y_ps[:, 0:D], h_t[:, k * P:(k + 1) * P], w2[:, ds(e * (KC * D) + k * D, D)],
                                       start=False, stop=(k == KC - 1))
                    mm.then_inc(y_made[s], 1)

                def step(q, s, n, last):
                    if not (isinstance(q, int) and q == 0):
                        turn_h(1 - s, n - 1 + s)
                    layer1(q, s, n)
                    if not last:
                        turn_x(1 - s, n + s)
                    if not (isinstance(q, int) and q == 0):
                        layer2(q - 1, 1 - s, n - 1 + s)

                turn_x(0, 0)
                over_tiles(pe, STS, step)
                turn_h(0, STS // 2)
                layer2(STS - 1, 0, STS // 2)

            @block.scalar
            def _(act):
                def gelu(q, s, n, last):
                    act.wait_ge(h_made[s], n + 1)
                    if not (isinstance(n, int) and n == 0):
                        act.wait_ge(h_turned[1], 2 * n - 1 + s)
                    act.sem_inc(gate7, 1)
                    act.activation(h[:, s, :], h_ps[:, s, :], ACT.Gelu).then_inc(h_gelu[s], 1)

                over_tiles(act, STS, gelu)

            @block.vector
            def _(dve):
                def copy_x(s, n):
                    slot_free(dve, h_made[s], n)
                    dve.wait_ge(xs_turned[s], n + 1)
                    dve.tensor_copy(xs_t[:, s, :], tp[:, 0:D]).then_inc(xs_copied[s], 1)

                def finish(s, n):
                    for g in range(2):
                        if g == 0 and not (isinstance(n, int) and n == 0 and s == 0):
                            dve.wait_ge(y_made[1 - s], n + s)
                        dve.wait_ge(h_turned[g], 2 * n + s + 1)
                        dve.tensor_copy(h_t[:, g * 512:(g + 1) * 512], ht_ps[:, g * 512:(g + 1) * 512]) \
                            .then_inc(h_copied[g], 1)

                def take(s, n):
                    slot_free(dve, y_stored[s], n, 16)
                    dve.wait_ge(y_made[s], n + 1)
                    dve.tensor_copy(y[:, s, :], y_ps[:, 0:D]).then_inc(y_taken[s], 1)

                def step(q, s, n, last):
                    first = isinstance(q, int) and q == 0
                    if not first:
                        finish(1 - s, n - 1 + s)
                    if not last:
                        copy_x(1 - s, n + s)
                    if not first:
                        take(1 - s, n - 1 + s)

                copy_x(0, 0)
                over_tiles(dve, STS, step)
                finish(0, STS // 2)
                take(0, STS // 2)

            @block.gpsimd
            def _(pool):
                def store(q, s, n, last):
                    pool.wait_ge(y_taken[s], n + 1)
                    pool.sem_inc(gate7s, 1)
                    pool.dma_start(slot_y[ds(q * P, P), :], y[:, s, :]).then_inc(y_stored[s], 16)

                over_tiles(pool, STS, store)
                pool.wait_ge(y_stored[0], 16 * (STS // 2 + 1))
                pool.wait_ge(y_stored[1], 16 * (STS // 2))

        next_phase()

        with ExitStack() as s8:
            yg = s8.enter_context(nc.sbuf_tensor("yg", [P, 2, 2, D], F32))
            o = s8.enter_context(nc.sbuf_tensor("o", [P, 2, D], F32))
            half_o = s8.enter_context(nc.sbuf_tensor("half_o", [P, 2, D], F32))
            slot_g = s8.enter_context(nc.sbuf_tensor("slot_g", [P, 2, 2], I32))
            slot_copied8 = named("slot_copied8")
            y_back = [[named(f"y_back{k}{j}") for j in range(2)] for k in range(2)]
            halved = [named(f"halved{k}") for k in range(2)]
            o_made = [named(f"o_made{k}") for k in range(2)]
            o_stored = [named(f"o_stored{k}") for k in range(2)]
            gate8 = named("gate8")
            block = s8.enter_context(nc.Block())

            @block.gpsimd
            def _(pool):
                def gather(t, s, n, last):
                    slot_free(pool, o_made[s], n)
                    pool.sem_inc(gate8, 1)
                    pool.tensor_copy(slot_g[:, s, :], slot_i[:, ds(t, 1), :].rearrange("p a k -> p (a k)")) \
                        .then_inc(slot_copied8, 1)
                    pool.wait_ge(slot_copied8, t + 1)
                    pool.sem_inc(gate8, 1)
                    for k in range(2):
                        pool.indirect_dma_start(yg[:, s, k, :], None, slot_y,
                                                bass.IndirectOffsetOnAxis(ap=slot_g[:, s, k:k + 1], axis=0)) \
                            .then_inc(y_back[s][k], 16)

                over_tiles(pool, NT, gather)

            @block.vector
            def _(dve):
                def combine(t, s, n, last):
                    slot_free(dve, o_stored[s], n, 16)
                    for k, (src_t, dst_t, made) in enumerate(((qx[:, ds(t * D, D)], half_o[:, s, :], halved[s]),
                                                              (half_o[:, s, :], o[:, s, :], o_made[s]))):
                        dve.wait_ge(y_back[s][k], 16 * n + 16)
                        dve.scalar_tensor_tensor(out=dst_t, in0=yg[:, s, k, :],
                                                 scalar=w_top[:, ds(t, 1), k:k + 1].rearrange("p a k -> p (a k)"),
                                                 in1=src_t, op0=ALU.mult, op1=ALU.add).then_inc(made, 1)
                        if k == 0:
                            dve.wait_ge(halved[s], n + 1)

                over_tiles(dve, NT, combine)

            @block.sync
            def _(sp):
                def store(t, s, n, last):
                    sp.wait_ge(o_made[s], n + 1)
                    sp.dma_start(out[ds(t * P, P), :], o[:, s, :]).then_inc(o_stored[s], 16)

                over_tiles(sp, NT, store)
                sp.wait_ge(o_stored[0], 16 * (NT // 2 + 1))
                sp.wait_ge(o_stored[1], 16 * (NT // 2))


def kernel(x, src, dst, edge_attr_64, edge_weight, L0_gnn_ln_g, L0_gnn_ln_b, L0_gnn_Wq, L0_gnn_bq, L0_gnn_Wk,
           L0_gnn_bk, L0_gnn_Wv, L0_gnn_bv, L0_gnn_Wo, L0_gnn_bo, L0_gnn_Wdk, L0_gnn_bdk, L0_gnn_Wdv, L0_gnn_bdv,
           L0_ffn_Wr, L0_ffn_br, L0_ffn_ln_g, L0_ffn_ln_b, L0_ffn_W1, L0_ffn_b1, L0_ffn_W2, L0_ffn_b2):
    import numpy as np
    import concourse.bacc as bacc
    from concourse.bass_utils import run_bass_kernel_spmd

    def padded(v, rows, fill=0):
        v = np.asarray(v)
        return np.concatenate([v, np.full((rows - v.shape[0],) + v.shape[1:], fill, v.dtype)])

    def columns(v):
        v = np.asarray(v)
        return np.moveaxis(v.reshape(v.shape[:-1] + (DC, P)), -1, 0)

    edges = ET * P
    arrays = {
        "x": padded(x, NT * P),
        "src": padded(src, edges).reshape(ET, P),
        "dst": padded(dst, edges, N - 1).reshape(ET, P),
        "edge_weight": padded(edge_weight, edges, CUT).reshape(ET, P),
        "edge_attr_t": padded(edge_attr_64, edges).reshape(ET, P, R).transpose(0, 2, 1),
        "wqkv_t": np.concatenate([np.asarray(w).T for w in (L0_gnn_Wk, L0_gnn_Wv, L0_gnn_Wq)], 1),
        "bqkv": np.concatenate([np.asarray(b) for b in (L0_gnn_bk, L0_gnn_bv, L0_gnn_bq)])[None],
        "gnn_g": columns(L0_gnn_ln_g),
        "gnn_b": columns(L0_gnn_ln_b),
        "wd_t": np.concatenate([np.concatenate([np.asarray(w).T, np.asarray(b)[None]])
                                for w, b in ((L0_gnn_Wdk, L0_gnn_bdk), (L0_gnn_Wdv, L0_gnn_bdv))], 1),
        "wo_t": np.asarray(L0_gnn_Wo).T,
        "bo": np.asarray(L0_gnn_bo)[None],
        "wr": L0_ffn_Wr,
        "br": np.asarray(L0_ffn_br)[None],
        "ffn_g": columns(L0_ffn_ln_g),
        "ffn_b": columns(L0_ffn_ln_b),
        "w1": L0_ffn_W1,
        "b1": np.repeat(np.asarray(L0_ffn_b1), 3, 0),
        "w2": L0_ffn_W2,
        "b2": np.repeat(np.asarray(L0_ffn_b2), 3, 0),
        "part_mask": np.tile(np.eye(3, dtype=np.float32), (NE, 1)),
        "pick": np.repeat(np.repeat(np.eye(NE, dtype=np.float32), 3, 0), P, 1),
    }
    arrays = {f"in_{name}": np.ascontiguousarray(v) for name, v in arrays.items()}
    nc = bacc.Bacc("TRN2", target_bir_lowering=False, num_devices=1)
    access = {name[3:]: nc.dram_tensor(name, v.shape, mybir.dt.from_np(v.dtype), kind="ExternalInput").ap()
              for name, v in arrays.items()}
    out = nc.dram_tensor("out_x", (NT * P, D), F32, kind="ExternalOutput").ap()
    build_program(nc, access, out)
    result = run_bass_kernel_spmd(nc, [arrays], core_ids=[0])
    return result.results[0]["out_x"][:N]
```

```python
import math
from contextlib import ExitStack

import concourse.bass as bass
from concourse import mybir

P = 128
N = 6250
E = 100000
D = 256
R = 64
NE = 8
HID = 1024
DC = D // P
KC = HID // P
NT = -(-N // P)
ET = -(-E // P)
EPS = 1e-5
CUT = 5.0

U = 12
PAIRS = U // 2
ITEMS_IT = 2 * U
CH = 120
HALVES_CH = CH // U
GROUPS = PAIRS // 2
HOT_LAG = 3
Q_LAG = 1
SUM_LAG = 3
MAX_CH = -(-(2 * -(-ET // 2) * NT) // CH)
MAX_ITEMS = MAX_CH * CH
MAX_IT = MAX_ITEMS // ITEMS_IT
FULL = ET // P
REST = ET - FULL * P
STS = (2 * NT * P + NE * (P - 1)) // P

F32 = mybir.dt.float32
I32 = mybir.dt.int32
BF16 = mybir.dt.bfloat16
F32R = mybir.dt.float32r
ALU = mybir.AluOpType
ACT = mybir.ActivationFunctionType
AX = mybir.AxisListType.X


def ds(start, size):
    return bass.ds(start, size)


def over_tiles(eng, count, body):
    for t in range(2):
        body(t, t, 0, False)
    with eng.Fori(1, count // 2) as i:
        for s in range(2):
            body(2 * i + s, s, i, False)
    if count % 2:
        body(count - 1, 0, count // 2, True)


def slot_free(eng, sem, n, per=1):
    if not (isinstance(n, int) and n == 0):
        eng.wait_ge(sem, n * per)


class Chain:

    def __init__(self, eng, sem):
        self.eng, self.sem, self.n = eng, sem, 0

    def __call__(self, ins):
        self.n += 1
        ins.then_inc(self.sem, 1)
        self.eng.wait_ge(self.sem, self.n)


def build_program(nc, a, out):
    ctx = ExitStack()
    with ctx:
        def dram(name, shape, dt=F32):
            return nc.dram_tensor(name, shape, dt, kind="Internal").ap()

        kv_table = dram("kv_table", [NT * P, 2 * D])
        res_table = dram("res_table", [NT * P, D])
        range_rows = dram("range_rows", [2, (FULL + 1) * P])
        meta_cols = dram("meta_cols", [MAX_ITEMS // U, P, 3 * U])
        rel_rows = dram("rel_rows", [MAX_ITEMS, P], BF16)
        item_tab = dram("item_tab", [2, MAX_ITEMS], I32)
        slot_x = dram("slot_x", [STS * P, D])
        slot_y = dram("slot_y", [STS * P, D])

        in_use = []

        def named(name):
            in_use.append(nc.alloc_semaphore(name))
            return in_use[-1]

        def next_phase():
            nc.clear_and_free_semaphores(in_use)
            in_use.clear()
            nc.all_engine_barrier()

        def outer(name, shape, dt=F32):
            return ctx.enter_context(nc.sbuf_tensor(name, shape, dt))

        ident = outer("ident", [P, P])
        iota_free = outer("iota_free", [P, P])
        iota_part = outer("iota_part", [P, 1])
        ones = outer("ones", [P, P])
        n_run = outer("n_run", [P, 2], I32)
        stats = outer("stats", [P, NT, 6])
        ln_s = outer("ln_s", [P, 8, NT])
        slot_i = outer("slot_i", [P, NT, 2], I32)
        w_top = outer("w_top", [P, NT, 2])
        expert_i = outer("expert_i", [1, STS], I32)

        agg_room, q_room = ExitStack(), ExitStack()
        agg = agg_room.enter_context(nc.sbuf_tensor("agg", [P, NT * D], F32))[:, :]
        q_hi = q_room.enter_context(nc.sbuf_tensor("q_hi", [P, NT * D], F32R, side="right"))[:, :]
        q_lo = q_room.enter_context(nc.sbuf_tensor("q_lo", [P, NT * D], F32R, side="right"))[:, :]

        mean, var, rstd, rstd2, bias_r, bias_s, tmp_a, tmp_b = (ln_s[:, k, :] for k in range(8))

        def norm_scales(dve, act_sem, chain, sqrt_sem, step):
            def refine(dst, v):
                chain(dve.reciprocal(dst, tmp_b))
                chain(dve.tensor_tensor(tmp_b, dst, dst, ALU.mult))
                chain(dve.tensor_tensor(tmp_b, tmp_b, tmp_a, ALU.mult))
                chain(dve.tensor_scalar(tmp_b, tmp_b, -0.5, 1.5, ALU.mult, ALU.add))
                chain(dve.tensor_tensor(dst, dst, tmp_b, ALU.mult))

            ev, od = stats[:, :, 1], stats[:, :, 4]
            chain(dve.tensor_tensor(mean, ev, od, ALU.add))
            chain(dve.tensor_scalar(mean, mean, 0.5, None, ALU.mult))
            chain(dve.tensor_tensor(tmp_a, ev, od, ALU.subtract))
            chain(dve.tensor_scalar(tmp_a, tmp_a, 0.5, None, ALU.mult))
            chain(dve.tensor_tensor(tmp_a, tmp_a, tmp_a, ALU.mult))
            chain(dve.tensor_tensor(var, stats[:, :, 2], stats[:, :, 5], ALU.add))
            chain(dve.scalar_tensor_tensor(out=var, in0=var, scalar=1.0 / D, in1=tmp_a, op0=ALU.mult, op1=ALU.add))
            dve.tensor_scalar(tmp_a, var, EPS, None, ALU.add).then_inc(sqrt_sem, 1)
            dve.wait_ge(act_sem, step + 1)
            refine(rstd, tmp_a)
            chain(dve.tensor_tensor(tmp_a, rstd, rstd, ALU.mult))
            chain(dve.tensor_tensor(tmp_a, tmp_a, var, ALU.mult))
            dve.tensor_scalar(tmp_a, tmp_a, EPS, None, ALU.add).then_inc(sqrt_sem, 1)
            dve.wait_ge(act_sem, step + 2)
            refine(rstd2, tmp_a)
            chain(dve.tensor_tensor(rstd2, rstd2, rstd, ALU.mult))
            chain(dve.scalar_tensor_tensor(out=bias_r, in0=mean, scalar=-1.0, in1=rstd, op0=ALU.mult, op1=ALU.mult))
            chain(dve.scalar_tensor_tensor(out=bias_s, in0=mean, scalar=-1.0, in1=rstd2, op0=ALU.mult, op1=ALU.mult))

        def norm_roots(act, act_sem, sqrt_sem):
            for k in range(2):
                act.wait_ge(sqrt_sem, k + 1)
                act.activation(tmp_b, tmp_a, ACT.Sqrt).then_inc(act_sem, 1)

        with ExitStack() as s1:
            def sb(name, shape, dt=F32):
                return s1.enter_context(nc.sbuf_tensor(name, shape, dt))

            def ps(name, shape):
                return s1.enter_context(nc.psum_tensor(name, shape, F32))

            def sem(name):
                return named(name)

            xt = agg.rearrange("p (t d) -> p t d", d=D)
            wqkv = sb("wqkv", [P, DC, 3 * D])
            g_col = sb("g_col", [P, DC])
            b_col = sb("b_col", [P, DC])
            b_rep = sb("b_rep", [P, DC, P])
            bias_in = sb("bias_in", [1, 3 * D])
            bias_all = sb("bias_all", [P, 3 * D])
            normed = sb("normed", [P, 2, D])
            normed_t = sb("normed_t", [P, 2, D])
            kv_out = sb("kv_out", [P, 2, 2 * D])
            q_out = sb("q_out", [P, 2, D])
            tp = ps("tp", [P, 2, 512])
            proj = ps("proj", [P, 2, 1024])

            s_x = [sem(f"s_x{k}") for k in range(7)]
            s_w = sem("s_w")
            s_bin = sem("s_bin")
            s_const = sem("s_const")
            s_chain = sem("s_chain")
            s_stats = sem("s_stats")
            s_var = sem("s_var")
            s_root = sem("s_root")
            s_scales = sem("s_scales")
            s_fold = sem("s_fold")
            s_bias_mm = sem("s_bias_mm")
            s_bias = sem("s_bias")
            normed_made = [sem(f"normed_made{k}") for k in range(2)]
            res_made = sem("res_made")
            transposed = [sem(f"transposed{k}") for k in range(2)]
            copied = [sem(f"copied{k}") for k in range(2)]
            projected = [sem(f"projected{k}") for k in range(2)]
            evacuated = [sem(f"evacuated{k}") for k in range(2)]
            kv_stored = [sem(f"kv_stored{k}") for k in range(2)]
            q_rounded = [sem(f"q_rounded{k}") for k in range(2)]
            q_split = [sem(f"q_split{k}") for k in range(2)]
            gate_q = sem("gate_q")
            gate = sem("gate1")
            s_res = sem("s_res")
            block = s1.enter_context(nc.Block())

            G = NT // 7
            x_rows = a["x"].rearrange("(t p) d -> p t d", p=P)

            @block.sync
            def _(sp):
                for k in range(7):
                    sp.dma_start(xt[:, k * G:(k + 1) * G, :], x_rows[:, k * G:(k + 1) * G, :]).then_inc(s_x[k], 16)
                sp.dma_start(wqkv[:, :, :], a["wqkv_t"].rearrange("(c p) n -> p c n", p=P)).then_inc(s_w, 16)
                sp.dma_start(g_col[:, :], a["gnn_g"]).then_inc(s_w, 16)
                sp.dma_start(b_col[:, :], a["gnn_b"]).then_inc(s_w, 16)
                sp.dma_start(bias_in[:, :], a["bqkv"]).then_inc(s_bin, 16)

                def store(t, s, n, last):
                    sp.wait_ge(evacuated[s], 2 * (n + 1))
                    sp.dma_start(kv_table[ds(t * P, P), :], kv_out[:, s, :]).then_inc(kv_stored[s], 16)

                over_tiles(sp, NT, store)
                sp.wait_ge(res_made, NT)
                sp.dma_start(res_table.rearrange("(t p) d -> p t d", p=P), xt[:, :, :]).then_inc(s_res, 16)
                sp.wait_ge(s_res, 16)
                sp.wait_ge(kv_stored[0], 16 * (NT // 2 + 1))
                sp.wait_ge(kv_stored[1], 16 * (NT // 2))

            @block.gpsimd
            def _(pool):
                c = Chain(pool, s_const)
                c(pool.memset(ones[:, :], 1.0))
                c(pool.affine_select(out=ident[:, :], in_=ones[:, :], compare_op=ALU.is_equal, fill=0.0, base=0,
                                     pattern=[[-1, P]], channel_multiplier=1))
                c(pool.iota(iota_free[:, :], pattern=[[1, P]], base=0, channel_multiplier=0,
                            allow_small_or_imprecise_dtypes=True))
                c(pool.iota(iota_part[:, :], pattern=[[0, 1]], base=0, channel_multiplier=1,
                            allow_small_or_imprecise_dtypes=True))

                def rest_of_q(t, s, n, last):
                    pool.wait_ge(q_rounded[s], n + 1)
                    pool.sem_inc(gate_q, 1)
                    pool.tensor_tensor(q_lo[:, ds(t * D, D)], q_out[:, s, :], q_hi[:, ds(t * D, D)].bitcast(F32),
                                       ALU.subtract) \
                        .then_inc(q_split[s], 1)

                over_tiles(pool, NT, rest_of_q)

            @block.scalar
            def _(act):
                norm_roots(act, s_root, s_var)
                act.wait_ge(s_scales, 1)

                def normalise(t, s, n, last):
                    slot_free(act, transposed[s], n)
                    act.sem_inc(gate, 1)
                    act.activation(normed[:, s, :], agg[:, ds(t * D, D)], ACT.Identity, scale=rstd2[:, ds(t, 1)],
                                   bias=bias_s[:, ds(t, 1)]).then_inc(normed_made[s], 1)
                    act.activation(agg[:, ds(t * D, D)], agg[:, ds(t * D, D)], ACT.Identity,
                                   scale=tmp_a[:, ds(t, 1)], bias=bias_r[:, ds(t, 1)]).then_inc(res_made, 1)

                def step(t, s, n, last):
                    normalise(t, s, n, last)
                    if not (isinstance(n, int) and n == 0):
                        q_hi_of(t - 2, s, n - 1)

                def q_hi_of(t, s, n):
                    act.wait_ge(evacuated[s], 2 * n + 2)
                    act.sem_inc(gate, 1)
                    act.activation(q_hi[:, ds(t * D, D)], q_out[:, s, :], ACT.Copy).then_inc(q_rounded[s], 1)

                over_tiles(act, NT, step)
                for t in (NT - 2, NT - 1):
                    q_hi_of(t, t % 2, t // 2)

            @block.vector
            def _(dve):
                c = Chain(dve, s_chain)
                for k in range(7):
                    dve.wait_ge(s_x[k], 16)
                    with dve.Fori(k * G, (k + 1) * G) as t:
                        dve.bn_stats(stats[:, ds(t, 1), :].rearrange("p a b -> p (a b)"), agg[:, ds(t * D, D)]) \
                            .then_inc(s_stats, 1)
                dve.wait_ge(s_stats, NT)
                norm_scales(dve, s_root, c, s_var, 0)
                dve.tensor_scalar(tmp_a, rstd, 1.0, None, ALU.add).then_inc(s_scales, 1)
                dve.wait_ge(s_w, 48)
                dve.wait_ge(s_const, 4)
                for k in range(DC):
                    dve.tensor_scalar(b_rep[:, k, :], ones[:, :], b_col[:, k:k + 1], None, ALU.mult).then_inc(s_fold, 1)
                dve.wait_ge(s_bias_mm, 1)
                for k in range(DC):
                    dve.tensor_scalar(wqkv[:, k, :], wqkv[:, k, :], g_col[:, k:k + 1], None, ALU.mult).then_inc(s_fold, 1)
                dve.tensor_copy(bias_all[:, :], proj[:, 0, 0:3 * D]).then_inc(s_bias, 1)
                dve.wait_ge(s_bias, 1)

                def copy(s, n):
                    slot_free(dve, projected[s], n)
                    dve.wait_ge(transposed[s], n + 1)
                    dve.tensor_copy(normed_t[:, s, :], tp[:, s, 0:D]).then_inc(copied[s], 1)

                def evacuate(t, s, n, last):
                    if not last:
                        copy(1 - s, n + s)
                    slot_free(dve, kv_stored[s], n, 16)
                    dve.wait_ge(projected[s], n + 1)
                    dve.tensor_tensor(kv_out[:, s, :], proj[:, s, 0:2 * D], bias_all[:, 0:2 * D], ALU.add) \
                        .then_inc(evacuated[s], 1)
                    slot_free(dve, q_split[s], n)
                    dve.tensor_tensor(q_out[:, s, :], proj[:, s, 2 * D:3 * D], bias_all[:, 2 * D:3 * D],
                                      ALU.add).then_inc(evacuated[s], 1)

                copy(0, 0)
                over_tiles(dve, NT, evacuate)

            @block.tensor
            def _(pe):
                pe.wait_ge(s_fold, DC)
                pe.wait_ge(s_w, 48)
                pe.wait_ge(s_bin, 16)
                for lo, hi in ((0, 512), (512, 3 * D)):
                    for k in range(DC):
                        pe.matmul(proj[:, 0, lo:hi], b_rep[:, k, :], wqkv[:, k, lo:hi], start=(k == 0), stop=False)
                    mm = pe.matmul(proj[:, 0, lo:hi], ones[0:1, :], bias_in[:, lo:hi], start=False, stop=True)
                mm.then_inc(s_bias_mm, 1)
                pe.wait_ge(s_fold, 2 * DC)
                pe.wait_ge(s_bias, 1)

                def transposes(s, n):
                    slot_free(pe, copied[s], n)
                    pe.wait_ge(normed_made[s], n + 1)
                    for k in range(DC):
                        mm = pe.transpose(tp[:, s, k * P:(k + 1) * P], normed[:, s, k * P:(k + 1) * P], ident[:, :])
                    mm.then_inc(transposed[s], 1)

                def products(t, s, n, last):
                    if not last:
                        transposes(1 - s, n + s)
                    slot_free(pe, evacuated[s], n, 2)
                    pe.wait_ge(copied[s], n + 1)
                    for lo, hi in ((0, 512), (512, 3 * D)):
                        for k in range(DC):
                            mm = pe.matmul(proj[:, s, lo:hi], normed_t[:, s, k * P:(k + 1) * P], wqkv[:, k, lo:hi],
                                           start=(k == 0), stop=(k == DC - 1))
                    mm.then_inc(projected[s], 1)

                transposes(0, 0)
                over_tiles(pe, NT, products)

        next_phase()

        with ExitStack() as s2:
            def sb(name, shape, dt=F32):
                return s2.enter_context(nc.sbuf_tensor(name, shape, dt))

            def sem(name):
                return named(name)

            dst_rows = sb("dst_rows", [P, FULL + 1, P], I32)
            least = sb("least", [P, 2, FULL + 1])
            block_i = sb("block_i", [P, 2, FULL + 1], I32)
            block_f = sb("block_f", [P, 2, FULL + 1])
            ranges = sb("ranges", [P, 2, ET])
            meets = sb("meets", [P, ET])
            pairs_i = sb("pairs_i", [P, 1], I32)
            of_block = sb("of_block", [P, 3])
            spread = sb("spread", [P, 3, P])
            by_block = sb("by_block", [P, 3, P])
            upto = sb("upto", [P, NT])
            count = sb("count", [P, 1])
            offset = sb("offset", [P, NT])
            iota_row = sb("iota_row", [P, MAX_IT])
            junk = sb("junk", [P, MAX_IT])
            n_f = sb("n_f", [P, 2])
            zero = sb("zero", [P, 7 * D])
            j_col = sb("j_col", [P, 1])
            blk_col = sb("blk_col", [P, 1])
            tile_col = sb("tile_col", [P, 1])
            last_col = sb("last_col", [P, 1])
            void_col = sb("void_col", [P, 1])
            base_col = sb("base_col", [P, 1])
            tab_i = sb("tab_i", [P, 2], I32)
            src_g = sb("src_g", [P, P], I32)
            dst_g = sb("dst_g", [P, P], I32)
            ew_g = sb("ew_g", [P, P])
            ew_turn = sb("ew_turn", [P, P])
            ew_whole = sb("ew_whole", [P, P], I32)
            half_pi = sb("half_pi", [P, 1])
            metas = sb("metas", [P, 3, P])
            rel_b = sb("rel_b", [P, P], BF16)
            meta_out = sb("meta_out", [P, HALVES_CH, 3, U])
            meta_ps = s2.enter_context(nc.psum_tensor("meta_ps", [P, 3, 512], F32))

            s_dst = sem("s_dst")
            s_c2 = sem("s_c2")
            s_pc2 = sem("s_pc2")
            s_blocks = sem("s_blocks")
            s_rng_st = sem("s_rng_st")
            s_rng = sem("s_rng")
            s_iota = sem("s_iota")
            s_zero = sem("s_zero")
            s_zfill = sem("s_zfill")
            s_spread = sem("s_spread")
            s_by_block = sem("s_by_block")
            s_count = sem("s_count")
            s_link = sem("s_link")
            tiles_known = sem("tiles_known")
            gathered = sem("gathered")
            turn_ready = sem("turn_ready")
            abs_made = sem("abs_made")
            sin_made = sem("sin_made")
            metas_made = sem("metas_made")
            metas_turned = sem("metas_turned")
            meta_copied = sem("meta_copied")
            chunk_stored = sem("chunk_stored")
            chunk_free = sem("chunk_free")
            gate_p = sem("gate_p2")
            gate_a = sem("gate_a2")
            block = s2.enter_context(nc.Block())

            @block.sync
            def _(sp):
                sp.sem_inc(chunk_free, 1)
                sp.dma_start(dst_rows[:, 0:FULL, :],
                             a["dst"][0:FULL * P, :].rearrange("(c p) e -> p c e", p=P)).then_inc(s_dst, 16)
                sp.dma_start(dst_rows[0:REST, FULL, :], a["dst"][FULL * P:ET, :]).then_inc(s_dst, 16)
                sp.wait_ge(s_blocks, 1)
                for k in range(2):
                    with nc.allow_non_contiguous_dma(reason="a column of seven numbers a partition"):
                        sp.dma_start(range_rows[k].rearrange("(c p) -> p c", p=P), block_f[:, k, :]) \
                            .then_inc(s_rng_st, 16)
                sp.wait_ge(s_rng_st, 32)
                sp.dma_start(ranges[:, :, :], range_rows[:, 0:ET].unsqueeze(0).to_broadcast([P, 2, ET])) \
                    .then_inc(s_rng, 16)
                sp.wait_ge(s_count, 1)
                chunks = sp.value_load(n_run[0:1, 1:2], min_val=1, max_val=MAX_CH)
                with sp.Fori(0, chunks) as c:
                    sp.wait_ge(meta_copied, c + 1)
                    sp.dma_start(meta_cols[ds(c * HALVES_CH, HALVES_CH)].rearrange("h p m -> p h m"),
                                 meta_out[:, :, :, :].rearrange("p h k u -> p h (k u)")).then_inc(chunk_stored, 16)
                    sp.dma_start(rel_rows[ds(c * CH, CH), :], rel_b[0:CH, :]).then_inc(chunk_stored, 16)
                    with nc.allow_non_contiguous_dma(reason="one number a partition"):
                        for k in range(2):
                            sp.dma_start(item_tab[k, ds(c * CH, CH)].unsqueeze(1), tab_i[0:CH, k:k + 1]) \
                                .then_inc(chunk_stored, 16)
                    sp.wait_ge(chunk_stored, 64 * c + 64)
                    sp.sem_inc(chunk_free, 1)

            @block.gpsimd
            def _(pool):
                c = Chain(pool, s_pc2)
                pool.iota(iota_row[:, :], pattern=[[1, MAX_IT]], base=0, channel_multiplier=0,
                          allow_small_or_imprecise_dtypes=True).then_inc(s_iota, 1)
                pool.iota(j_col[:, :], pattern=[[0, 1]], base=-CH, channel_multiplier=1,
                          allow_small_or_imprecise_dtypes=True).then_inc(s_iota, 1)
                pool.memset(zero[:, :], 0.0).then_inc(s_zero, 1)
                c(pool.memset(agg, 0.0))
                pool.wait_ge(s_count, 1)
                chunks = pool.value_load(n_run[0:1, 1:2], min_val=1, max_val=MAX_CH)
                with pool.Fori(0, chunks) as k:
                    pool.wait_ge(tiles_known, k + 1)
                    pool.sem_inc(gate_p, 1)
                    for row, name in ((src_g, "src"), (dst_g, "dst"), (ew_g, "edge_weight")):
                        pool.indirect_dma_start(row[0:CH, :], None, a[name],
                                                bass.IndirectOffsetOnAxis(ap=tab_i[0:CH, 0:1], axis=0)) \
                            .then_inc(gathered, 16)

            @block.vector
            def _(dve):
                c = Chain(dve, s_c2)
                c(dve.memset(least[:, :, :], 0.0))
                dve.memset(half_pi[:, :], math.pi / 2).then_inc(s_c2, 1)
                c.n += 1
                dve.wait_ge(s_dst, 32)
                for k, op in ((0, ALU.min), (1, ALU.max)):
                    c(dve.tensor_reduce(least[:, k, 0:FULL], dst_rows[:, 0:FULL, :], AX, op))
                    c(dve.tensor_reduce(least[0:REST, k, FULL:FULL + 1], dst_rows[0:REST, FULL, :], AX, op))
                c(dve.tensor_copy(block_i[:, :, :], least[:, :, :]))
                c(dve.tensor_scalar(block_i[:, :, :], block_i[:, :, :], 7, None, ALU.arith_shift_right))
                c(dve.tensor_copy(block_f[:, :, :], block_i[:, :, :]))
                dve.sem_inc(s_blocks, 1)
                dve.wait_ge(s_rng, 16)
                dve.wait_ge(s_iota, 2)
                c(dve.tensor_scalar(meets[:, :], ranges[:, 0, :], iota_part[:, 0:1], None, ALU.is_le))
                c(dve.scalar_tensor_tensor(out=meets[:, :], in0=ranges[:, 1, :], scalar=iota_part[:, 0:1],
                                           in1=meets[:, :], op0=ALU.is_ge, op1=ALU.mult))
                c(dve.scalar_tensor_tensor(out=junk[:, 0:ET], in0=iota_row[:, 0:ET], scalar=1.0, in1=meets[:, :],
                                           op0=ALU.add, op1=ALU.mult))
                c(dve.tensor_reduce(of_block[:, 2:3], junk[:, 0:ET], AX, ALU.max))
                c(dve.scalar_tensor_tensor(out=junk[:, 0:ET], in0=iota_row[:, 0:ET], scalar=-float(ET),
                                           in1=meets[:, :], op0=ALU.add, op1=ALU.mult))
                c(dve.tensor_reduce(of_block[:, 1:2], junk[:, 0:ET], AX, ALU.min))
                c(dve.tensor_scalar(of_block[:, 1:2], of_block[:, 1:2], float(ET), None, ALU.add))
                c(dve.tensor_tensor(of_block[:, 0:1], of_block[:, 2:3], of_block[:, 1:2], ALU.subtract))
                c(dve.tensor_scalar(pairs_i[:, :], of_block[:, 0:1], 0.0, 1.0, ALU.max, ALU.add))
                c(dve.tensor_scalar(pairs_i[:, :], pairs_i[:, :], 1, None, ALU.arith_shift_right))
                c(dve.tensor_scalar(of_block[:, 0:1], pairs_i[:, :], 2.0, None, ALU.mult))
                c(dve.tensor_scalar(of_block[:, 2:3], of_block[:, 2:3], -1.0, None, ALU.add))
                for m in range(3):
                    c(dve.tensor_scalar(spread[:, m, :], ident[:, :], of_block[:, m:m + 1], None, ALU.mult))
                dve.sem_inc(s_spread, 1)
                dve.wait_ge(s_by_block, 1)
                c(dve.tensor_copy(by_block[:, :, :].rearrange("p m b -> p (m b)"), meta_ps[:, 0, 0:3 * P]))
                c(dve.tensor_tensor_scan(upto[:, :], ones[:, 0:NT], by_block[:, 0, 0:NT], 0.0, ALU.mult, ALU.add))
                c(dve.tensor_tensor(offset[:, :], by_block[:, 1, 0:NT], upto[:, :], ALU.subtract))
                c(dve.tensor_tensor(offset[:, :], offset[:, :], by_block[:, 0, 0:NT], ALU.add))
                for k, n, per, most in ((0, upto[:, NT - 1:NT], ITEMS_IT, MAX_IT),
                                        (1, n_f[:, 0:1], CH // ITEMS_IT, MAX_CH)):
                    c(dve.tensor_scalar(count[:, 0:1], n, 1.0 / per, None, ALU.mult))
                    c(dve.tensor_scalar(junk[:, 0:most], iota_row[:, 0:most], count[:, 0:1], None, ALU.is_lt,
                                        ALU.add, accum_out=n_f[:, k:k + 1]))
                c(dve.tensor_scalar(n_f[:, 0:1], n_f[:, 0:1], -1.0, None, ALU.add))
                c(dve.tensor_copy(n_run[:, :], n_f[:, :]))
                dve.sem_inc(s_count, 1)
                chunks = dve.value_load(n_run[0:1, 1:2], min_val=1, max_val=MAX_CH)
                LINKS = 17
                with dve.Fori(0, chunks) as k:
                    done = 0

                    def link(ins):
                        nonlocal done
                        done += 1
                        ins.then_inc(s_link, 1)
                        dve.wait_ge(s_link, k * LINKS + done)

                    dve.wait_ge(chunk_free, k + 1)
                    link(dve.tensor_scalar(j_col[:, :], j_col[:, :], float(CH), None, ALU.add))
                    link(dve.tensor_scalar(junk[:, 0:NT - 1], upto[:, 0:NT - 1], j_col[:, 0:1], None, ALU.is_le,
                                           ALU.add, accum_out=blk_col[:, :]))
                    link(dve.scalar_tensor_tensor(out=junk[:, 0:NT], in0=iota_row[:, 0:NT], scalar=blk_col[:, 0:1],
                                                  in1=offset[:, :], op0=ALU.is_equal, op1=ALU.mult,
                                                  accum_out=tile_col[:, :]))
                    link(dve.scalar_tensor_tensor(out=junk[:, 0:NT], in0=iota_row[:, 0:NT], scalar=blk_col[:, 0:1],
                                                  in1=by_block[:, 2, 0:NT], op0=ALU.is_equal, op1=ALU.mult,
                                                  accum_out=last_col[:, :]))
                    link(dve.tensor_tensor(tile_col[:, :], tile_col[:, :], j_col[:, :], ALU.add))
                    link(dve.tensor_tensor(void_col[:, :], tile_col[:, :], last_col[:, :], ALU.is_gt))
                    link(dve.tensor_tensor(tile_col[:, :], tile_col[:, :], last_col[:, :], ALU.min))
                    link(dve.tensor_scalar(tile_col[:, :], tile_col[:, :], 0.0, None, ALU.max))
                    dve.tensor_copy(tab_i[:, 0:1], tile_col[:, :]).then_inc(tiles_known, 1)
                    link(dve.tensor_scalar(void_col[:, :], void_col[:, :], -float(1 << 20), None, ALU.mult))
                    link(dve.scalar_tensor_tensor(out=base_col[:, :], in0=blk_col[:, :], scalar=float(P),
                                                  in1=void_col[:, :], op0=ALU.mult, op1=ALU.add))
                    link(dve.tensor_copy(tab_i[:, 1:2], blk_col[:, :]))
                    dve.wait_ge(gathered, 48 * k + 48)
                    link(dve.tensor_scalar(ew_turn[0:CH, :], ew_g[0:CH, :], 0.5 / CUT, None, ALU.mult))
                    link(dve.tensor_copy(ew_whole[0:CH, :], ew_turn[0:CH, :]))
                    dve.tensor_tensor(ew_turn[0:CH, :], ew_turn[0:CH, :], ew_whole[0:CH, :], ALU.subtract) \
                        .then_inc(turn_ready, 1)
                    dve.tensor_copy(metas[0:CH, 0, :], src_g[0:CH, :]).then_inc(metas_made, 1)
                    link(dve.tensor_scalar(metas[0:CH, 1, :], dst_g[0:CH, :], base_col[0:CH, 0:1], -1.0,
                                           ALU.subtract, ALU.max))
                    link(dve.tensor_scalar(metas[0:CH, 1, :], metas[0:CH, 1, :], float(P), None, ALU.min))
                    dve.tensor_copy(rel_b[0:CH, :], metas[0:CH, 1, :]).then_inc(metas_made, 1)
                    dve.wait_ge(sin_made, k + 1)
                    link(dve.tensor_scalar(ew_turn[0:CH, :], ew_turn[0:CH, :], 0.5, 0.5, ALU.mult, ALU.add))
                    link(dve.scalar_tensor_tensor(out=metas[0:CH, 2, :], in0=ew_g[0:CH, :], scalar=CUT,
                                                  in1=ew_turn[0:CH, :], op0=ALU.is_lt, op1=ALU.mult))
                    dve.sem_inc(metas_made, 1)
                    assert done == LINKS
                    dve.wait_ge(metas_turned, k + 1)
                    for m in range(3):
                        ins = dve.tensor_copy(meta_out[:, :, m, :],
                                              meta_ps[:, m, 0:CH].rearrange("p (h u) -> p h u", u=U))
                    ins.then_inc(meta_copied, 1)

            @block.scalar
            def _(act):
                act.wait_ge(s_zero, 1)
                for k in range(-(-STS // 7)):
                    n = min(7, STS - 7 * k)
                    act.dma_start(slot_x[7 * k * P:(7 * k + n) * P, :].rearrange("(p r) d -> p (r d)", p=P),
                                  zero[:, 0:n * D]).then_inc(s_zfill, 16)
                act.wait_ge(s_count, 1)
                chunks = act.value_load(n_run[0:1, 1:2], min_val=1, max_val=MAX_CH)
                with act.Fori(0, chunks) as k:
                    act.wait_ge(turn_ready, k + 1)
                    act.sem_inc(gate_a, 1)
                    act.activation(ew_turn[0:CH, :], ew_turn[0:CH, :], ACT.Abs).then_inc(abs_made, 1)
                    act.wait_ge(abs_made, k + 1)
                    act.sem_inc(gate_a, 1)
                    act.activation(ew_turn[0:CH, :], ew_turn[0:CH, :], ACT.Sin, scale=-2.0 * math.pi,
                                   bias=half_pi[0:CH, 0:1]).then_inc(sin_made, 1)
                act.wait_ge(s_zfill, 16 * -(-STS // 7))

            @block.tensor
            def _(pe):
                pe.wait_ge(s_spread, 1)
                pe.matmul(meta_ps[:, 0, 0:3 * P], ones[:, :], spread[:, :, :].rearrange("p m b -> p (m b)"),
                          start=True, stop=True).then_inc(s_by_block, 1)
                pe.wait_ge(s_count, 1)
                chunks = pe.value_load(n_run[0:1, 1:2], min_val=1, max_val=MAX_CH)
                with pe.Fori(0, chunks) as k:
                    pe.wait_ge(metas_made, 3 * k + 3)
                    for m in range(3):
                        mm = pe.transpose(meta_ps[:, m, 0:CH], metas[0:CH, m, :], ident[0:CH, 0:CH])
                    mm.then_inc(metas_turned, 1)

        next_phase()

        with ExitStack() as s3:
            def sb(name, shape, dt=F32):
                return s3.enter_context(nc.sbuf_tensor(name, shape, dt))

            def ps(name, shape):
                return s3.enter_context(nc.psum_tensor(name, shape, F32))

            def sem(name):
                return named(name)

            kv_in = sb("kv_in", [P, U, 2 * D])
            w_in = kv_in[:, 0, :]
            b_in = kv_in[0:2, 1, :]
            b_hi = kv_in[0:2, 2, :]
            w_hi = sb("w_hi", [P, 2 * D], F32R)
            w_lo = sb("w_lo", [P, 2 * D], F32R)
            b_parts = sb("b_parts", [2, 2 * D], F32R)
            part_sel = sb("part_sel", [2, 2])
            ones_r = sb("ones_r", [2, P], F32R)
            ea_in = sb("ea_in", [P, U, P])
            ea_parts = sb("ea_parts", [P, U, P], F32R)
            src_in = sb("src_in", [P, 2, U])
            meta_in = sb("meta_in", [P, 2, 2, U])
            rel_in = sb("rel_in", [P, GROUPS, 4 * P], BF16)
            tiles_in = sb("tiles_in", [1, 2, U], I32)
            blocks_in = sb("blocks_in", [1, 2, U], I32)
            src_i = sb("src_i", [P, 2, U], I32)
            distance = stats[:, :, :].rearrange("p t s -> p (t s)").bitcast(BF16)[:, 0:4 * P]
            onehot_t = sb("onehot_t", [P, GROUPS, 4 * P], F32R)
            onehot = sb("onehot", [P, 3, 2, P])
            logit = sb("logit", [P, 3, 2])
            gated = sb("gated", [P, 3, 2])
            attn = sb("attn", [P, 3, 2])
            neg_part = sb("neg_part", [P, 1])
            dkv = ps("dkv", [P, 3, 2, 2 * D])
            q_ps = ps("q_ps", [P, 2, D])
            agg_ps = ps("agg_ps", [P, 512])

            s_wd = sem("s_wd")
            s_w_hi = sem("s_w_hi")
            s_w_parts = sem("s_w_parts")
            s_npart = sem("s_npart")
            kv_landed = [sem(f"kv_landed{u}") for u in range(U)]
            ea_landed = [sem(f"ea_landed{p}") for p in range(PAIRS)]
            meta_landed = [sem(f"meta_landed{h}") for h in range(2)]
            rel_landed = [sem(f"rel_landed{g}") for g in range(GROUPS)]
            tiles_landed = [sem(f"tiles_landed{h}") for h in range(2)]
            blocks_landed = [sem(f"blocks_landed{h}") for h in range(2)]
            src_landed = [sem(f"src_landed{h}") for h in range(2)]
            src_ready = sem("src_ready")
            gate_pool = sem("gate_pool3")
            gate_act = sem("gate_act3")
            gate_sp = sem("gate_sp3")
            gate_pe = sem("gate_pe3")
            gate_dve = sem("gate_dve3")

            def each(name):
                return [sem(f"{name}{p}") for p in range(3)]

            ea_rounded = each("ea_rounded")
            ea_split = each("ea_split")
            turned = each("turned")
            onehot_t_made = each("onehot_t_made")
            dkv_made = each("dkv_made")
            dkv_silu = each("dkv_silu")
            q_made = each("q_made")
            kd_made = each("kd_made")
            onehot_made = each("onehot_made")
            logit_made = each("logit_made")
            logit_silu = each("logit_silu")
            attn_made = each("attn_made")
            msg_made = each("msg_made")
            sum_made = each("sum_made")
            added = each("added")
            block = s3.enter_context(nc.Block())

            def before(h, half, p, lag):
                return (h, half, p - lag) if p >= lag else (1 - h, half - 1, p - lag + PAIRS)

            def landed(h, half):
                return 16 if isinstance(half, int) else 8 * (half - h) + 16

            def exists(half):
                return not (isinstance(half, int) and half < 0)

            def done(eng, sems, at):
                h, half, p = at
                if exists(half):
                    eng.wait_ge(sems[p % 3], 2 * half + p // 3 + 1)

            def group_done(eng, sems, half, g):
                if exists(half):
                    eng.wait_ge(sems[g], half + 1)

            def half_steps(eng, body, drain=None):
                for h in range(2):
                    body(h, h)
                more = eng.value_load(n_run[0:1, 0:1], min_val=1, max_val=MAX_IT - 1)
                with eng.Fori(1, more + 1) as i:
                    for h in range(2):
                        body(h, 2 * i + h)
                if drain:
                    drain(0, 2 * more + 2)

            @block.sync
            def _(sp):
                sp.dma_start(w_in, a["wd_t"]).then_inc(s_wd, 16)
                sp.dma_start(b_in, a["bd"]).then_inc(s_wd, 16)
                sp.dma_start(part_sel[:, :], a["part_sel"]).then_inc(s_wd, 16)

                def half_step(h, half):
                    with nc.allow_non_contiguous_dma(reason="twelve numbers a partition"):
                        sp.dma_start(tiles_in[:, h, :], item_tab[0, ds(half * U, U)].unsqueeze(0)) \
                            .then_inc(tiles_landed[h], 16)
                        if not isinstance(half, int):
                            sp.wait_ge(src_ready, half - 1)
                        sp.dma_start(src_in[:, h, :], meta_cols[ds(half, 1), :, 0:U].rearrange("a p m -> (a p) m")) \
                            .then_inc(src_landed[h], 16)
                    sp.wait_ge(tiles_landed[h], landed(h, half))
                    sp.sem_inc(gate_sp, 1)
                    for p in range(PAIRS):
                        if p % 2 == 0:
                            group_done(sp, turned, half - 1, p // 2)
                            sp.dma_start(rel_in[:, p // 2, :],
                                         rel_rows[ds(half * U + 2 * p, 4), :].rearrange("u e -> (u e)")
                                         .unsqueeze(0).to_broadcast([P, 4 * P])).then_inc(rel_landed[p // 2], 16)
                        t = sp.value_load(tiles_in[0:1, h, 2 * p:2 * p + 1], min_val=0, max_val=ET - 1)
                        group_done(sp, ea_split, half - 1, p // 2)
                        sp.dma_start(ea_in[:, 2 * p:2 * p + 2, :], a["edge_attr_t"][ds(t, 2)]
                                     .rearrange("a r e -> r a e")).then_inc(ea_landed[p], 16)
                    done(sp, added, (h, half - 2, PAIRS - 1))
                    with nc.allow_non_contiguous_dma(reason="twelve numbers"):
                        sp.dma_start(blocks_in[:, h, :], item_tab[1, ds(half * U, U)].unsqueeze(0)) \
                            .then_inc(blocks_landed[h], 16)
                    sp.dma_start(meta_in[:, h, :, :].rearrange("p k u -> p (k u)"),
                                 meta_cols[ds(half, 1), :, U:3 * U].rearrange("a p m -> (a p) m")) \
                        .then_inc(meta_landed[h], 16)

                half_steps(sp, half_step)

            @block.gpsimd
            def _(pool):
                pool.wait_ge(s_w_parts, 4)
                pool.sem_inc(gate_pool, 1)
                pool.tensor_scalar(neg_part[:, :], iota_part[:, :], -1.0, None, ALU.mult).then_inc(s_npart, 1)

                def rest_of_edges(half, g):
                    group_done(pool, ea_rounded, half, g)
                    pool.sem_inc(gate_pool, 1)
                    lo = ea_parts[0:R, 4 * g:4 * g + 4, :]
                    pool.tensor_tensor(lo, ea_in[0:R, 4 * g:4 * g + 4, :], lo.bitcast(F32), ALU.subtract) \
                        .then_inc(ea_split[g], 1)

                def half_step(h, half):
                    pool.wait_ge(src_landed[h], landed(h, half))
                    pool.sem_inc(gate_pool, 1)
                    pool.tensor_copy(src_i[:, h, :], src_in[:, h, :]).then_inc(src_ready, 1)
                    pool.wait_ge(src_ready, half + 1)
                    pool.sem_inc(gate_pool, 1)
                    for p in range(PAIRS):
                        done(pool, sum_made, (1 - h, half - 1, p))
                        pool.sem_inc(gate_pool, 1)
                        for u in (2 * p, 2 * p + 1):
                            pool.indirect_dma_start(kv_in[:, u, :], None, kv_table,
                                                    bass.IndirectOffsetOnAxis(ap=src_i[:, h, u:u + 1], axis=0)) \
                                .then_inc(kv_landed[u], 16)
                        if p % 2 == 0:
                            rest_of_edges(half, p // 2)

                half_steps(pool, half_step)

            @block.scalar
            def _(act):
                act.wait_ge(s_wd, 48)
                act.activation(w_hi[:, :], w_in, ACT.Copy).then_inc(s_w_hi, 1)
                act.activation(b_hi.bitcast(F32R), b_in, ACT.Copy).then_inc(s_w_hi, 1)
                act.wait_ge(s_npart, 1)

                def group_ahead(h, half, g):
                    act.wait_ge(rel_landed[g], 16 * half + 16)
                    act.sem_inc(gate_act, 1)
                    group_done(act, onehot_t_made, *((half - 1, GROUPS - 1) if g == 0 else (half, g - 1)))
                    act.sem_inc(gate_act, 1)
                    act.activation(distance, rel_in[:, g, :], ACT.Abs,
                                   bias=neg_part[:, 0:1]).then_inc(turned[g], 1)
                    for p in (2 * g, 2 * g + 1):
                        act.wait_ge(ea_landed[p], 16 * half + 16)
                        act.sem_inc(gate_act, 1)
                    done(act, dkv_made, (1 - h, half - 1, 2 * g + 1))
                    act.sem_inc(gate_act, 1)
                    act.activation(ea_parts[:, 4 * g:4 * g + 4, :], ea_in[:, 4 * g:4 * g + 4, :], ACT.Copy) \
                        .then_inc(ea_rounded[g], 1)
                    done(act, q_made, (1 - h, half - 1, 2 * g + 1))
                    act.sem_inc(gate_act, 1)
                    group_done(act, turned, half, g)
                    act.sem_inc(gate_act, 1)
                    act.activation(onehot_t[:, g, :], distance, ACT.Relu, bias=1.0,
                                   scale=-1.0).then_inc(onehot_t_made[g], 1)

                def silu(at):
                    h, half, p = at
                    if exists(half):
                        done(act, dkv_made, at)
                        act.sem_inc(gate_act, 1)
                        act.activation(dkv[:, p % 3, :, :], dkv[:, p % 3, :, :], ACT.Silu).then_inc(dkv_silu[p % 3], 1)

                def attention(at):
                    h, half, p = at
                    if exists(half):
                        done(act, logit_made, at)
                        act.sem_inc(gate_act, 1)
                        act.activation(gated[:, p % 3, :], logit[:, p % 3, :], ACT.Silu).then_inc(logit_silu[p % 3], 1)

                def half_step(h, half):
                    for p in range(PAIRS):
                        if p % 2 == 0:
                            group_ahead(h, half, p // 2)
                        silu(before(h, half, p, 2))
                        attention(before(h, half, p, 3))

                def drain(h, half):
                    silu(before(h, half, 0, 2))
                    attention(before(h, half, 0, 3))
                    silu(before(h, half, 0, 1))
                    attention(before(h, half, 0, 2))
                    attention(before(h, half, 0, 1))

                half_steps(act, half_step, drain)

            @block.tensor
            def _(pe):
                pe.wait_ge(s_w_parts, 4)

                def products(h, half, p):
                    group_done(pe, ea_split, half, p // 2)
                    done(pe, msg_made, before(h, half, p, 3))
                    for k in range(2):
                        o = dkv[:, p % 3, k, :]
                        pe.matmul(o, ea_parts[:, 2 * p + k, :], w_hi[:, :], start=True, stop=False)
                        pe.matmul(o, ea_parts[:, 2 * p + k, :], w_lo[:, :], start=False, stop=False)
                        mm = pe.matmul(o, ones_r[:, :], b_parts[:, :], start=False, stop=True)
                    mm.then_inc(dkv_made[p % 3], 1)

                def q_rows(at):
                    h, half, p = at
                    if exists(half):
                        if p == 0:
                            pe.wait_ge(blocks_landed[h], landed(h, half))
                        group_done(pe, onehot_t_made, half, p // 2)
                        done(pe, logit_made, before(h, half, p, 1))
                        pe.sem_inc(gate_pe, 1)
                        b = pe.value_load(blocks_in[0:1, h, 2 * p:2 * p + 1], min_val=0, max_val=NT - 1)
                        for k in range(2):
                            hot = onehot_t[:, p // 2, (2 * p + k) % 4 * P:((2 * p + k) % 4 + 1) * P]
                            pe.matmul(q_ps[:, k, :], hot, q_hi[:, ds(b * D, D)], start=True, stop=False)
                            mm = pe.matmul(q_ps[:, k, :], hot, q_lo[:, ds(b * D, D)], start=False, stop=True)
                        mm.then_inc(q_made[p % 3], 1)

                def sums(at):
                    h, half, p = at
                    if exists(half):
                        done(pe, onehot_made, at)
                        done(pe, msg_made, at)
                        done(pe, added, before(h, half, p, 1))
                        for k in range(2):
                            mm = pe.matmul(agg_ps[:, 0:D], onehot[:, p % 3, k, :], kv_in[:, 2 * p + k, D:2 * D],
                                           start=(k == 0), stop=(k == 1))
                        mm.then_inc(sum_made[p % 3], 1)

                def half_step(h, half):
                    for p in range(PAIRS):
                        products(h, half, p)
                        q_rows(before(h, half, p, Q_LAG))
                        sums(before(h, half, p, SUM_LAG))

                def drain(h, half):
                    for p in range(SUM_LAG):
                        if p < Q_LAG:
                            q_rows(before(h, half, 0, Q_LAG - p))
                        sums(before(h, half, 0, SUM_LAG - p))

                half_steps(pe, half_step, drain)

            @block.vector
            def _(dve):
                dve.wait_ge(s_w_hi, 2)
                dve.tensor_copy(ones_r[:, :], ones[0:2, :]).then_inc(s_w_parts, 1)
                dve.tensor_tensor(w_lo[:, :], w_in, w_hi[:, :].bitcast(F32), ALU.subtract).then_inc(s_w_parts, 1)
                dve.tensor_scalar(b_in, b_in, part_sel[:, 0:1], None, ALU.mult).then_inc(s_w_parts, 1)
                dve.wait_ge(s_w_parts, 3)
                dve.scalar_tensor_tensor(out=b_parts[:, :], in0=b_hi, scalar=part_sel[:, 1:2],
                                         in1=b_in, op0=ALU.mult, op1=ALU.add).then_inc(s_w_parts, 1)

                def k_dk(h, half, p):
                    done(dve, dkv_silu, (h, half, p))
                    for k in range(2):
                        dve.wait_ge(kv_landed[2 * p + k], 16 * half + 16)
                    kd = kv_in[:, 2 * p:2 * p + 2, 0:D]
                    dve.tensor_tensor(kd, kd, dkv[:, p % 3, :, 0:D], ALU.mult).then_inc(kd_made[p % 3], 1)

                def one_hots(h, half, p):
                    if p == 0:
                        dve.wait_ge(meta_landed[h], landed(h, half))
                    done(dve, sum_made, before(h, half, p, 3))
                    for k in range(2):
                        ins = dve.tensor_scalar(onehot[:, p % 3, k, :], iota_free[:, :],
                                                meta_in[:, h, 0, 2 * p + k:2 * p + k + 1], None, ALU.is_equal)
                    ins.then_inc(onehot_made[p % 3], 1)

                def logits(h, half, p):
                    done(dve, q_made, (h, half, p))
                    done(dve, kd_made, (h, half, p))
                    for k in range(2):
                        kd = kv_in[:, 2 * p + k, 0:D]
                        ins = dve.tensor_tensor_reduce(kd, kd, q_ps[:, k, :], 1.0, 0.0, ALU.mult, ALU.add,
                                                       logit[:, p % 3, k:k + 1])
                    ins.then_inc(logit_made[p % 3], 1)

                def cutoff(at):
                    h, half, p = at
                    if exists(half):
                        done(dve, logit_silu, at)
                        dve.tensor_tensor(attn[:, p % 3, :], gated[:, p % 3, :],
                                          meta_in[:, h, 1, 2 * p:2 * p + 2], ALU.mult).then_inc(attn_made[p % 3], 1)

                def messages(at):
                    h, half, p = at
                    if exists(half):
                        done(dve, attn_made, at)
                        for k in range(2):
                            v = kv_in[:, 2 * p + k, D:2 * D]
                            ins = dve.scalar_tensor_tensor(out=v, in0=v, scalar=attn[:, p % 3, k:k + 1],
                                                           in1=dkv[:, p % 3, k, D:2 * D], op0=ALU.mult, op1=ALU.mult)
                        ins.then_inc(msg_made[p % 3], 1)

                def add(at):
                    h, half, p = at
                    if exists(half):
                        if p == 0:
                            dve.wait_ge(blocks_landed[h], landed(h, half))
                            dve.sem_inc(gate_dve, 1)
                        b = dve.value_load(blocks_in[0:1, h, 2 * p:2 * p + 1], min_val=0, max_val=NT - 1)
                        done(dve, sum_made, at)
                        done(dve, added, before(h, half, p, 1))
                        dve.tensor_tensor(agg[:, ds(b * D, D)], agg[:, ds(b * D, D)], agg_ps[:, 0:D],
                                          ALU.add).then_inc(added[p % 3], 1)

                def half_step(h, half):
                    for p in range(PAIRS):
                        k_dk(h, half, p)
                        cutoff(before(h, half, p, 1))
                        one_hots(h, half, p)
                        messages(before(h, half, p, 1))
                        add(before(h, half, p, SUM_LAG))
                        logits(h, half, p)

                def drain(h, half):
                    cutoff(before(h, half, 0, 1))
                    messages(before(h, half, 0, 1))
                    for lag in range(SUM_LAG, 0, -1):
                        add(before(h, half, 0, lag))

                half_steps(dve, half_step, drain)

        q_room.close()
        qx = ctx.enter_context(nc.sbuf_tensor("qx", [P, NT * D], F32, side="right"))[:, :]
        w1 = ctx.enter_context(nc.sbuf_tensor("w1_all", [P, NE * DC * HID], F32, side="right"))[:, :]

        def late(name, shape, dt=F32):
            return ctx.enter_context(nc.sbuf_tensor(name, shape, dt, side="right"))

        BR = 3 * NE
        bias1 = late("bias1", [P, HID], BF16)
        bias2 = late("bias2", [P, D], BF16)
        pick = late("pick_sb", [P, NE * P], BF16)

        next_phase()

        with ExitStack() as s4:
            def sb(name, shape, dt=F32):
                return s4.enter_context(nc.sbuf_tensor(name, shape, dt))

            def ps(name, shape):
                return s4.enter_context(nc.psum_tensor(name, shape, F32))

            wo = sb("wo", [P, DC, D])
            bo = sb("bo_sb", [1, D])
            offs = sb("offs", [P, NE, DC])
            offs_rep = sb("offs_rep", [P, NE, DC, BR])
            b1_in = sb("b1_in", [BR, HID])
            b2_in = sb("b2_in", [BR, D])
            mask = sb("mask", [BR, 3])
            pick_in = sb("pick_in", [BR, NE * P])
            part_b = sb("part_b", [BR, HID], BF16)
            agg_in = sb("agg_in", [P, 2, D])
            agg_t = sb("agg_t", [P, 2, D])
            tp = ps("tp4", [P, 2, 512])
            prod = ps("prod", [P, 2, 512])
            b1_ps = ps("b1_ps", [BR, HID])
            res_landed = [named(f"res_landed{k}") for k in range(7)]
            wo_landed = named("wo_landed")
            small_landed = named("small_landed")
            w1_landed = named("w1_landed")
            rep_made = named("rep_made")
            bias_mm = named("bias_mm4")
            turned4 = [named(f"turned4_{k}") for k in range(2)]
            copied4 = [named(f"copied4_{k}") for k in range(2)]
            prod_made = [named(f"prod_made{k}") for k in range(2)]
            x2_made = [named(f"x2_made{k}") for k in range(2)]
            stats_made = named("stats_made4")
            staged = [named(f"staged{k}") for k in range(2)]
            gate4 = named("gate4")
            s_c4 = named("s_c4")
            s_var4 = named("s_var4")
            s_root4 = named("s_root4")
            block = s4.enter_context(nc.Block())
            G = NT // 7

            @block.sync
            def _(sp):
                sp.dma_start(wo[:, :, :], a["wo_t"].rearrange("(c p) n -> p c n", p=P)).then_inc(wo_landed, 16)
                sp.dma_start(bo[:, :], a["bo"]).then_inc(wo_landed, 16)
                for k in range(7):
                    sp.dma_start(qx[:, k * G * D:(k + 1) * G * D].rearrange("p (t d) -> p t d", d=D),
                                 res_table[k * G * P:(k + 1) * G * P, :].rearrange("(t p) d -> p t d", p=P)) \
                        .then_inc(res_landed[k], 16)
                for tile, name in ((offs[:, :, :], "ffn_b"), (b1_in[:, :], "b1"), (b2_in[:, :], "b2"),
                                   (mask[:, :], "part_mask"), (pick_in[:, :], "pick")):
                    sp.dma_start(tile, a[name]).then_inc(small_landed, 16)
                for e in range(NE):
                    sp.dma_start(w1[:, e * DC * HID:(e + 1) * DC * HID].rearrange("p (c h) -> p c h", c=DC),
                                 a["w1"][e].rearrange("(c p) h -> p c h", p=P)).then_inc(w1_landed, 16)
                sp.wait_ge(w1_landed, 16 * NE)

            @block.scalar
            def _(act):
                def stage(t, s, n, last):
                    slot_free(act, turned4[s], n)
                    act.sem_inc(gate4, 1)
                    act.activation(agg_in[:, s, :], agg[:, ds(t * D, D)], ACT.Copy).then_inc(staged[s], 1)

                over_tiles(act, NT, stage)
                norm_roots(act, s_root4, s_var4)

            @block.tensor
            def _(pe):
                pe.wait_ge(wo_landed, 32)

                def transposes(s, n):
                    slot_free(pe, copied4[s], n)
                    pe.wait_ge(staged[s], n + 1)
                    for k in range(DC):
                        mm = pe.transpose(tp[:, s, k * P:(k + 1) * P], agg_in[:, s, k * P:(k + 1) * P], ident[:, :])
                    mm.then_inc(turned4[s], 1)

                def product(t, s, n, last):
                    if not last:
                        transposes(1 - s, n + s)
                    slot_free(pe, x2_made[s], n)
                    pe.wait_ge(copied4[s], n + 1)
                    for k in range(DC):
                        pe.matmul(prod[:, s, 0:D], agg_t[:, s, k * P:(k + 1) * P], wo[:, k, :], start=(k == 0),
                                  stop=False)
                    pe.matmul(prod[:, s, 0:D], ones[0:1, :], bo[:, :], start=False, stop=True) \
                        .then_inc(prod_made[s], 1)

                transposes(0, 0)
                over_tiles(pe, NT, product)
                pe.wait_ge(rep_made, 1)
                pe.wait_ge(w1_landed, 16 * NE)
                for e in range(NE):
                    for c in range(DC):
                        for lo in range(0, HID, 512):
                            mm = pe.matmul(b1_ps[:, lo:lo + 512], offs_rep[:, e, c, :],
                                           w1[:, (e * DC + c) * HID + lo:(e * DC + c) * HID + lo + 512],
                                           start=(e == 0 and c == 0), stop=(e == NE - 1 and c == DC - 1))
                mm.then_inc(bias_mm, 1)

            @block.vector
            def _(dve):
                c = Chain(dve, s_c4)

                def copy(s, n):
                    slot_free(dve, prod_made[s], n)
                    dve.wait_ge(turned4[s], n + 1)
                    dve.tensor_copy(agg_t[:, s, :], tp[:, s, 0:D]).then_inc(copied4[s], 1)

                def add(t, s, n, last):
                    if not last:
                        copy(1 - s, n + s)
                    dve.wait_ge(prod_made[s], n + 1)
                    dve.tensor_tensor(qx[:, ds(t * D, D)], qx[:, ds(t * D, D)], prod[:, s, 0:D], ALU.add) \
                        .then_inc(x2_made[s], 1)
                    dve.wait_ge(x2_made[s], n + 1)
                    dve.bn_stats(stats[:, ds(t, 1), :].rearrange("p a b -> p (a b)"), qx[:, ds(t * D, D)]) \
                        .then_inc(stats_made, 1)

                for k in range(7):
                    dve.wait_ge(res_landed[k], 16)
                copy(0, 0)
                over_tiles(dve, NT, add)
                dve.wait_ge(stats_made, NT)
                norm_scales(dve, s_root4, c, s_var4, 0)
                dve.wait_ge(small_landed, 16 * 5)
                c(dve.memset(offs_rep[:, :, :, :], 0.0))
                for e in range(NE):
                    ins = dve.tensor_copy(offs_rep[:, e, :, 3 * e:3 * e + 3],
                                          offs[:, e, :].unsqueeze(2).to_broadcast([P, DC, 3]))
                ins.then_inc(rep_made, 1)
                c(dve.memset(pick[:, :], 0.0))
                c(dve.memset(bias1[:, :], 0.0))
                c(dve.memset(bias2[:, :], 0.0))
                c(dve.tensor_copy(pick[0:BR, :], pick_in[:, :]))
                dve.wait_ge(bias_mm, 1)
                c(dve.tensor_tensor(b1_in[:, :], b1_in[:, :], b1_ps[:, :], ALU.add))
                for full, out_b, n in ((b1_in, bias1, HID), (b2_in, bias2, D)):
                    c(dve.tensor_copy(part_b[:, 0:n], full[:, :]))
                    c(dve.tensor_scalar(out_b[0:BR, :], part_b[:, 0:n], mask[:, 0:1], None, ALU.mult))
                    for m in range(1, 3):
                        c(dve.tensor_tensor(full[:, :], full[:, :], part_b[:, 0:n], ALU.subtract))
                        c(dve.tensor_copy(part_b[:, 0:n], full[:, :]))
                        c(dve.scalar_tensor_tensor(out=out_b[0:BR, :], in0=part_b[:, 0:n], scalar=mask[:, m:m + 1],
                                                   in1=out_b[0:BR, :], op0=ALU.mult, op1=ALU.add))

        next_phase()

        agg_room.close()
        w2 = ctx.enter_context(nc.sbuf_tensor("w2_all", [P, NE * KC * D], F32))[:, :]

        with ExitStack() as s5:
            def sb(name, shape, dt=F32):
                return s5.enter_context(nc.sbuf_tensor(name, shape, dt))

            def ps(name, shape):
                return s5.enter_context(nc.psum_tensor(name, shape, F32))

            wr = sb("wr_sb", [P, DC, NE])
            br = sb("br_sb", [1, NE])
            gains = sb("gains", [P, NE, DC])
            z = sb("z", [P, 2, D])
            z_t = sb("z_t", [P, 2, D])
            tri = sb("tri", [P, P])
            down = sb("down", [P, NE])
            rows = sb("rows", [P, NT])
            tiles = sb("tiles", [P, STS])
            lg = sb("lg", [P, NT, NE])
            hot1 = sb("hot1", [P, NT, NE])
            hot2 = sb("hot2", [P, NT, NE])
            work = sb("work", [P, NT, NE])
            cum = sb("cum", [P, NE, NT])
            cmp = sb("cmp", [P, NE, NT])
            over = sb("over", [1, STS, NE - 1])
            m1 = sb("m1", [P, NT])
            m2 = sb("m2", [P, NT])
            d12 = sb("d12", [P, NT])
            n_tiles = sb("n_tiles", [P, NE])
            end = sb("end", [P, NE])
            base = sb("base", [P, NE])
            slot_f = sb("slot_f", [P, NT, 2])
            expert_f = sb("expert_f", [1, STS])
            tp = ps("tp5", [P, 2, 512])
            lg_ps = ps("lg_ps", [P, 512])
            rank = ps("rank", [P, 512])
            total = ps("total", [P, 512])
            wr_landed = named("wr_landed")
            gains_landed = named("gains_landed")
            w2_landed = named("w2_landed")
            w1_scaled = named("w1_scaled")
            z_made = [named(f"z_made{k}") for k in range(2)]
            turned5 = [named(f"turned5_{k}") for k in range(2)]
            copied5 = [named(f"copied5_{k}") for k in range(2)]
            lg_made = [named(f"lg_made{k}") for k in range(2)]
            gate5 = named("gate5")
            gap_made = named("gap_made")
            exp_made = named("exp_made")
            hot_made = named("hot_made")
            ranks_made = named("ranks_made")
            const5 = named("const5")
            s_c5 = named("s_c5")
            block = s5.enter_context(nc.Block())

            @block.sync
            def _(sp):
                sp.dma_start(wr[:, :, :], a["wr"].rearrange("(c p) e -> p c e", p=P)).then_inc(wr_landed, 16)
                sp.dma_start(br[:, :], a["br"]).then_inc(wr_landed, 16)
                sp.dma_start(gains[:, :, :], a["ffn_g"]).then_inc(gains_landed, 16)
                for e in range(NE):
                    sp.dma_start(w2[:, e * KC * D:(e + 1) * KC * D].rearrange("p (k d) -> p k d", k=KC),
                                 a["w2"][e].rearrange("(k p) d -> p k d", p=P)).then_inc(w2_landed, 16)
                sp.wait_ge(w2_landed, 16 * NE)

            @block.gpsimd
            def _(pool):
                c = Chain(pool, const5)
                c(pool.affine_select(out=tri[:, :], in_=ones[:, :], compare_op=ALU.is_gt, fill=0.0, base=0,
                                     pattern=[[1, P]], channel_multiplier=-1))
                c(pool.iota(down[:, :], pattern=[[-1, NE]], base=NE, channel_multiplier=0,
                            allow_small_or_imprecise_dtypes=True))
                c(pool.iota(rows[:, :], pattern=[[P, NT]], base=0, channel_multiplier=0,
                            allow_small_or_imprecise_dtypes=True))
                c(pool.iota(tiles[:, :], pattern=[[1, STS]], base=0, channel_multiplier=0,
                            allow_small_or_imprecise_dtypes=True))
                pool.wait_ge(gains_landed, 16)
                for e in range(NE):
                    for k in range(DC):
                        w = w1[:, (e * DC + k) * HID:(e * DC + k + 1) * HID]
                        pool.tensor_scalar(w, w, gains[:, e, k:k + 1], None, ALU.mult).then_inc(w1_scaled, 1)

            @block.scalar
            def _(act):
                def norm(t, s, n, last):
                    slot_free(act, turned5[s], n)
                    act.sem_inc(gate5, 1)
                    act.activation(z[:, s, :], qx[:, ds(t * D, D)], ACT.Identity, scale=rstd[:, ds(t, 1)],
                                   bias=bias_r[:, ds(t, 1)]).then_inc(z_made[s], 1)

                over_tiles(act, NT, norm)
                act.wait_ge(gap_made, 1)
                act.activation(m2[:, :], m2[:, :], ACT.Exp).then_inc(exp_made, 1)

            @block.tensor
            def _(pe):
                pe.wait_ge(wr_landed, 32)

                def transposes(s, n):
                    slot_free(pe, copied5[s], n)
                    pe.wait_ge(z_made[s], n + 1)
                    for k in range(DC):
                        mm = pe.transpose(tp[:, s, k * P:(k + 1) * P], z[:, s, k * P:(k + 1) * P], ident[:, :])
                    mm.then_inc(turned5[s], 1)

                def logits(t, s, n, last):
                    if not last:
                        transposes(1 - s, n + s)
                    pe.wait_ge(copied5[s], n + 1)
                    o = lg_ps[:, ds(t * NE, NE)]
                    for k in range(DC):
                        pe.matmul(o, z_t[:, s, k * P:(k + 1) * P], wr[:, k, :], start=(k == 0), stop=False)
                    pe.matmul(o, ones[0:1, :], br[:, :], start=False, stop=True).then_inc(lg_made[s], 1)

                transposes(0, 0)
                over_tiles(pe, NT, logits)
                pe.wait_ge(hot_made, 1)
                pe.wait_ge(const5, 4)
                both = work[:, :, :].rearrange("p t e -> p (t e)")
                pe.matmul(rank[:, 0:NT * NE], tri[:, :], both, start=True, stop=True)
                pe.matmul(total[:, 0:NT * NE], ones[:, :], both, start=True, stop=True).then_inc(ranks_made, 1)

            @block.vector
            def _(dve):
                c = Chain(dve, s_c5)

                def copy(t, s, n, last):
                    slot_free(dve, lg_made[s], n)
                    dve.wait_ge(turned5[s], n + 1)
                    dve.tensor_copy(z_t[:, s, :], tp[:, s, 0:D]).then_inc(copied5[s], 1)

                over_tiles(dve, NT, copy)
                dve.wait_ge(lg_made[0], NT // 2 + 1)
                dve.wait_ge(lg_made[1], NT // 2)
                dve.wait_ge(const5, 4)
                c(dve.tensor_copy(lg[:, :, :].rearrange("p t e -> p (t e)"), lg_ps[:, 0:NT * NE]))
                down_b = down[:, :].unsqueeze(1).to_broadcast([P, NT, NE])

                def wide(v):
                    return v[:, :].unsqueeze(2).to_broadcast([P, NT, NE])

                def best(m, hot):
                    c(dve.tensor_reduce(m[:, :], lg[:, :, :], AX, ALU.max))
                    c(dve.tensor_tensor(work[:, :, :], lg[:, :, :], wide(m), ALU.is_ge))
                    c(dve.tensor_tensor(work[:, :, :], work[:, :, :], down_b, ALU.mult))
                    c(dve.tensor_reduce(d12[:, :], work[:, :, :], AX, ALU.max))
                    c(dve.tensor_tensor(hot[:, :, :], down_b, wide(d12), ALU.is_equal))

                best(m1, hot1)
                c(dve.scalar_tensor_tensor(out=lg[:, :, :], in0=hot1[:, :, :], scalar=-3.0e38, in1=lg[:, :, :],
                                           op0=ALU.mult, op1=ALU.add))
                best(m2, hot2)
                c(dve.tensor_tensor(work[:, :, :], hot1[:, :, :], hot2[:, :, :], ALU.add))
                dve.sem_inc(hot_made, 1)
                c(dve.tensor_tensor(m2[:, :], m2[:, :], m1[:, :], ALU.subtract))
                dve.sem_inc(gap_made, 1)
                dve.wait_ge(exp_made, 1)
                c(dve.tensor_scalar(m1[:, :], m2[:, :], 1.0, None, ALU.add))
                c(dve.reciprocal(w_top[:, :, 0], m1[:, :]))
                c(dve.tensor_tensor(w_top[:, :, 1], m2[:, :], w_top[:, :, 0], ALU.mult))
                dve.wait_ge(ranks_made, 1)
                tot = total[:, 0:NT * NE].rearrange("p (t e) -> p t e", e=NE)
                for e in range(NE):
                    c(dve.tensor_tensor_scan(cum[:, e, :], ones[:, 0:NT], tot[:, :, e], 0.0, ALU.mult, ALU.add))
                c(dve.tensor_tensor(cmp[:, :, :], cum[:, :, NT - 1:NT].to_broadcast([P, NE, NT]),
                                    rows[:, :].unsqueeze(1).to_broadcast([P, NE, NT]), ALU.is_gt))
                c(dve.tensor_reduce(n_tiles[:, :], cmp[:, :, :], AX, ALU.add))
                c(dve.tensor_tensor_scan(end[:, :], ones[:, 0:NE], n_tiles[:, :], 0.0, ALU.mult, ALU.add))
                c(dve.tensor_tensor(base[:, :], end[:, :], n_tiles[:, :], ALU.subtract))
                c(dve.tensor_scalar(base[:, :], base[:, :], float(P), None, ALU.mult))
                c(dve.tensor_tensor(work[:, :, :], cum[:, :, :].rearrange("p e t -> p t e"), tot, ALU.subtract))
                c(dve.tensor_tensor(work[:, :, :], work[:, :, :],
                                    rank[:, 0:NT * NE].rearrange("p (t e) -> p t e", e=NE), ALU.add))
                c(dve.tensor_tensor(work[:, :, :], work[:, :, :],
                                    base[:, :].unsqueeze(1).to_broadcast([P, NT, NE]), ALU.add))
                for k, hot in enumerate((hot1, hot2)):
                    c(dve.tensor_tensor(hot[:, :, :], hot[:, :, :], work[:, :, :], ALU.mult))
                    c(dve.tensor_reduce(slot_f[:, :, k], hot[:, :, :], AX, ALU.add))
                c(dve.tensor_copy(slot_i[:, :, :], slot_f[:, :, :]))
                c(dve.tensor_tensor(over[:, :, :], tiles[0:1, :].unsqueeze(2).to_broadcast([1, STS, NE - 1]),
                                    end[0:1, 0:NE - 1].unsqueeze(1).to_broadcast([1, STS, NE - 1]), ALU.is_ge))
                c(dve.tensor_reduce(expert_f[:, :], over[:, :, :], AX, ALU.add))
                c(dve.tensor_copy(expert_i[:, :], expert_f[:, :]))

        next_phase()

        with ExitStack() as s6:
            xn = s6.enter_context(nc.sbuf_tensor("xn", [P, 2, D], F32))
            slot_s = s6.enter_context(nc.sbuf_tensor("slot_s", [P, 2, 2], I32))
            xn_made = [named(f"xn_made{k}") for k in range(2)]
            slot_copied = named("slot_copied")
            scattered = [named(f"scattered{k}") for k in range(2)]
            gate6a = named("gate6a")
            gate6p = named("gate6p")
            block = s6.enter_context(nc.Block())

            @block.scalar
            def _(act):
                def norm(t, s, n, last):
                    slot_free(act, scattered[s], n, 32)
                    act.sem_inc(gate6a, 1)
                    act.activation(xn[:, s, :], qx[:, ds(t * D, D)], ACT.Identity, scale=rstd2[:, ds(t, 1)],
                                   bias=bias_s[:, ds(t, 1)]).then_inc(xn_made[s], 1)

                over_tiles(act, NT, norm)

            @block.gpsimd
            def _(pool):
                def scatter(t, s, n, last):
                    slot_free(pool, scattered[s], n, 32)
                    pool.sem_inc(gate6p, 1)
                    pool.tensor_copy(slot_s[:, s, :], slot_i[:, ds(t, 1), :].rearrange("p a k -> p (a k)")) \
                        .then_inc(slot_copied, 1)
                    pool.wait_ge(slot_copied, t + 1)
                    pool.wait_ge(xn_made[s], n + 1)
                    pool.sem_inc(gate6p, 1)
                    for k in range(2):
                        pool.indirect_dma_start(slot_x, bass.IndirectOffsetOnAxis(ap=slot_s[:, s, k:k + 1], axis=0),
                                                xn[:, s, :], None).then_inc(scattered[s], 16)

                over_tiles(pool, NT, scatter)
                pool.wait_ge(scattered[0], 32 * (NT // 2 + 1))
                pool.wait_ge(scattered[1], 32 * (NT // 2))

        next_phase()

        with ExitStack() as s7:
            def sb(name, shape, dt=F32):
                return s7.enter_context(nc.sbuf_tensor(name, shape, dt))

            def ps(name, shape):
                return s7.enter_context(nc.psum_tensor(name, shape, F32))

            xs = sb("xs", [P, 2, D])
            xs_t = sb("xs_t", [P, 2, D])
            h = sb("h", [P, 2, HID])
            h_t = sb("h_t", [P, HID])
            y = sb("y", [P, 2, D])
            tp = ps("tp7", [P, 512])
            h_ps = ps("h_ps", [P, 2, HID])
            ht_ps = ps("ht_ps", [P, HID])
            y_ps = ps("y_ps", [P, 512])
            xs_landed = [named(f"xs_landed{k}") for k in range(2)]
            xs_turned = [named(f"xs_turned{k}") for k in range(2)]
            xs_copied = [named(f"xs_copied{k}") for k in range(2)]
            h_made = [named(f"h_made{k}") for k in range(2)]
            h_gelu = [named(f"h_gelu{k}") for k in range(2)]
            h_turned = [named(f"h_turned{k}") for k in range(2)]
            h_copied = [named(f"h_copied{k}") for k in range(2)]
            y_made = [named(f"y_made{k}") for k in range(2)]
            y_taken = [named(f"y_taken{k}") for k in range(2)]
            y_stored = [named(f"y_stored{k}") for k in range(2)]
            gate7 = named("gate7")
            gate7p = named("gate7p")
            gate7s = named("gate7s")
            block = s7.enter_context(nc.Block())

            @block.sync
            def _(sp):
                def load(q, s, n, last):
                    slot_free(sp, xs_turned[s], n)
                    sp.dma_start(xs[:, s, :], slot_x[ds(q * P, P), :]).then_inc(xs_landed[s], 16)

                over_tiles(sp, STS, load)

            @block.tensor
            def _(pe):
                def turn_x(s, n):
                    pe.wait_ge(xs_landed[s], 16 * n + 16)
                    if not (isinstance(n, int) and n == 0 and s == 0):
                        pe.wait_ge(xs_copied[1 - s], n + s)
                    for k in range(DC):
                        mm = pe.transpose(tp[:, k * P:(k + 1) * P], xs[:, s, k * P:(k + 1) * P], ident[:, :])
                    mm.then_inc(xs_turned[s], 1)

                def turn_h(s, n):
                    pe.wait_ge(h_gelu[s], n + 1)
                    for g in range(2):
                        if not (isinstance(n, int) and n == 0 and s == 0):
                            pe.wait_ge(h_copied[g], 2 * n + s)
                        for k in range(KC // 2 * g, KC // 2 * (g + 1)):
                            mm = pe.transpose(ht_ps[:, k * P:(k + 1) * P], h[:, s, k * P:(k + 1) * P], ident[:, :])
                        mm.then_inc(h_turned[g], 1)

                def expert(q):
                    pe.sem_inc(gate7p, 1)
                    return pe.value_load(expert_i[0:1, ds(q, 1)], min_val=0, max_val=NE - 1)

                def layer1(q, s, n):
                    pe.wait_ge(xs_copied[s], n + 1)
                    slot_free(pe, h_gelu[s], n)
                    e = expert(q)
                    for lo in range(0, HID, 512):
                        for k in range(DC):
                            pe.matmul(h_ps[:, s, lo:lo + 512], xs_t[:, s, k * P:(k + 1) * P],
                                      w1[:, ds(e * (DC * HID) + (k * HID + lo), 512)], start=(k == 0), stop=False)
                        mm = pe.matmul(h_ps[:, s, lo:lo + 512], pick[:, ds(e * P, P)], bias1[:, lo:lo + 512],
                                       start=False, stop=True)
                    mm.then_inc(h_made[s], 1)

                def layer2(q, s, n):
                    e = expert(q)
                    if not (isinstance(n, int) and n == 0 and s == 0):
                        pe.wait_ge(y_taken[1 - s], n + s)
                    pe.matmul(y_ps[:, 0:D], pick[:, ds(e * P, P)], bias2[:, :], start=True, stop=False)
                    for k in range(KC):
                        if k % (KC // 2) == 0:
                            pe.wait_ge(h_copied[k // (KC // 2)], 2 * n + s + 1)
                        mm = pe.matmul(y_ps[:, 0:D], h_t[:, k * P:(k + 1) * P], w2[:, ds(e * (KC * D) + k * D, D)],
                                       start=False, stop=(k == KC - 1))
                    mm.then_inc(y_made[s], 1)

                def step(q, s, n, last):
                    if not (isinstance(q, int) and q == 0):
                        turn_h(1 - s, n - 1 + s)
                    layer1(q, s, n)
                    if not last:
                        turn_x(1 - s, n + s)
                    if not (isinstance(q, int) and q == 0):
                        layer2(q - 1, 1 - s, n - 1 + s)

                turn_x(0, 0)
                over_tiles(pe, STS, step)
                turn_h(0, STS // 2)
                layer2(STS - 1, 0, STS // 2)

            @block.scalar
            def _(act):
                def gelu(q, s, n, last):
                    act.wait_ge(h_made[s], n + 1)
                    if not (isinstance(n, int) and n == 0):
                        act.wait_ge(h_turned[1], 2 * n - 1 + s)
                    act.sem_inc(gate7, 1)
                    act.activation(h[:, s, :], h_ps[:, s, :], ACT.Gelu).then_inc(h_gelu[s], 1)

                over_tiles(act, STS, gelu)

            @block.vector
            def _(dve):
                def copy_x(s, n):
                    slot_free(dve, h_made[s], n)
                    dve.wait_ge(xs_turned[s], n + 1)
                    dve.tensor_copy(xs_t[:, s, :], tp[:, 0:D]).then_inc(xs_copied[s], 1)

                def finish(s, n):
                    for g in range(2):
                        if g == 0 and not (isinstance(n, int) and n == 0 and s == 0):
                            dve.wait_ge(y_made[1 - s], n + s)
                        dve.wait_ge(h_turned[g], 2 * n + s + 1)
                        dve.tensor_copy(h_t[:, g * 512:(g + 1) * 512], ht_ps[:, g * 512:(g + 1) * 512]) \
                            .then_inc(h_copied[g], 1)

                def take(s, n):
                    slot_free(dve, y_stored[s], n, 16)
                    dve.wait_ge(y_made[s], n + 1)
                    dve.tensor_copy(y[:, s, :], y_ps[:, 0:D]).then_inc(y_taken[s], 1)

                def step(q, s, n, last):
                    first = isinstance(q, int) and q == 0
                    if not first:
                        finish(1 - s, n - 1 + s)
                    if not last:
                        copy_x(1 - s, n + s)
                    if not first:
                        take(1 - s, n - 1 + s)

                copy_x(0, 0)
                over_tiles(dve, STS, step)
                finish(0, STS // 2)
                take(0, STS // 2)

            @block.gpsimd
            def _(pool):
                def store(q, s, n, last):
                    pool.wait_ge(y_taken[s], n + 1)
                    pool.sem_inc(gate7s, 1)
                    pool.dma_start(slot_y[ds(q * P, P), :], y[:, s, :]).then_inc(y_stored[s], 16)

                over_tiles(pool, STS, store)
                pool.wait_ge(y_stored[0], 16 * (STS // 2 + 1))
                pool.wait_ge(y_stored[1], 16 * (STS // 2))

        next_phase()

        with ExitStack() as s8:
            yg = s8.enter_context(nc.sbuf_tensor("yg", [P, 2, 2, D], F32))
            o = s8.enter_context(nc.sbuf_tensor("o", [P, 2, D], F32))
            half_o = s8.enter_context(nc.sbuf_tensor("half_o", [P, 2, D], F32))
            slot_g = s8.enter_context(nc.sbuf_tensor("slot_g", [P, 2, 2], I32))
            slot_copied8 = named("slot_copied8")
            y_back = [[named(f"y_back{k}{j}") for j in range(2)] for k in range(2)]
            halved = [named(f"halved{k}") for k in range(2)]
            o_made = [named(f"o_made{k}") for k in range(2)]
            o_stored = [named(f"o_stored{k}") for k in range(2)]
            gate8 = named("gate8")
            block = s8.enter_context(nc.Block())

            @block.gpsimd
            def _(pool):
                def gather(t, s, n, last):
                    slot_free(pool, o_made[s], n)
                    pool.sem_inc(gate8, 1)
                    pool.tensor_copy(slot_g[:, s, :], slot_i[:, ds(t, 1), :].rearrange("p a k -> p (a k)")) \
                        .then_inc(slot_copied8, 1)
                    pool.wait_ge(slot_copied8, t + 1)
                    pool.sem_inc(gate8, 1)
                    for k in range(2):
                        pool.indirect_dma_start(yg[:, s, k, :], None, slot_y,
                                                bass.IndirectOffsetOnAxis(ap=slot_g[:, s, k:k + 1], axis=0)) \
                            .then_inc(y_back[s][k], 16)

                over_tiles(pool, NT, gather)

            @block.vector
            def _(dve):
                def combine(t, s, n, last):
                    slot_free(dve, o_stored[s], n, 16)
                    for k, (src_t, dst_t, made) in enumerate(((qx[:, ds(t * D, D)], half_o[:, s, :], halved[s]),
                                                              (half_o[:, s, :], o[:, s, :], o_made[s]))):
                        dve.wait_ge(y_back[s][k], 16 * n + 16)
                        dve.scalar_tensor_tensor(out=dst_t, in0=yg[:, s, k, :],
                                                 scalar=w_top[:, ds(t, 1), k:k + 1].rearrange("p a k -> p (a k)"),
                                                 in1=src_t, op0=ALU.mult, op1=ALU.add).then_inc(made, 1)
                        if k == 0:
                            dve.wait_ge(halved[s], n + 1)

                over_tiles(dve, NT, combine)

            @block.sync
            def _(sp):
                def store(t, s, n, last):
                    sp.wait_ge(o_made[s], n + 1)
                    sp.dma_start(out[ds(t * P, P), :], o[:, s, :]).then_inc(o_stored[s], 16)

                over_tiles(sp, NT, store)
                sp.wait_ge(o_stored[0], 16 * (NT // 2 + 1))
                sp.wait_ge(o_stored[1], 16 * (NT // 2))


def kernel(x, src, dst, edge_attr_64, edge_weight, L0_gnn_ln_g, L0_gnn_ln_b, L0_gnn_Wq, L0_gnn_bq, L0_gnn_Wk,
           L0_gnn_bk, L0_gnn_Wv, L0_gnn_bv, L0_gnn_Wo, L0_gnn_bo, L0_gnn_Wdk, L0_gnn_bdk, L0_gnn_Wdv, L0_gnn_bdv,
           L0_ffn_Wr, L0_ffn_br, L0_ffn_ln_g, L0_ffn_ln_b, L0_ffn_W1, L0_ffn_b1, L0_ffn_W2, L0_ffn_b2):
    import numpy as np
    import concourse.bacc as bacc
    from concourse.bass_utils import run_bass_kernel_spmd

    def padded(v, rows, fill=0):
        v = np.asarray(v)
        return np.concatenate([v, np.full((rows - v.shape[0],) + v.shape[1:], fill, v.dtype)])

    def columns(v):
        v = np.asarray(v)
        return np.moveaxis(v.reshape(v.shape[:-1] + (DC, P)), -1, 0)

    edges = ET * P
    arrays = {
        "x": padded(x, NT * P),
        "src": padded(src, edges).reshape(ET, P),
        "dst": padded(dst, edges, N - 1).reshape(ET, P),
        "edge_weight": padded(edge_weight, edges, CUT).reshape(ET, P),
        "edge_attr_t": np.tile(padded(edge_attr_64, edges + P).reshape(ET + 1, P, R).transpose(0, 2, 1), (1, 2, 1)),
        "wqkv_t": np.concatenate([np.asarray(w).T for w in (L0_gnn_Wk, L0_gnn_Wv, L0_gnn_Wq)], 1),
        "bqkv": np.concatenate([np.asarray(b) for b in (L0_gnn_bk, L0_gnn_bv, L0_gnn_bq)])[None],
        "gnn_g": columns(L0_gnn_ln_g),
        "gnn_b": columns(L0_gnn_ln_b),
        "wd_t": np.tile(np.concatenate([np.asarray(L0_gnn_Wdk).T, np.asarray(L0_gnn_Wdv).T], 1), (2, 1)),
        "bd": np.tile(np.concatenate([np.asarray(L0_gnn_bdk), np.asarray(L0_gnn_bdv)])[None], (2, 1)),
        "wo_t": np.asarray(L0_gnn_Wo).T,
        "bo": np.asarray(L0_gnn_bo)[None],
        "wr": L0_ffn_Wr,
        "br": np.asarray(L0_ffn_br)[None],
        "ffn_g": columns(L0_ffn_ln_g),
        "ffn_b": columns(L0_ffn_ln_b),
        "w1": L0_ffn_W1,
        "b1": np.repeat(np.asarray(L0_ffn_b1), 3, 0),
        "w2": L0_ffn_W2,
        "b2": np.repeat(np.asarray(L0_ffn_b2), 3, 0),
        "part_sel": np.array([[0, 1], [1, -1]], np.float32),
        "part_mask": np.tile(np.eye(3, dtype=np.float32), (NE, 1)),
        "pick": np.repeat(np.repeat(np.eye(NE, dtype=np.float32), 3, 0), P, 1),
    }
    arrays = {f"in_{name}": np.ascontiguousarray(v) for name, v in arrays.items()}
    nc = bacc.Bacc("TRN2", target_bir_lowering=False, num_devices=1)
    access = {name[3:]: nc.dram_tensor(name, v.shape, mybir.dt.from_np(v.dtype), kind="ExternalInput").ap()
              for name, v in arrays.items()}
    out = nc.dram_tensor("out_x", (NT * P, D), F32, kind="ExternalOutput").ap()
    build_program(nc, access, out)
    result = run_bass_kernel_spmd(nc, [arrays], core_ids=[0])
    return result.results[0]["out_x"][:N]
```

```python
import math
from contextlib import ExitStack

import concourse.bass as bass
from concourse import mybir

P = 128
N = 6250
E = 100000
D = 256
R = 64
NE = 8
HID = 1024
DC = D // P
KC = HID // P
NT = -(-N // P)
ET = -(-E // P)
EPS = 1e-5
CUT = 5.0

U = 12
PAIRS = U // 2
ITEMS_IT = 2 * U
CH = 120
HALVES_CH = CH // U
GROUPS = PAIRS // 2
HOT_LAG = 3
Q_LAG = 1
SUM_LAG = 3
MAX_CH = -(-(2 * -(-ET // 2) * NT) // CH)
MAX_ITEMS = MAX_CH * CH
MAX_IT = MAX_ITEMS // ITEMS_IT
FULL = ET // P
REST = ET - FULL * P
G256 = 2 * P
SGS = (2 * NT * P + NE * G256) // G256
ZERO_FILLS = -(-2 * (SGS + 2) // 7)
assert NT % 7 == 0

F32 = mybir.dt.float32
I32 = mybir.dt.int32
BF16 = mybir.dt.bfloat16
F32R = mybir.dt.float32r
ALU = mybir.AluOpType
ACT = mybir.ActivationFunctionType
AX = mybir.AxisListType.X


def ds(start, size):
    return bass.ds(start, size)


def over_tiles(eng, count, body):
    for t in range(2):
        body(t, t, 0, False)
    with eng.Fori(1, count // 2) as i:
        for s in range(2):
            body(2 * i + s, s, i, False)
    if count % 2:
        body(count - 1, 0, count // 2, True)


def over_sevens(eng, body):
    for u in range(7):
        body(u, u, 0)
    with eng.Fori(1, NT // 7) as i:
        for u in range(7):
            body(7 * i + u, u, i)


def slot_free(eng, sem, n, per=1):
    if not (isinstance(n, int) and n == 0):
        eng.wait_ge(sem, n * per)


class Chain:

    def __init__(self, eng, sem):
        self.eng, self.sem, self.n = eng, sem, 0

    def __call__(self, ins):
        self.n += 1
        ins.then_inc(self.sem, 1)
        self.eng.wait_ge(self.sem, self.n)


def build_program(nc, a, out):
    ctx = ExitStack()
    with ctx:
        def dram(name, shape, dt=F32):
            return nc.dram_tensor(name, shape, dt, kind="Internal").ap()

        kv_table = dram("kv_table", [NT * P, 2 * D])
        res_table = dram("res_table", [NT * P, D])
        range_rows = dram("range_rows", [2, (FULL + 1) * P])
        meta_cols = dram("meta_cols", [MAX_ITEMS // U, P, 3 * U])
        rel_rows = dram("rel_rows", [MAX_ITEMS, P], BF16)
        item_tab = dram("item_tab", [2, MAX_ITEMS], I32)
        slot_x = dram("slot_x", [(SGS + 2) * G256, D])
        slot_y = dram("slot_y", [SGS * G256, D])

        in_use = []

        def named(name):
            in_use.append(nc.alloc_semaphore(name))
            return in_use[-1]

        def next_phase():
            nc.clear_and_free_semaphores(in_use)
            in_use.clear()
            nc.all_engine_barrier()

        def outer(name, shape, dt=F32):
            return ctx.enter_context(nc.sbuf_tensor(name, shape, dt))

        ident = outer("ident", [P, P])
        iota_free = outer("iota_free", [P, P])
        iota_part = outer("iota_part", [P, 1])
        ones = outer("ones", [P, P])
        n_run = outer("n_run", [P, 2], I32)
        stats = outer("stats", [P, NT, 6])
        ln_s = outer("ln_s", [P, 8, NT])
        slot_i = outer("slot_i", [P, NT, 2], I32)
        w_top = outer("w_top", [P, NT, 2])
        expert_i = outer("expert_i", [1, SGS + 1], I32)
        bounds = outer("bounds", [1, NE + 2], I32)

        agg_room, q_room = ExitStack(), ExitStack()
        agg = agg_room.enter_context(nc.sbuf_tensor("agg", [P, NT * D], F32))[:, :]
        q_hi = q_room.enter_context(nc.sbuf_tensor("q_hi", [P, NT * D], F32R, side="right"))[:, :]
        q_lo = q_room.enter_context(nc.sbuf_tensor("q_lo", [P, NT * D], F32R, side="right"))[:, :]

        mean, var, rstd, rstd2, bias_r, bias_s, tmp_a, tmp_b = (ln_s[:, k, :] for k in range(8))

        def norm_scales(dve, act_sem, chain, sqrt_sem, step):
            def refine(dst, v):
                chain(dve.reciprocal(dst, tmp_b))
                chain(dve.tensor_tensor(tmp_b, dst, dst, ALU.mult))
                chain(dve.tensor_tensor(tmp_b, tmp_b, tmp_a, ALU.mult))
                chain(dve.tensor_scalar(tmp_b, tmp_b, -0.5, 1.5, ALU.mult, ALU.add))
                chain(dve.tensor_tensor(dst, dst, tmp_b, ALU.mult))

            ev, od = stats[:, :, 1], stats[:, :, 4]
            chain(dve.tensor_tensor(mean, ev, od, ALU.add))
            chain(dve.tensor_scalar(mean, mean, 0.5, None, ALU.mult))
            chain(dve.tensor_tensor(tmp_a, ev, od, ALU.subtract))
            chain(dve.tensor_scalar(tmp_a, tmp_a, 0.5, None, ALU.mult))
            chain(dve.tensor_tensor(tmp_a, tmp_a, tmp_a, ALU.mult))
            chain(dve.tensor_tensor(var, stats[:, :, 2], stats[:, :, 5], ALU.add))
            chain(dve.scalar_tensor_tensor(out=var, in0=var, scalar=1.0 / D, in1=tmp_a, op0=ALU.mult, op1=ALU.add))
            dve.tensor_scalar(tmp_a, var, EPS, None, ALU.add).then_inc(sqrt_sem, 1)
            dve.wait_ge(act_sem, step + 1)
            refine(rstd, tmp_a)
            chain(dve.tensor_tensor(tmp_a, rstd, rstd, ALU.mult))
            chain(dve.tensor_tensor(tmp_a, tmp_a, var, ALU.mult))
            dve.tensor_scalar(tmp_a, tmp_a, EPS, None, ALU.add).then_inc(sqrt_sem, 1)
            dve.wait_ge(act_sem, step + 2)
            refine(rstd2, tmp_a)
            chain(dve.tensor_tensor(rstd2, rstd2, rstd, ALU.mult))
            chain(dve.scalar_tensor_tensor(out=bias_r, in0=mean, scalar=-1.0, in1=rstd, op0=ALU.mult, op1=ALU.mult))
            chain(dve.scalar_tensor_tensor(out=bias_s, in0=mean, scalar=-1.0, in1=rstd2, op0=ALU.mult, op1=ALU.mult))

        def norm_roots(act, act_sem, sqrt_sem):
            for k in range(2):
                act.wait_ge(sqrt_sem, k + 1)
                act.activation(tmp_b, tmp_a, ACT.Sqrt).then_inc(act_sem, 1)

        with ExitStack() as s1:
            def sb(name, shape, dt=F32):
                return s1.enter_context(nc.sbuf_tensor(name, shape, dt))

            def ps(name, shape):
                return s1.enter_context(nc.psum_tensor(name, shape, F32))

            def sem(name):
                return named(name)

            xt = agg.rearrange("p (t d) -> p t d", d=D)
            wqkv = sb("wqkv", [P, DC, 3 * D])
            g_col = sb("g_col", [P, DC])
            b_col = sb("b_col", [P, DC])
            b_rep = sb("b_rep", [P, DC, P])
            bias_in = sb("bias_in", [1, 3 * D])
            bias_all = sb("bias_all", [P, 3 * D])
            normed = sb("normed", [P, 2, D])
            wqkv_hi = sb("wqkv_hi", [P, DC, 3 * D], F32R)
            wqkv_lo = sb("wqkv_lo", [P, DC, 3 * D], F32R)
            turned_hi = sb("turned_hi", [P, 2, D], F32R)
            turned_lo = sb("turned_lo", [P, 2, D], F32R)
            kv_out = sb("kv_out", [P, 2, 2 * D])
            q_out = sb("q_out", [P, 2, D])
            tp = ps("tp", [P, 2, 512])
            proj = ps("proj", [P, 2, 1024])

            s_x = [sem(f"s_x{k}") for k in range(7)]
            s_w = sem("s_w")
            s_bin = sem("s_bin")
            s_const = sem("s_const")
            s_chain = sem("s_chain")
            s_stats = sem("s_stats")
            s_var = sem("s_var")
            s_root = sem("s_root")
            s_scales = sem("s_scales")
            s_fold = sem("s_fold")
            s_bias_mm = sem("s_bias_mm")
            s_bias = sem("s_bias")
            normed_made = [sem(f"normed_made{k}") for k in range(2)]
            res_made = sem("res_made")
            transposed = [sem(f"transposed{k}") for k in range(2)]
            rounded = [sem(f"rounded{k}") for k in range(2)]
            copied = [sem(f"copied{k}") for k in range(2)]
            projected = [sem(f"projected{k}") for k in range(2)]
            evacuated = [sem(f"evacuated{k}") for k in range(2)]
            kv_stored = [sem(f"kv_stored{k}") for k in range(2)]
            q_rounded = [sem(f"q_rounded{k}") for k in range(2)]
            q_split = [sem(f"q_split{k}") for k in range(2)]
            gate_q = sem("gate_q")
            gate = sem("gate1")
            s_res = sem("s_res")
            block = s1.enter_context(nc.Block())

            G = NT // 7
            x_rows = a["x"].rearrange("(t p) d -> p t d", p=P)

            @block.sync
            def _(sp):
                for k in range(7):
                    sp.dma_start(xt[:, k * G:(k + 1) * G, :], x_rows[:, k * G:(k + 1) * G, :]).then_inc(s_x[k], 16)
                sp.dma_start(wqkv[:, :, :], a["wqkv_t"].rearrange("(c p) n -> p c n", p=P)).then_inc(s_w, 16)
                sp.dma_start(g_col[:, :], a["gnn_g"]).then_inc(s_w, 16)
                sp.dma_start(b_col[:, :], a["gnn_b"]).then_inc(s_w, 16)
                sp.dma_start(bias_in[:, :], a["bqkv"]).then_inc(s_bin, 16)

                def store(t, s, n, last):
                    sp.wait_ge(evacuated[s], 2 * (n + 1))
                    sp.dma_start(kv_table[ds(t * P, P), :], kv_out[:, s, :]).then_inc(kv_stored[s], 16)

                over_tiles(sp, NT, store)
                sp.wait_ge(kv_stored[0], 16 * (NT // 2 + 1))
                sp.wait_ge(kv_stored[1], 16 * (NT // 2))

            @block.gpsimd
            def _(pool):
                c = Chain(pool, s_const)
                c(pool.memset(ones[:, :], 1.0))
                c(pool.affine_select(out=ident[:, :], in_=ones[:, :], compare_op=ALU.is_equal, fill=0.0, base=0,
                                     pattern=[[-1, P]], channel_multiplier=1))
                c(pool.iota(iota_free[:, :], pattern=[[1, P]], base=0, channel_multiplier=0,
                            allow_small_or_imprecise_dtypes=True))
                c(pool.iota(iota_part[:, :], pattern=[[0, 1]], base=0, channel_multiplier=1,
                            allow_small_or_imprecise_dtypes=True))

                def split_q(t, s, n, last):
                    pool.wait_ge(evacuated[s], 2 * n + 2)
                    pool.sem_inc(gate_q, 1)
                    pool.tensor_copy(q_hi[:, ds(t * D, D)], q_out[:, s, :]).then_inc(q_rounded[s], 1)
                    pool.wait_ge(q_rounded[s], n + 1)
                    pool.sem_inc(gate_q, 1)
                    pool.tensor_tensor(q_lo[:, ds(t * D, D)], q_out[:, s, :], q_hi[:, ds(t * D, D)].bitcast(F32),
                                       ALU.subtract) \
                        .then_inc(q_split[s], 1)

                over_tiles(pool, NT, split_q)

            @block.scalar
            def _(act):
                norm_roots(act, s_root, s_var)
                act.wait_ge(s_scales, 1)

                def normalise(t, s, n, last):
                    slot_free(act, transposed[s], n)
                    act.sem_inc(gate, 1)
                    act.activation(normed[:, s, :], agg[:, ds(t * D, D)], ACT.Identity, scale=rstd2[:, ds(t, 1)],
                                   bias=bias_s[:, ds(t, 1)]).then_inc(normed_made[s], 1)
                    act.activation(agg[:, ds(t * D, D)], agg[:, ds(t * D, D)], ACT.Identity,
                                   scale=tmp_a[:, ds(t, 1)], bias=bias_r[:, ds(t, 1)]).then_inc(res_made, 1)

                def round_turned(s, n):
                    slot_free(act, projected[s], n)
                    act.sem_inc(gate, 1)
                    act.wait_ge(transposed[s], n + 1)
                    act.sem_inc(gate, 1)
                    act.activation(turned_hi[:, s, :], tp[:, s, 0:D], ACT.Copy).then_inc(rounded[s], 1)

                def step(t, s, n, last):
                    if not (isinstance(t, int) and t == 0):
                        round_turned(1 - s, n - 1 + s)
                    normalise(t, s, n, last)
                    if not (isinstance(t, int) and t == 0):
                        store_res(t - 1)

                def store_res(t):
                    act.wait_ge(res_made, t + 1)
                    act.sem_inc(gate, 1)
                    act.dma_start(res_table[ds(t * P, P), :], agg[:, ds(t * D, D)]).then_inc(s_res, 16)

                over_tiles(act, NT, step)
                round_turned((NT - 1) % 2, (NT - 1) // 2)
                store_res(NT - 1)
                act.wait_ge(s_res, 16 * NT)

            @block.vector
            def _(dve):
                c = Chain(dve, s_chain)
                for k in range(7):
                    dve.wait_ge(s_x[k], 16)
                    with dve.Fori(k * G, (k + 1) * G) as t:
                        dve.bn_stats(stats[:, ds(t, 1), :].rearrange("p a b -> p (a b)"), agg[:, ds(t * D, D)]) \
                            .then_inc(s_stats, 1)
                dve.wait_ge(s_stats, NT)
                norm_scales(dve, s_root, c, s_var, 0)
                dve.tensor_scalar(tmp_a, rstd, 1.0, None, ALU.add).then_inc(s_scales, 1)
                dve.wait_ge(s_w, 48)
                dve.wait_ge(s_const, 4)
                for k in range(DC):
                    dve.tensor_scalar(b_rep[:, k, :], ones[:, :], b_col[:, k:k + 1], None, ALU.mult).then_inc(s_fold, 1)
                dve.wait_ge(s_bias_mm, 1)
                for k in range(DC):
                    dve.tensor_scalar(wqkv_hi[:, k, :], wqkv[:, k, :], g_col[:, k:k + 1], None, ALU.mult) \
                        .then_inc(s_fold, 1)
                dve.wait_ge(s_fold, 2 * DC)
                for k in range(DC):
                    dve.scalar_tensor_tensor(out=wqkv_lo[:, k, :], in0=wqkv[:, k, :], scalar=g_col[:, k:k + 1],
                                             in1=wqkv_hi[:, k, :].bitcast(F32), op0=ALU.mult, op1=ALU.subtract) \
                        .then_inc(s_fold, 1)
                dve.tensor_copy(bias_all[:, :], proj[:, 0, 0:3 * D]).then_inc(s_bias, 1)
                dve.wait_ge(s_bias, 1)

                def copy(s, n):
                    slot_free(dve, projected[s], n)
                    dve.wait_ge(rounded[s], n + 1)
                    dve.tensor_tensor(turned_lo[:, s, :], tp[:, s, 0:D], turned_hi[:, s, :].bitcast(F32),
                                      ALU.subtract).then_inc(copied[s], 1)

                def evacuate(t, s, n, last):
                    if not last:
                        copy(1 - s, n + s)
                    slot_free(dve, kv_stored[s], n, 16)
                    dve.wait_ge(projected[s], n + 1)
                    dve.tensor_tensor(kv_out[:, s, :], proj[:, s, 0:2 * D], bias_all[:, 0:2 * D], ALU.add) \
                        .then_inc(evacuated[s], 1)
                    slot_free(dve, q_split[s], n)
                    dve.tensor_tensor(q_out[:, s, :], proj[:, s, 2 * D:3 * D], bias_all[:, 2 * D:3 * D],
                                      ALU.add).then_inc(evacuated[s], 1)

                copy(0, 0)
                over_tiles(dve, NT, evacuate)

            @block.tensor
            def _(pe):
                pe.wait_ge(s_fold, DC)
                pe.wait_ge(s_w, 48)
                pe.wait_ge(s_bin, 16)
                for lo, hi in ((0, 512), (512, 3 * D)):
                    for k in range(DC):
                        pe.matmul(proj[:, 0, lo:hi], b_rep[:, k, :], wqkv[:, k, lo:hi], start=(k == 0), stop=False)
                    mm = pe.matmul(proj[:, 0, lo:hi], ones[0:1, :], bias_in[:, lo:hi], start=False, stop=True)
                mm.then_inc(s_bias_mm, 1)
                pe.wait_ge(s_fold, 3 * DC)
                pe.wait_ge(s_bias, 1)

                def transposes(s, n):
                    slot_free(pe, copied[s], n)
                    pe.wait_ge(normed_made[s], n + 1)
                    for k in range(DC):
                        mm = pe.transpose(tp[:, s, k * P:(k + 1) * P], normed[:, s, k * P:(k + 1) * P], ident[:, :])
                    mm.then_inc(transposed[s], 1)

                def products(t, s, n, last):
                    if not last:
                        transposes(1 - s, n + s)
                    slot_free(pe, evacuated[s], n, 2)
                    pe.wait_ge(copied[s], n + 1)
                    parts = [(x, w, k) for k in range(DC) for x, w in ((turned_hi, wqkv_hi), (turned_hi, wqkv_lo),
                                                                       (turned_lo, wqkv_hi))]
                    for lo, hi in ((0, 512), (512, 3 * D)):
                        for i, (x, w, k) in enumerate(parts):
                            mm = pe.matmul(proj[:, s, lo:hi], x[:, s, k * P:(k + 1) * P], w[:, k, lo:hi],
                                           start=(i == 0), stop=(i == len(parts) - 1))
                    mm.then_inc(projected[s], 1)

                transposes(0, 0)
                over_tiles(pe, NT, products)

        next_phase()

        with ExitStack() as s2:
            def sb(name, shape, dt=F32):
                return s2.enter_context(nc.sbuf_tensor(name, shape, dt))

            def sem(name):
                return named(name)

            dst_rows = sb("dst_rows", [P, FULL + 1, P], I32)
            least = sb("least", [P, 2, FULL + 1])
            block_i = sb("block_i", [P, 2, FULL + 1], I32)
            block_f = sb("block_f", [P, 2, FULL + 1])
            ranges = sb("ranges", [P, 2, ET])
            meets = sb("meets", [P, ET])
            pairs_i = sb("pairs_i", [P, 1], I32)
            of_block = sb("of_block", [P, 3])
            spread = sb("spread", [P, 3, P])
            by_block = sb("by_block", [P, 3, P])
            upto = sb("upto", [P, NT])
            count = sb("count", [P, 1])
            offset = sb("offset", [P, NT])
            iota_row = sb("iota_row", [P, MAX_IT])
            junk = sb("junk", [P, MAX_IT])
            n_f = sb("n_f", [P, 2])
            j_col = sb("j_col", [P, 1])
            blk_col = sb("blk_col", [P, 1])
            tile_col = sb("tile_col", [P, 1])
            last_col = sb("last_col", [P, 1])
            void_col = sb("void_col", [P, 1])
            base_col = sb("base_col", [P, 1])
            tab_i = sb("tab_i", [P, 2], I32)
            src_g = sb("src_g", [P, P], I32)
            dst_g = sb("dst_g", [P, P], I32)
            ew_g = sb("ew_g", [P, P])
            ew_turn = sb("ew_turn", [P, P])
            ew_whole = sb("ew_whole", [P, P], I32)
            half_pi = sb("half_pi", [P, 1])
            metas = sb("metas", [P, 3, P])
            rel_b = sb("rel_b", [P, P], BF16)
            meta_out = sb("meta_out", [P, HALVES_CH, 3, U])
            meta_ps = s2.enter_context(nc.psum_tensor("meta_ps", [P, 3, 512], F32))

            s_dst = sem("s_dst")
            s_c2 = sem("s_c2")
            s_pc2 = sem("s_pc2")
            s_blocks = sem("s_blocks")
            s_rng_st = sem("s_rng_st")
            s_rng = sem("s_rng")
            s_iota = sem("s_iota")
            s_spread = sem("s_spread")
            s_by_block = sem("s_by_block")
            s_count = sem("s_count")
            s_link = sem("s_link")
            tiles_known = sem("tiles_known")
            gathered = sem("gathered")
            turn_ready = sem("turn_ready")
            sin_made = sem("sin_made")
            metas_made = sem("metas_made")
            metas_turned = sem("metas_turned")
            meta_copied = sem("meta_copied")
            chunk_stored = sem("chunk_stored")
            chunk_free = sem("chunk_free")
            gate_p = sem("gate_p2")
            gate_a = sem("gate_a2")
            block = s2.enter_context(nc.Block())

            @block.sync
            def _(sp):
                sp.sem_inc(chunk_free, 1)
                sp.dma_start(dst_rows[:, 0:FULL, :],
                             a["dst"][0:FULL * P, :].rearrange("(c p) e -> p c e", p=P)).then_inc(s_dst, 16)
                sp.dma_start(dst_rows[0:REST, FULL, :], a["dst"][FULL * P:ET, :]).then_inc(s_dst, 16)
                sp.wait_ge(s_blocks, 1)
                for k in range(2):
                    with nc.allow_non_contiguous_dma(reason="a column of seven numbers a partition"):
                        sp.dma_start(range_rows[k].rearrange("(c p) -> p c", p=P), block_f[:, k, :]) \
                            .then_inc(s_rng_st, 16)
                sp.wait_ge(s_rng_st, 32)
                sp.dma_start(ranges[:, :, :], range_rows[:, 0:ET].unsqueeze(0).to_broadcast([P, 2, ET])) \
                    .then_inc(s_rng, 16)
                sp.wait_ge(s_count, 1)
                chunks = sp.value_load(n_run[0:1, 1:2], min_val=1, max_val=MAX_CH)
                with sp.Fori(0, chunks) as c:
                    sp.wait_ge(meta_copied, c + 1)
                    sp.dma_start(meta_cols[ds(c * HALVES_CH, HALVES_CH)].rearrange("h p m -> p h m"),
                                 meta_out[:, :, :, :].rearrange("p h k u -> p h (k u)")).then_inc(chunk_stored, 16)
                    sp.dma_start(rel_rows[ds(c * CH, CH), :], rel_b[0:CH, :]).then_inc(chunk_stored, 16)
                    with nc.allow_non_contiguous_dma(reason="one number a partition"):
                        for k in range(2):
                            sp.dma_start(item_tab[k, ds(c * CH, CH)].unsqueeze(1), tab_i[0:CH, k:k + 1]) \
                                .then_inc(chunk_stored, 16)
                    sp.wait_ge(chunk_stored, 64 * c + 64)
                    sp.sem_inc(chunk_free, 1)

            @block.gpsimd
            def _(pool):
                c = Chain(pool, s_pc2)
                pool.iota(iota_row[:, :], pattern=[[1, MAX_IT]], base=0, channel_multiplier=0,
                          allow_small_or_imprecise_dtypes=True).then_inc(s_iota, 1)
                pool.iota(j_col[:, :], pattern=[[0, 1]], base=-CH, channel_multiplier=1,
                          allow_small_or_imprecise_dtypes=True).then_inc(s_iota, 1)
                c(pool.memset(agg, 0.0))
                pool.wait_ge(s_count, 1)
                chunks = pool.value_load(n_run[0:1, 1:2], min_val=1, max_val=MAX_CH)
                with pool.Fori(0, chunks) as k:
                    pool.wait_ge(tiles_known, k + 1)
                    pool.sem_inc(gate_p, 1)
                    for row, name in ((src_g, "src"), (dst_g, "dst"), (ew_g, "edge_weight")):
                        pool.indirect_dma_start(row[0:CH, :], None, a[name],
                                                bass.IndirectOffsetOnAxis(ap=tab_i[0:CH, 0:1], axis=0)) \
                            .then_inc(gathered, 16)

            @block.vector
            def _(dve):
                c = Chain(dve, s_c2)
                c(dve.memset(least[:, :, :], 0.0))
                dve.memset(half_pi[:, :], math.pi / 2).then_inc(s_c2, 1)
                c.n += 1
                dve.wait_ge(s_dst, 32)
                for k, op in ((0, ALU.min), (1, ALU.max)):
                    c(dve.tensor_reduce(least[:, k, 0:FULL], dst_rows[:, 0:FULL, :], AX, op))
                    c(dve.tensor_reduce(least[0:REST, k, FULL:FULL + 1], dst_rows[0:REST, FULL, :], AX, op))
                c(dve.tensor_copy(block_i[:, :, :], least[:, :, :]))
                c(dve.tensor_scalar(block_i[:, :, :], block_i[:, :, :], 7, None, ALU.arith_shift_right))
                c(dve.tensor_copy(block_f[:, :, :], block_i[:, :, :]))
                dve.sem_inc(s_blocks, 1)
                dve.wait_ge(s_rng, 16)
                dve.wait_ge(s_iota, 2)
                c(dve.tensor_scalar(meets[:, :], ranges[:, 0, :], iota_part[:, 0:1], None, ALU.is_le))
                c(dve.scalar_tensor_tensor(out=meets[:, :], in0=ranges[:, 1, :], scalar=iota_part[:, 0:1],
                                           in1=meets[:, :], op0=ALU.is_ge, op1=ALU.mult))
                c(dve.scalar_tensor_tensor(out=junk[:, 0:ET], in0=iota_row[:, 0:ET], scalar=1.0, in1=meets[:, :],
                                           op0=ALU.add, op1=ALU.mult))
                c(dve.tensor_reduce(of_block[:, 2:3], junk[:, 0:ET], AX, ALU.max))
                c(dve.scalar_tensor_tensor(out=junk[:, 0:ET], in0=iota_row[:, 0:ET], scalar=-float(ET),
                                           in1=meets[:, :], op0=ALU.add, op1=ALU.mult))
                c(dve.tensor_reduce(of_block[:, 1:2], junk[:, 0:ET], AX, ALU.min))
                c(dve.tensor_scalar(of_block[:, 1:2], of_block[:, 1:2], float(ET), None, ALU.add))
                c(dve.tensor_tensor(of_block[:, 0:1], of_block[:, 2:3], of_block[:, 1:2], ALU.subtract))
                c(dve.tensor_scalar(pairs_i[:, :], of_block[:, 0:1], 0.0, 1.0, ALU.max, ALU.add))
                c(dve.tensor_scalar(pairs_i[:, :], pairs_i[:, :], 1, None, ALU.arith_shift_right))
                c(dve.tensor_scalar(of_block[:, 0:1], pairs_i[:, :], 2.0, None, ALU.mult))
                c(dve.tensor_scalar(of_block[:, 2:3], of_block[:, 2:3], -1.0, None, ALU.add))
                for m in range(3):
                    c(dve.tensor_scalar(spread[:, m, :], ident[:, :], of_block[:, m:m + 1], None, ALU.mult))
                dve.sem_inc(s_spread, 1)
                dve.wait_ge(s_by_block, 1)
                c(dve.tensor_copy(by_block[:, :, :].rearrange("p m b -> p (m b)"), meta_ps[:, 0, 0:3 * P]))
                c(dve.tensor_tensor_scan(upto[:, :], ones[:, 0:NT], by_block[:, 0, 0:NT], 0.0, ALU.mult, ALU.add))
                c(dve.tensor_tensor(offset[:, :], by_block[:, 1, 0:NT], upto[:, :], ALU.subtract))
                c(dve.tensor_tensor(offset[:, :], offset[:, :], by_block[:, 0, 0:NT], ALU.add))
                for k, n, per, most in ((0, upto[:, NT - 1:NT], ITEMS_IT, MAX_IT),
                                        (1, n_f[:, 0:1], CH // ITEMS_IT, MAX_CH)):
                    c(dve.tensor_scalar(count[:, 0:1], n, 1.0 / per, None, ALU.mult))
                    c(dve.tensor_scalar(junk[:, 0:most], iota_row[:, 0:most], count[:, 0:1], None, ALU.is_lt,
                                        ALU.add, accum_out=n_f[:, k:k + 1]))
                c(dve.tensor_scalar(n_f[:, 0:1], n_f[:, 0:1], -1.0, None, ALU.add))
                c(dve.tensor_copy(n_run[:, :], n_f[:, :]))
                dve.sem_inc(s_count, 1)
                chunks = dve.value_load(n_run[0:1, 1:2], min_val=1, max_val=MAX_CH)
                LINKS = 18
                with dve.Fori(0, chunks) as k:
                    done = 0

                    def link(ins):
                        nonlocal done
                        done += 1
                        ins.then_inc(s_link, 1)
                        dve.wait_ge(s_link, k * LINKS + done)

                    link(dve.tensor_scalar(j_col[:, :], j_col[:, :], float(CH), None, ALU.add))
                    link(dve.tensor_scalar(junk[:, 0:NT - 1], upto[:, 0:NT - 1], j_col[:, 0:1], None, ALU.is_le,
                                           ALU.add, accum_out=blk_col[:, :]))
                    link(dve.scalar_tensor_tensor(out=junk[:, 0:NT], in0=iota_row[:, 0:NT], scalar=blk_col[:, 0:1],
                                                  in1=offset[:, :], op0=ALU.is_equal, op1=ALU.mult,
                                                  accum_out=tile_col[:, :]))
                    link(dve.scalar_tensor_tensor(out=junk[:, 0:NT], in0=iota_row[:, 0:NT], scalar=blk_col[:, 0:1],
                                                  in1=by_block[:, 2, 0:NT], op0=ALU.is_equal, op1=ALU.mult,
                                                  accum_out=last_col[:, :]))
                    link(dve.tensor_tensor(tile_col[:, :], tile_col[:, :], j_col[:, :], ALU.add))
                    link(dve.tensor_tensor(void_col[:, :], tile_col[:, :], last_col[:, :], ALU.is_gt))
                    link(dve.tensor_tensor(tile_col[:, :], tile_col[:, :], last_col[:, :], ALU.min))
                    link(dve.tensor_scalar(tile_col[:, :], tile_col[:, :], 0.0, None, ALU.max))
                    dve.wait_ge(chunk_free, k + 1)
                    dve.tensor_copy(tab_i[:, 0:1], tile_col[:, :]).then_inc(tiles_known, 1)
                    link(dve.tensor_scalar(void_col[:, :], void_col[:, :], -float(1 << 20), None, ALU.mult))
                    link(dve.scalar_tensor_tensor(out=base_col[:, :], in0=blk_col[:, :], scalar=float(P),
                                                  in1=void_col[:, :], op0=ALU.mult, op1=ALU.add))
                    link(dve.tensor_copy(tab_i[:, 1:2], blk_col[:, :]))
                    dve.wait_ge(gathered, 48 * k + 48)
                    link(dve.tensor_scalar(ew_turn[0:CH, :], ew_g[0:CH, :], 0.5 / CUT, None, ALU.mult))
                    link(dve.tensor_copy(ew_whole[0:CH, :], ew_turn[0:CH, :]))
                    link(dve.tensor_tensor(ew_turn[0:CH, :], ew_turn[0:CH, :], ew_whole[0:CH, :], ALU.subtract))
                    dve.scalar_tensor_tensor(out=ew_turn[0:CH, :], in0=ew_turn[0:CH, :], scalar=-1.0,
                                             in1=ew_turn[0:CH, :], op0=ALU.mult, op1=ALU.max).then_inc(turn_ready, 1)
                    dve.tensor_copy(metas[0:CH, 0, :], src_g[0:CH, :]).then_inc(metas_made, 1)
                    link(dve.tensor_scalar(metas[0:CH, 1, :], dst_g[0:CH, :], base_col[0:CH, 0:1], -1.0,
                                           ALU.subtract, ALU.max))
                    link(dve.tensor_scalar(metas[0:CH, 1, :], metas[0:CH, 1, :], float(P), None, ALU.min))
                    dve.tensor_copy(rel_b[0:CH, :], metas[0:CH, 1, :]).then_inc(metas_made, 1)
                    dve.wait_ge(sin_made, k + 1)
                    link(dve.tensor_scalar(ew_turn[0:CH, :], ew_turn[0:CH, :], 0.5, 0.5, ALU.mult, ALU.add))
                    link(dve.scalar_tensor_tensor(out=metas[0:CH, 2, :], in0=ew_g[0:CH, :], scalar=CUT,
                                                  in1=ew_turn[0:CH, :], op0=ALU.is_lt, op1=ALU.mult))
                    dve.sem_inc(metas_made, 1)
                    assert done == LINKS
                    dve.wait_ge(metas_turned, k + 1)
                    for m in range(3):
                        ins = dve.tensor_copy(meta_out[:, :, m, :],
                                              meta_ps[:, m, 0:CH].rearrange("p (h u) -> p h u", u=U))
                    ins.then_inc(meta_copied, 1)

            @block.scalar
            def _(act):
                act.wait_ge(s_count, 1)
                chunks = act.value_load(n_run[0:1, 1:2], min_val=1, max_val=MAX_CH)
                with act.Fori(0, chunks) as k:
                    act.wait_ge(turn_ready, k + 1)
                    act.sem_inc(gate_a, 1)
                    act.activation(ew_turn[0:CH, :], ew_turn[0:CH, :], ACT.Sin, scale=-2.0 * math.pi,
                                   bias=half_pi[0:CH, 0:1]).then_inc(sin_made, 1)

            @block.tensor
            def _(pe):
                pe.wait_ge(s_spread, 1)
                pe.matmul(meta_ps[:, 0, 0:3 * P], ones[:, :], spread[:, :, :].rearrange("p m b -> p (m b)"),
                          start=True, stop=True).then_inc(s_by_block, 1)
                pe.wait_ge(s_count, 1)
                chunks = pe.value_load(n_run[0:1, 1:2], min_val=1, max_val=MAX_CH)
                with pe.Fori(0, chunks) as k:
                    pe.wait_ge(metas_made, 3 * k + 3)
                    for m in range(3):
                        mm = pe.transpose(meta_ps[:, m, 0:CH], metas[0:CH, m, :], ident[0:CH, 0:CH])
                    mm.then_inc(metas_turned, 1)

        next_phase()

        with ExitStack() as s3:
            def sb(name, shape, dt=F32):
                return s3.enter_context(nc.sbuf_tensor(name, shape, dt))

            def ps(name, shape):
                return s3.enter_context(nc.psum_tensor(name, shape, F32))

            def sem(name):
                return named(name)

            kv_in = sb("kv_in", [P, U, 2 * D])
            w_in = kv_in[:, 0, :]
            b_in = kv_in[0:2, 1, :]
            b_hi = kv_in[0:2, 2, :]
            w_hi = sb("w_hi", [P, 2 * D], F32R)
            w_lo = sb("w_lo", [P, 2 * D], F32R)
            b_parts = sb("b_parts", [2, 2 * D], F32R)
            part_sel = sb("part_sel", [2, 2])
            ones_r = sb("ones_r", [2, P], F32R)
            ea_in = sb("ea_in", [P, U, P])
            ea_parts = sb("ea_parts", [P, U, P], F32R)
            src_in = sb("src_in", [P, 2, U])
            meta_in = sb("meta_in", [P, 2, 2, U])
            rel_in = sb("rel_in", [P, GROUPS, 4 * P], BF16)
            tiles_in = sb("tiles_in", [1, 2, U], I32)
            blocks_in = sb("blocks_in", [1, 2, U], I32)
            src_i = sb("src_i", [P, 2, U], I32)
            distance = stats[:, :, :].rearrange("p t s -> p (t s)").bitcast(BF16)[:, 0:4 * P]
            onehot_t = sb("onehot_t", [P, GROUPS, 4 * P], F32R)
            onehot = sb("onehot", [P, 3, 2, P])
            logit = sb("logit", [P, 3, 2])
            gated = sb("gated", [P, 3, 2])
            factor = sb("factor", [P, 3, 2])
            neg_part = sb("neg_part", [P, 1])
            dkv = ps("dkv", [P, 3, 2, 2 * D])
            q_ps = ps("q_ps", [P, 2, D])
            agg_ps = ps("agg_ps", [P, 512])

            s_wd = sem("s_wd")
            s_w_hi = sem("s_w_hi")
            s_w_parts = sem("s_w_parts")
            s_npart = sem("s_npart")
            kv_landed = [sem(f"kv_landed{u}") for u in range(U)]
            ea_landed = [sem(f"ea_landed{p}") for p in range(PAIRS)]
            meta_landed = [sem(f"meta_landed{h}") for h in range(2)]
            rel_landed = [sem(f"rel_landed{g}") for g in range(GROUPS)]
            tiles_landed = [sem(f"tiles_landed{h}") for h in range(2)]
            blocks_landed = [sem(f"blocks_landed{h}") for h in range(2)]
            src_landed = [sem(f"src_landed{h}") for h in range(2)]
            src_ready = sem("src_ready")
            gate_pool = sem("gate_pool3")
            gate_act = sem("gate_act3")
            gate_sp = sem("gate_sp3")
            gate_pe = sem("gate_pe3")
            gate_dve = sem("gate_dve3")

            def each(name):
                return [sem(f"{name}{p}") for p in range(3)]

            ea_rounded = each("ea_rounded")
            ea_split = each("ea_split")
            turned = each("turned")
            onehot_t_made = each("onehot_t_made")
            dkv_made = each("dkv_made")
            dkv_silu = each("dkv_silu")
            q_made = each("q_made")
            kv_made = each("kv_made")
            onehot_made = each("onehot_made")
            logit_made = each("logit_made")
            logit_silu = each("logit_silu")
            factor_made = each("factor_made")
            sum_made = each("sum_made")
            added = each("added")
            block = s3.enter_context(nc.Block())

            def before(h, half, p, lag):
                return (h, half, p - lag) if p >= lag else (1 - h, half - 1, p - lag + PAIRS)

            def landed(h, half):
                return 16 if isinstance(half, int) else 8 * (half - h) + 16

            def exists(half):
                return not (isinstance(half, int) and half < 0)

            def done(eng, sems, at):
                h, half, p = at
                if exists(half):
                    eng.wait_ge(sems[p % 3], 2 * half + p // 3 + 1)

            def group_done(eng, sems, half, g):
                if exists(half):
                    eng.wait_ge(sems[g], half + 1)

            def half_steps(eng, body, drain=None):
                for h in range(2):
                    body(h, h)
                more = eng.value_load(n_run[0:1, 0:1], min_val=1, max_val=MAX_IT - 1)
                with eng.Fori(1, more + 1) as i:
                    for h in range(2):
                        body(h, 2 * i + h)
                if drain:
                    drain(0, 2 * more + 2)

            @block.sync
            def _(sp):
                sp.dma_start(w_in, a["wd_t"]).then_inc(s_wd, 16)
                sp.dma_start(b_in, a["bd"]).then_inc(s_wd, 16)
                sp.dma_start(part_sel[:, :], a["part_sel"]).then_inc(s_wd, 16)

                def half_step(h, half):
                    with nc.allow_non_contiguous_dma(reason="twelve numbers a partition"):
                        sp.dma_start(tiles_in[:, h, :], item_tab[0, ds(half * U, U)].unsqueeze(0)) \
                            .then_inc(tiles_landed[h], 16)
                        if not isinstance(half, int):
                            sp.wait_ge(src_ready, half - 1)
                        sp.dma_start(src_in[:, h, :], meta_cols[ds(half, 1), :, 0:U].rearrange("a p m -> (a p) m")) \
                            .then_inc(src_landed[h], 16)
                    sp.wait_ge(tiles_landed[h], landed(h, half))
                    sp.sem_inc(gate_sp, 1)
                    for p in range(PAIRS):
                        if p % 2 == 0:
                            group_done(sp, turned, half - 1, p // 2)
                            sp.dma_start(rel_in[:, p // 2, :],
                                         rel_rows[ds(half * U + 2 * p, 4), :].rearrange("u e -> (u e)")
                                         .unsqueeze(0).to_broadcast([P, 4 * P])).then_inc(rel_landed[p // 2], 16)
                        t = sp.value_load(tiles_in[0:1, h, 2 * p:2 * p + 1], min_val=0, max_val=ET - 1)
                        group_done(sp, ea_split, half - 1, p // 2)
                        sp.dma_start(ea_in[:, 2 * p:2 * p + 2, :], a["edge_attr_t"][ds(t, 2)]
                                     .rearrange("a r e -> r a e")).then_inc(ea_landed[p], 16)
                    done(sp, added, (h, half - 2, PAIRS - 1))
                    with nc.allow_non_contiguous_dma(reason="twelve numbers"):
                        sp.dma_start(blocks_in[:, h, :], item_tab[1, ds(half * U, U)].unsqueeze(0)) \
                            .then_inc(blocks_landed[h], 16)
                    sp.dma_start(meta_in[:, h, :, :].rearrange("p k u -> p (k u)"),
                                 meta_cols[ds(half, 1), :, U:3 * U].rearrange("a p m -> (a p) m")) \
                        .then_inc(meta_landed[h], 16)

                half_steps(sp, half_step)

            @block.gpsimd
            def _(pool):
                pool.wait_ge(s_w_parts, 4)
                pool.sem_inc(gate_pool, 1)
                pool.tensor_scalar(neg_part[:, :], iota_part[:, :], -1.0, None, ALU.mult).then_inc(s_npart, 1)

                def rest_of_edges(half, g):
                    group_done(pool, ea_rounded, half, g)
                    pool.sem_inc(gate_pool, 1)
                    lo = ea_parts[0:R, 4 * g:4 * g + 4, :]
                    pool.tensor_tensor(lo, ea_in[0:R, 4 * g:4 * g + 4, :], lo.bitcast(F32), ALU.subtract) \
                        .then_inc(ea_split[g], 1)

                def half_step(h, half):
                    pool.wait_ge(src_landed[h], landed(h, half))
                    pool.sem_inc(gate_pool, 1)
                    pool.tensor_copy(src_i[:, h, :], src_in[:, h, :]).then_inc(src_ready, 1)
                    pool.wait_ge(src_ready, half + 1)
                    pool.sem_inc(gate_pool, 1)
                    for p in range(PAIRS):
                        done(pool, sum_made, (1 - h, half - 1, p))
                        pool.sem_inc(gate_pool, 1)
                        for u in (2 * p, 2 * p + 1):
                            pool.indirect_dma_start(kv_in[:, u, :], None, kv_table,
                                                    bass.IndirectOffsetOnAxis(ap=src_i[:, h, u:u + 1], axis=0)) \
                                .then_inc(kv_landed[u], 16)
                        if p % 2 == 0:
                            rest_of_edges(half, p // 2)

                half_steps(pool, half_step)

            @block.scalar
            def _(act):
                act.wait_ge(s_wd, 48)
                act.activation(w_hi[:, :], w_in, ACT.Copy).then_inc(s_w_hi, 1)
                act.activation(b_hi.bitcast(F32R), b_in, ACT.Copy).then_inc(s_w_hi, 1)
                act.wait_ge(s_npart, 1)

                def round_edges(half, g):
                    for p in (2 * g, 2 * g + 1):
                        act.wait_ge(ea_landed[p], 16 * half + 16)
                        act.sem_inc(gate_act, 1)
                    done(act, dkv_made, (None, half - 1, 2 * g + 1))
                    act.sem_inc(gate_act, 1)
                    act.activation(ea_parts[:, 4 * g:4 * g + 4, :], ea_in[:, 4 * g:4 * g + 4, :], ACT.Copy) \
                        .then_inc(ea_rounded[g], 1)

                def one_hots_t(half, g):
                    act.wait_ge(rel_landed[g], 16 * half + 16)
                    act.sem_inc(gate_act, 1)
                    group_done(act, onehot_t_made, *((half - 1, GROUPS - 1) if g == 0 else (half, g - 1)))
                    act.sem_inc(gate_act, 1)
                    act.activation(distance, rel_in[:, g, :], ACT.Abs, bias=neg_part[:, 0:1]).then_inc(turned[g], 1)
                    done(act, q_made, (None, half - 1, 2 * g + 1))
                    act.sem_inc(gate_act, 1)
                    group_done(act, turned, half, g)
                    act.sem_inc(gate_act, 1)
                    act.activation(onehot_t[:, g, :], distance, ACT.Relu, bias=1.0,
                                   scale=-1.0).then_inc(onehot_t_made[g], 1)

                def silu(at):
                    h, half, p = at
                    if exists(half):
                        done(act, dkv_made, at)
                        act.sem_inc(gate_act, 1)
                        act.activation(dkv[:, p % 3, :, :], dkv[:, p % 3, :, :], ACT.Silu).then_inc(dkv_silu[p % 3], 1)

                def attention(at):
                    h, half, p = at
                    if exists(half):
                        done(act, logit_made, at)
                        act.sem_inc(gate_act, 1)
                        act.activation(gated[:, p % 3, :], logit[:, p % 3, :], ACT.Silu).then_inc(logit_silu[p % 3], 1)

                def half_step(h, half):
                    for p in range(PAIRS):
                        if p % 2 == 0:
                            round_edges(half, p // 2)
                        else:
                            one_hots_t(half, p // 2)
                        silu(before(h, half, p, 2))
                        attention(before(h, half, p, 3))

                def drain(h, half):
                    for lag in (2, 1, 0):
                        if lag:
                            silu(before(h, half, 0, lag))
                        attention(before(h, half, 0, lag + 1))

                half_steps(act, half_step, drain)

            @block.tensor
            def _(pe):
                pe.wait_ge(s_w_parts, 4)

                def products(h, half, p):
                    group_done(pe, ea_split, half, p // 2)
                    done(pe, kv_made, before(h, half, p, 3))
                    for k in range(2):
                        o = dkv[:, p % 3, k, :]
                        pe.matmul(o, ea_parts[:, 2 * p + k, :], w_hi[:, :], start=True, stop=False)
                        pe.matmul(o, ea_parts[:, 2 * p + k, :], w_lo[:, :], start=False, stop=False)
                        mm = pe.matmul(o, ones_r[:, :], b_parts[:, :], start=False, stop=True)
                    mm.then_inc(dkv_made[p % 3], 1)

                def q_rows(at):
                    h, half, p = at
                    if exists(half):
                        if p == 0:
                            pe.wait_ge(blocks_landed[h], landed(h, half))
                        group_done(pe, onehot_t_made, half, p // 2)
                        done(pe, logit_made, before(h, half, p, 1))
                        pe.sem_inc(gate_pe, 1)
                        b = pe.value_load(blocks_in[0:1, h, 2 * p:2 * p + 1], min_val=0, max_val=NT - 1)
                        for k in range(2):
                            hot = onehot_t[:, p // 2, (2 * p + k) % 4 * P:((2 * p + k) % 4 + 1) * P]
                            pe.matmul(q_ps[:, k, :], hot, q_hi[:, ds(b * D, D)], start=True, stop=False)
                            mm = pe.matmul(q_ps[:, k, :], hot, q_lo[:, ds(b * D, D)], start=False, stop=True)
                        mm.then_inc(q_made[p % 3], 1)

                def sums(at):
                    h, half, p = at
                    if exists(half):
                        done(pe, onehot_made, at)
                        done(pe, kv_made, at)
                        done(pe, added, before(h, half, p, 1))
                        for k in range(2):
                            mm = pe.matmul(agg_ps[:, 0:D], onehot[:, p % 3, k, :], kv_in[:, 2 * p + k, D:2 * D],
                                           start=(k == 0), stop=(k == 1))
                        mm.then_inc(sum_made[p % 3], 1)

                def half_step(h, half):
                    for p in range(PAIRS):
                        products(h, half, p)
                        q_rows(before(h, half, p, Q_LAG))
                        sums(before(h, half, p, SUM_LAG))

                def drain(h, half):
                    for p in range(SUM_LAG):
                        if p < Q_LAG:
                            q_rows(before(h, half, 0, Q_LAG - p))
                        sums(before(h, half, 0, SUM_LAG - p))

                half_steps(pe, half_step, drain)

            @block.vector
            def _(dve):
                dve.wait_ge(s_w_hi, 2)
                dve.tensor_copy(ones_r[:, :], ones[0:2, :]).then_inc(s_w_parts, 1)
                dve.tensor_tensor(w_lo[:, :], w_in, w_hi[:, :].bitcast(F32), ALU.subtract).then_inc(s_w_parts, 1)
                dve.tensor_scalar(b_in, b_in, part_sel[:, 0:1], None, ALU.mult).then_inc(s_w_parts, 1)
                dve.wait_ge(s_w_parts, 3)
                dve.scalar_tensor_tensor(out=b_parts[:, :], in0=b_hi, scalar=part_sel[:, 1:2],
                                         in1=b_in, op0=ALU.mult, op1=ALU.add).then_inc(s_w_parts, 1)

                def products(h, half, p):
                    done(dve, dkv_silu, (h, half, p))
                    for k in range(2):
                        dve.wait_ge(kv_landed[2 * p + k], 16 * half + 16)
                    kv = kv_in[:, 2 * p:2 * p + 2, :]
                    dve.tensor_tensor(kv, kv, dkv[:, p % 3, :, :], ALU.mult).then_inc(kv_made[p % 3], 1)

                def factors(at):
                    h, half, p = at
                    if exists(half):
                        if p == 0:
                            dve.wait_ge(meta_landed[h], landed(h, half))
                        done(dve, logit_silu, at)
                        dve.tensor_tensor(factor[:, p % 3, :], gated[:, p % 3, :], meta_in[:, h, 1, 2 * p:2 * p + 2],
                                          ALU.mult).then_inc(factor_made[p % 3], 1)

                def one_hots(at):
                    h, half, p = at
                    if exists(half):
                        done(dve, factor_made, at)
                        done(dve, sum_made, before(h, half, p, 3))
                        for k in range(2):
                            ins = dve.tensor_scalar(onehot[:, p % 3, k, :], iota_free[:, :],
                                                    meta_in[:, h, 0, 2 * p + k:2 * p + k + 1],
                                                    factor[:, p % 3, k:k + 1], ALU.is_equal, ALU.mult)
                        ins.then_inc(onehot_made[p % 3], 1)

                def logits(h, half, p):
                    done(dve, q_made, (h, half, p))
                    done(dve, kv_made, (h, half, p))
                    for k in range(2):
                        kd = kv_in[:, 2 * p + k, 0:D]
                        ins = dve.tensor_tensor_reduce(kd, kd, q_ps[:, k, :], 1.0, 0.0, ALU.mult, ALU.add,
                                                       logit[:, p % 3, k:k + 1])
                    ins.then_inc(logit_made[p % 3], 1)

                def add(at):
                    h, half, p = at
                    if exists(half):
                        if p == 0:
                            dve.wait_ge(blocks_landed[h], landed(h, half))
                            dve.sem_inc(gate_dve, 1)
                        b = dve.value_load(blocks_in[0:1, h, 2 * p:2 * p + 1], min_val=0, max_val=NT - 1)
                        done(dve, sum_made, at)
                        done(dve, added, before(h, half, p, 1))
                        dve.tensor_tensor(agg[:, ds(b * D, D)], agg[:, ds(b * D, D)], agg_ps[:, 0:D],
                                          ALU.add).then_inc(added[p % 3], 1)

                def half_step(h, half):
                    for p in range(PAIRS):
                        products(h, half, p)
                        factors(before(h, half, p, 1))
                        add(before(h, half, p, SUM_LAG))
                        one_hots(before(h, half, p, 1))
                        logits(h, half, p)

                def drain(h, half):
                    factors(before(h, half, 0, 1))
                    one_hots(before(h, half, 0, 1))
                    for lag in range(SUM_LAG, 0, -1):
                        add(before(h, half, 0, lag))

                half_steps(dve, half_step, drain)

        q_room.close()
        qx = ctx.enter_context(nc.sbuf_tensor("qx", [P, NT * D], F32, side="right"))[:, :]

        next_phase()

        with ExitStack() as s4:
            def sb(name, shape, dt=F32):
                return s4.enter_context(nc.sbuf_tensor(name, shape, dt))

            def ps(name, shape):
                return s4.enter_context(nc.psum_tensor(name, shape, F32))

            wo = sb("wo", [P, DC, D])
            bo = sb("bo_sb", [P, D])
            agg_in = sb("agg_in", [P, 2, D])
            agg_t = sb("agg_t", [P, 2, D])
            tp = ps("tp4", [P, 2, 512])
            prod = ps("prod", [P, 2, 512])
            res_landed = [named(f"res_landed{k}") for k in range(7)]
            wo_landed = named("wo_landed")
            bo_landed = named("bo_landed")
            res_biased = named("res_biased")
            turned4 = [named(f"turned4_{k}") for k in range(2)]
            copied4 = [named(f"copied4_{k}") for k in range(2)]
            prod_made = [named(f"prod_made{k}") for k in range(2)]
            x2_made = [named(f"x2_made{k}") for k in range(2)]
            stats_made = named("stats_made4")
            staged = [named(f"staged{k}") for k in range(2)]
            gate4 = named("gate4")
            gate4p = named("gate4p")
            s_c4 = named("s_c4")
            s_var4 = named("s_var4")
            s_root4 = named("s_root4")
            block = s4.enter_context(nc.Block())
            G = NT // 7

            @block.sync
            def _(sp):
                sp.dma_start(wo[:, :, :], a["wo_t"].rearrange("(c p) n -> p c n", p=P)).then_inc(wo_landed, 16)
                sp.dma_start(bo[:, :], a["bo"].to_broadcast([P, D])).then_inc(bo_landed, 16)
                for k in range(7):
                    sp.dma_start(qx[:, k * G * D:(k + 1) * G * D].rearrange("p (t d) -> p t d", d=D),
                                 res_table[k * G * P:(k + 1) * G * P, :].rearrange("(t p) d -> p t d", p=P)) \
                        .then_inc(res_landed[k], 16)

            @block.gpsimd
            def _(pool):
                pool.wait_ge(bo_landed, 16)
                for k in range(7):
                    pool.wait_ge(res_landed[k], 16)
                    pool.sem_inc(gate4p, 1)
                    with pool.Fori(k * G, (k + 1) * G) as t:
                        pool.tensor_tensor(qx[:, ds(t * D, D)], qx[:, ds(t * D, D)], bo[:, :], ALU.add) \
                            .then_inc(res_biased, 1)

            @block.scalar
            def _(act):
                def stage(t, s, n, last):
                    slot_free(act, turned4[s], n)
                    act.sem_inc(gate4, 1)
                    act.activation(agg_in[:, s, :], agg[:, ds(t * D, D)], ACT.Copy).then_inc(staged[s], 1)

                over_tiles(act, NT, stage)
                norm_roots(act, s_root4, s_var4)

            @block.tensor
            def _(pe):
                pe.wait_ge(wo_landed, 16)

                def transposes(s, n):
                    slot_free(pe, copied4[s], n)
                    pe.wait_ge(staged[s], n + 1)
                    for k in range(DC):
                        mm = pe.transpose(tp[:, s, k * P:(k + 1) * P], agg_in[:, s, k * P:(k + 1) * P], ident[:, :])
                    mm.then_inc(turned4[s], 1)

                def product(t, s, n, last):
                    if not last:
                        transposes(1 - s, n + s)
                    slot_free(pe, x2_made[s], n)
                    pe.wait_ge(copied4[s], n + 1)
                    for k in range(DC):
                        mm = pe.matmul(prod[:, s, 0:D], agg_t[:, s, k * P:(k + 1) * P], wo[:, k, :], start=(k == 0),
                                       stop=(k == DC - 1))
                    mm.then_inc(prod_made[s], 1)

                transposes(0, 0)
                over_tiles(pe, NT, product)

            @block.vector
            def _(dve):
                c = Chain(dve, s_c4)

                def copy(s, n):
                    slot_free(dve, prod_made[s], n)
                    dve.wait_ge(turned4[s], n + 1)
                    dve.tensor_copy(agg_t[:, s, :], tp[:, s, 0:D]).then_inc(copied4[s], 1)

                def add(t, s, n, last):
                    if not last:
                        copy(1 - s, n + s)
                    dve.wait_ge(res_biased, t + 1)
                    dve.wait_ge(prod_made[s], n + 1)
                    dve.tensor_tensor(qx[:, ds(t * D, D)], qx[:, ds(t * D, D)], prod[:, s, 0:D], ALU.add) \
                        .then_inc(x2_made[s], 1)
                    dve.wait_ge(x2_made[s], n + 1)
                    dve.bn_stats(stats[:, ds(t, 1), :].rearrange("p a b -> p (a b)"), qx[:, ds(t * D, D)]) \
                        .then_inc(stats_made, 1)

                copy(0, 0)
                over_tiles(dve, NT, add)
                dve.wait_ge(stats_made, NT)
                norm_scales(dve, s_root4, c, s_var4, 0)

        next_phase()

        agg_room.close()

        with ExitStack() as s5:
            def sb(name, shape, dt=F32):
                return s5.enter_context(nc.sbuf_tensor(name, shape, dt))

            def ps(name, shape):
                return s5.enter_context(nc.psum_tensor(name, shape, F32))

            zero = sb("zero", [P, 7 * D])
            wr = sb("wr_sb", [P, DC, NE])
            br = sb("br_sb", [P, NE])
            z = sb("z", [P, 2, D])
            z_t = sb("z_t", [P, 2, D])
            tri = sb("tri", [P, P])
            down = sb("down", [P, NE])
            rows = sb("rows", [P, NT])
            numbers = sb("numbers", [P, SGS + 1])
            lg = sb("lg", [P, NT, NE])
            hot1 = sb("hot1", [P, NT, NE])
            hot2 = sb("hot2", [P, NT, NE])
            work = sb("work", [P, NT, NE])
            cum = sb("cum", [P, NE, NT])
            cmp = sb("cmp", [P, NE, NT])
            over = sb("over", [1, SGS + 1, NE - 1])
            m1 = sb("m1", [P, NT])
            m2 = sb("m2", [P, NT])
            d12 = sb("d12", [P, NT])
            n_groups = sb("n_groups", [P, NE])
            end = sb("end", [P, NE])
            base = sb("base", [P, NE])
            slot_f = sb("slot_f", [P, NT, 2])
            expert_f = sb("expert_f", [1, SGS + 1])
            bounds_f = sb("bounds_f", [1, NE + 2])
            tp = ps("tp5", [P, 2, 512])
            lg_ps = ps("lg_ps", [P, 512])
            rank = ps("rank", [P, 512])
            total = ps("total", [P, 512])
            zero_made = named("zero_made")
            filled = named("filled")
            wr_landed = named("wr_landed")
            z_made = [named(f"z_made{k}") for k in range(2)]
            turned5 = [named(f"turned5_{k}") for k in range(2)]
            copied5 = [named(f"copied5_{k}") for k in range(2)]
            lg_made = [named(f"lg_made{k}") for k in range(2)]
            gate5 = named("gate5")
            gap_made = named("gap_made")
            exp_made = named("exp_made")
            hot_made = named("hot_made")
            ranks_made = named("ranks_made")
            const5 = named("const5")
            s_c5 = named("s_c5")
            block = s5.enter_context(nc.Block())

            @block.sync
            def _(sp):
                sp.dma_start(wr[:, :, :], a["wr"].rearrange("(c p) e -> p c e", p=P)).then_inc(wr_landed, 16)
                sp.dma_start(br[:, :], a["br"].to_broadcast([P, NE])).then_inc(wr_landed, 16)
                sp.wait_ge(zero_made, 1)
                for k in range(ZERO_FILLS):
                    n = min(7, 2 * (SGS + 2) - 7 * k)
                    sp.dma_start(slot_x[7 * k * P:(7 * k + n) * P, :].rearrange("(p r) d -> p (r d)", p=P),
                                 zero[:, 0:n * D]).then_inc(filled, 16)
                for k in range(NT, SGS):
                    sp.dma_start(slot_y[k * G256:(k + 1) * G256, :].rearrange("(p r) d -> p (r d)", p=P),
                                 zero[:, 0:2 * D]).then_inc(filled, 16)
                sp.wait_ge(filled, 16 * (ZERO_FILLS + SGS - NT))

            @block.gpsimd
            def _(pool):
                pool.memset(zero[:, :], 0.0).then_inc(zero_made, 1)
                c = Chain(pool, const5)
                c(pool.affine_select(out=tri[:, :], in_=ones[:, :], compare_op=ALU.is_gt, fill=0.0, base=0,
                                     pattern=[[1, P]], channel_multiplier=-1))
                c(pool.iota(down[:, :], pattern=[[-1, NE]], base=NE, channel_multiplier=0,
                            allow_small_or_imprecise_dtypes=True))
                c(pool.iota(rows[:, :], pattern=[[G256, NT]], base=0, channel_multiplier=0,
                            allow_small_or_imprecise_dtypes=True))
                c(pool.iota(numbers[:, :], pattern=[[1, SGS + 1]], base=0, channel_multiplier=0,
                            allow_small_or_imprecise_dtypes=True))

            @block.scalar
            def _(act):
                def norm(t, s, n, last):
                    slot_free(act, turned5[s], n)
                    act.sem_inc(gate5, 1)
                    act.activation(z[:, s, :], qx[:, ds(t * D, D)], ACT.Identity, scale=rstd[:, ds(t, 1)],
                                   bias=bias_r[:, ds(t, 1)]).then_inc(z_made[s], 1)

                over_tiles(act, NT, norm)
                act.wait_ge(gap_made, 1)
                act.activation(m2[:, :], m2[:, :], ACT.Exp).then_inc(exp_made, 1)

            @block.tensor
            def _(pe):
                pe.wait_ge(wr_landed, 32)

                def transposes(s, n):
                    slot_free(pe, copied5[s], n)
                    pe.wait_ge(z_made[s], n + 1)
                    for k in range(DC):
                        mm = pe.transpose(tp[:, s, k * P:(k + 1) * P], z[:, s, k * P:(k + 1) * P], ident[:, :])
                    mm.then_inc(turned5[s], 1)

                def logits(t, s, n, last):
                    if not last:
                        transposes(1 - s, n + s)
                    pe.wait_ge(copied5[s], n + 1)
                    o = lg_ps[:, ds(t * NE, NE)]
                    for k in range(DC):
                        mm = pe.matmul(o, z_t[:, s, k * P:(k + 1) * P], wr[:, k, :], start=(k == 0),
                                       stop=(k == DC - 1))
                    mm.then_inc(lg_made[s], 1)

                transposes(0, 0)
                over_tiles(pe, NT, logits)
                pe.wait_ge(hot_made, 1)
                pe.wait_ge(const5, 4)
                both = work[:, :, :].rearrange("p t e -> p (t e)")
                pe.matmul(rank[:, 0:NT * NE], tri[:, :], both, start=True, stop=True)
                pe.matmul(total[:, 0:NT * NE], ones[:, :], both, start=True, stop=True).then_inc(ranks_made, 1)

            @block.vector
            def _(dve):
                c = Chain(dve, s_c5)

                def copy(t, s, n, last):
                    slot_free(dve, lg_made[s], n)
                    dve.wait_ge(turned5[s], n + 1)
                    dve.tensor_copy(z_t[:, s, :], tp[:, s, 0:D]).then_inc(copied5[s], 1)

                over_tiles(dve, NT, copy)
                dve.wait_ge(lg_made[0], NT // 2 + 1)
                dve.wait_ge(lg_made[1], NT // 2)
                dve.wait_ge(const5, 4)
                dve.wait_ge(wr_landed, 32)
                c(dve.tensor_tensor(lg[:, :, :], lg_ps[:, 0:NT * NE].rearrange("p (t e) -> p t e", e=NE),
                                    br[:, :].unsqueeze(1).to_broadcast([P, NT, NE]), ALU.add))
                down_b = down[:, :].unsqueeze(1).to_broadcast([P, NT, NE])

                def wide(v):
                    return v[:, :].unsqueeze(2).to_broadcast([P, NT, NE])

                def best(m, hot):
                    c(dve.tensor_reduce(m[:, :], lg[:, :, :], AX, ALU.max))
                    c(dve.tensor_tensor(work[:, :, :], lg[:, :, :], wide(m), ALU.is_ge))
                    c(dve.tensor_tensor(work[:, :, :], work[:, :, :], down_b, ALU.mult))
                    c(dve.tensor_reduce(d12[:, :], work[:, :, :], AX, ALU.max))
                    c(dve.tensor_tensor(hot[:, :, :], down_b, wide(d12), ALU.is_equal))

                best(m1, hot1)
                c(dve.scalar_tensor_tensor(out=lg[:, :, :], in0=hot1[:, :, :], scalar=-3.0e38, in1=lg[:, :, :],
                                           op0=ALU.mult, op1=ALU.add))
                best(m2, hot2)
                c(dve.tensor_tensor(work[:, :, :], hot1[:, :, :], hot2[:, :, :], ALU.add))
                dve.sem_inc(hot_made, 1)
                c(dve.tensor_tensor(m2[:, :], m2[:, :], m1[:, :], ALU.subtract))
                dve.sem_inc(gap_made, 1)
                dve.wait_ge(exp_made, 1)
                c(dve.tensor_scalar(m1[:, :], m2[:, :], 1.0, None, ALU.add))
                c(dve.reciprocal(w_top[:, :, 0], m1[:, :]))
                c(dve.tensor_tensor(w_top[:, :, 1], m2[:, :], w_top[:, :, 0], ALU.mult))
                dve.wait_ge(ranks_made, 1)
                tot = total[:, 0:NT * NE].rearrange("p (t e) -> p t e", e=NE)
                for e in range(NE):
                    c(dve.tensor_tensor_scan(cum[:, e, :], ones[:, 0:NT], tot[:, :, e], 0.0, ALU.mult, ALU.add))
                c(dve.tensor_tensor(cmp[:, :, :], cum[:, :, NT - 1:NT].to_broadcast([P, NE, NT]),
                                    rows[:, :].unsqueeze(1).to_broadcast([P, NE, NT]), ALU.is_gt))
                c(dve.tensor_reduce(n_groups[:, :], cmp[:, :, :], AX, ALU.add))
                c(dve.tensor_scalar(n_groups[:, :], n_groups[:, :], 1.0, None, ALU.max))
                c(dve.tensor_tensor_scan(end[:, :], ones[:, 0:NE], n_groups[:, :], 0.0, ALU.mult, ALU.add))
                c(dve.tensor_tensor(base[:, :], end[:, :], n_groups[:, :], ALU.subtract))
                c(dve.tensor_scalar(base[:, :], base[:, :], float(G256), None, ALU.mult))
                c(dve.tensor_tensor(work[:, :, :], cum[:, :, :].rearrange("p e t -> p t e"), tot, ALU.subtract))
                c(dve.tensor_tensor(work[:, :, :], work[:, :, :],
                                    rank[:, 0:NT * NE].rearrange("p (t e) -> p t e", e=NE), ALU.add))
                c(dve.tensor_tensor(work[:, :, :], work[:, :, :],
                                    base[:, :].unsqueeze(1).to_broadcast([P, NT, NE]), ALU.add))
                for k, hot in enumerate((hot1, hot2)):
                    c(dve.tensor_tensor(hot[:, :, :], hot[:, :, :], work[:, :, :], ALU.mult))
                    c(dve.tensor_reduce(slot_f[:, :, k], hot[:, :, :], AX, ALU.add))
                c(dve.tensor_copy(slot_i[:, :, :], slot_f[:, :, :]))
                c(dve.tensor_tensor(over[:, :, :], numbers[0:1, :].unsqueeze(2).to_broadcast([1, SGS + 1, NE - 1]),
                                    end[0:1, 0:NE - 1].unsqueeze(1).to_broadcast([1, SGS + 1, NE - 1]), ALU.is_ge))
                c(dve.tensor_reduce(expert_f[:, :], over[:, :, :], AX, ALU.add))
                c(dve.tensor_copy(expert_i[:, :], expert_f[:, :]))
                c(dve.memset(bounds_f[:, :], 0.0))
                c(dve.tensor_copy(bounds_f[:, 2:], end[0:1, :]))
                c(dve.tensor_copy(bounds[:, :], bounds_f[:, :]))

        next_phase()

        raw_room = ctx.enter_context(ExitStack())

        def late(name, shape, dt=F32):
            return raw_room.enter_context(nc.sbuf_tensor(name, shape, dt))

        raw = [late("w1_raw", [P, DC * HID]), late("w2_raw", [P, KC * D])]
        w1_hi, w1_lo = ([late(f"w1_{x}{s}", [P, DC, HID], F32R) for s in range(2)] for x in ("hi", "lo"))
        w2_hi, w2_lo = ([late(f"w2_{x}{s}", [P, KC, D], F32R) for s in range(2)] for x in ("hi", "lo"))

        gains = late("gains", [P, NE * DC])
        offs = late("offs", [P, NE * DC])
        b1_cols = late("b1_cols", [P, NE * KC])
        b2_rows = late("b2_rows", [P, NE * D])

        def load_weights(eng, e, landed):
            for m, name in enumerate(("w1", "w2")):
                eng.dma_start(raw[m][:, :].rearrange("p (c n) -> p c n", c=(DC, KC)[m]),
                              a[name][ds(e, 1)].rearrange("a (c p) n -> p (a c) n", p=P)).then_inc(landed, 16)

        def flat_parts(s):
            return [[v[:, :, :].rearrange("p c n -> p (c n)") for v in pair]
                    for pair in ((w1_hi[s], w1_lo[s]), (w2_hi[s], w2_lo[s]))]

        with ExitStack() as s6:
            xn = s6.enter_context(nc.sbuf_tensor("xn", [P, 7, D], F32))
            slot_s = s6.enter_context(nc.sbuf_tensor("slot_s", [P, 7, 2], I32))
            xn_made = [named(f"xn_made{k}") for k in range(7)]
            scattered = [named(f"scattered{k}") for k in range(7)]
            first_landed = named("first_landed")
            small_landed = named("small_landed")
            first_split = named("first_split")
            gate6a = named("gate6a")
            gate6p = named("gate6p")
            block = s6.enter_context(nc.Block())

            @block.sync
            def _(sp):
                for tile, name in ((gains[:, :], "ffn_g"), (offs[:, :], "ffn_b"), (b1_cols[:, :], "b1")):
                    sp.dma_start(tile, a[name]).then_inc(small_landed, 16)
                sp.dma_start(b2_rows[:, :], a["b2"].to_broadcast([P, NE * D])).then_inc(small_landed, 16)
                for e in range(2):
                    if e:
                        sp.wait_ge(first_split, 4)
                    load_weights(sp, e, first_landed)
                sp.wait_ge(small_landed, 64)

            @block.vector
            def _(dve):
                c = Chain(dve, first_split)
                for e in range(2):
                    dve.wait_ge(first_landed, 32 * e + 32)
                    for m, (hi, lo) in enumerate(flat_parts(e)):
                        c(dve.tensor_copy(hi, raw[m][:, :]))
                        c(dve.tensor_tensor(lo, raw[m][:, :], hi.bitcast(F32), ALU.subtract))

            @block.scalar
            def _(act):
                def norm(t, s, n):
                    slot_free(act, scattered[s], n, 32)
                    act.sem_inc(gate6a, 1)
                    act.activation(xn[:, s, :], qx[:, ds(t * D, D)], ACT.Identity, scale=rstd2[:, ds(t, 1)],
                                   bias=bias_s[:, ds(t, 1)]).then_inc(xn_made[s], 1)
                    act.activation(slot_s[:, s, :], slot_i[:, ds(t, 1), :].rearrange("p a k -> p (a k)"), ACT.Copy) \
                        .then_inc(xn_made[s], 1)

                over_sevens(act, norm)

            @block.gpsimd
            def _(pool):
                def scatter(t, s, n):
                    pool.wait_ge(xn_made[s], 2 * n + 2)
                    pool.sem_inc(gate6p, 1)
                    for k in range(2):
                        pool.indirect_dma_start(slot_x, bass.IndirectOffsetOnAxis(ap=slot_s[:, s, k:k + 1], axis=0),
                                                xn[:, s, :], None).then_inc(scattered[s], 16)

                over_sevens(pool, scatter)
                for s in range(7):
                    pool.wait_ge(scattered[s], 32 * (NT // 7))

        next_phase()

        with ExitStack() as s7:
            def sb(name, shape, dt=F32):
                return s7.enter_context(nc.sbuf_tensor(name, shape, dt))

            def ps(name, shape):
                return s7.enter_context(nc.psum_tensor(name, shape, F32))

            xs = sb("xs", [P, 2, D])
            xe = sb("xe", [P, DC, G256])
            x_hi = sb("x_hi", [P, DC, G256], F32R)
            x_lo = sb("x_lo", [P, DC, G256], F32R)
            h = sb("h", [P, KC, G256])
            h_hi = sb("h_hi", [P, KC, G256], F32R)
            h_lo = sb("h_lo", [P, KC, G256], F32R)
            y = sb("y", [P, 2, D])
            warm = sb("warm", [P, 1])
            xt_ps = ps("xt_ps", [P, DC, G256])
            h_ps = ps("h_ps", [P, KC, G256])
            y_ps = ps("y_ps", [P, 2, 512])
            BANKS = KC // 2

            raw_landed = named("raw_landed")
            weights_split = named("weights_split")
            xs_landed = named("xs_landed")
            x_turned = named("x_turned")
            xe_made = named("xe_made")
            x_rounded = named("x_rounded")
            x_split = named("x_split")
            h_made = named("h_made")
            gelu_made = named("gelu_made")
            h_rounded = named("h_rounded")
            h_split = named("h_split")
            y_made = named("y_made")
            y_taken = named("y_taken")
            y_stored = named("y_stored")
            gate7p, gate7a, gate7w = named("gate7p"), named("gate7a"), named("gate7w")
            gate7d, gate7s = named("gate7d"), named("gate7s")
            block = s7.enter_context(nc.Block())

            def groups(eng):
                return eng.value_load(bounds[0:1, NE + 1:NE + 2], min_val=1, max_val=SGS)

            def expert(eng, g):
                return eng.value_load(expert_i[0:1, ds(g, 1)], min_val=0, max_val=NE - 1)

            @block.gpsimd
            def _(pool):
                pool.sem_inc(weights_split, 8)

                def split(e, s):
                    freed = pool.value_load(bounds[0:1, ds(e, 1)], min_val=0, max_val=SGS)
                    pool.wait_ge(weights_split, 4 * e)
                    pool.sem_inc(gate7w, 1)
                    load_weights(pool, e, raw_landed)
                    pool.wait_ge(y_made, freed + 1)
                    pool.sem_inc(gate7w, 1)
                    pool.wait_ge(raw_landed, 32 * e - 32)
                    pool.sem_inc(gate7w, 1)
                    for m, (hi, lo) in enumerate(flat_parts(s)):
                        pool.tensor_copy(hi, raw[m][:, :]).then_inc(weights_split, 1)
                        pool.wait_ge(weights_split, 4 * e + (2 * m + 1))
                        pool.sem_inc(gate7w, 1)
                        pool.tensor_tensor(lo, raw[m][:, :], hi.bitcast(F32), ALU.subtract) \
                            .then_inc(weights_split, 1)

                with pool.Fori(1, NE // 2) as k:
                    for s in range(2):
                        split(2 * k + s, s)

            @block.sync
            def _(sp):
                sp.sem_inc(y_stored, 16)

                def load(g):
                    sp.dma_start(xs[:, :, :], slot_x[ds(g * G256, G256), :].rearrange("(k p) d -> p k d", p=P)) \
                        .then_inc(xs_landed, 16)

                load(0)
                sp.wait_ge(x_turned, 1)
                load(1)
                n = groups(sp)
                with sp.Fori(0, n) as g:
                    sp.wait_ge(x_turned, g + 2)
                    sp.sem_inc(gate7s, 1)
                    load(g + 2)
                    sp.wait_ge(y_taken, g + 2)
                    sp.sem_inc(gate7s, 1)
                    sp.dma_start(slot_y[ds(g * G256, G256), :].rearrange("(k p) d -> p k d", p=P), y[:, :, :]) \
                        .then_inc(y_stored, 16)
                sp.wait_ge(y_stored, 16 * n + 16)
                sp.sem_inc(gate7s, 1)
                sp.wait_ge(xs_landed, 16 * n + 32)
                sp.sem_inc(gate7s, 1)

            @block.tensor
            def _(pe):
                pe.sem_inc(y_made, 1)

                def turn(g):
                    pe.wait_ge(xs_landed, 16 * g + 16)
                    for k in range(2):
                        for c in range(DC):
                            mm = pe.transpose(xt_ps[:, c, k * P:(k + 1) * P], xs[:, k, c * P:(c + 1) * P], ident[:, :])
                    mm.then_inc(x_turned, 1)

                def layer1(g, s):
                    pe.wait_ge(x_split, g + 1)
                    for j in range(KC):
                        if j == KC // 2:
                            turn(g + 1)
                        parts = [(w, x, c) for w, x in ((w1_hi[s], x_hi), (w1_hi[s], x_lo), (w1_lo[s], x_hi))
                                 for c in range(DC)]
                        for i, (w, x, c) in enumerate(parts):
                            mm = pe.matmul(h_ps[:, j, :], w[:, c, j * P:(j + 1) * P], x[:, c, :],
                                           start=(i == 0), stop=(i == len(parts) - 1))
                        if j % 2:
                            mm.then_inc(h_made, 1)

                def layer2(g, s):
                    pe.wait_ge(y_taken, g + 1)
                    for j in range(KC):
                        if j % 2 == 0:
                            pe.wait_ge(h_split, BANKS * g + (j // 2 + 1))
                        parts = ((h_hi, w2_hi[s]), (h_hi, w2_lo[s]), (h_lo, w2_hi[s]))
                        for k in range(2):
                            for i, (x, w) in enumerate(parts):
                                mm = pe.matmul(y_ps[:, k, 0:D], x[:, j, k * P:(k + 1) * P], w[:, j, :],
                                               start=(j == 0 and i == 0), stop=(j == KC - 1 and i == 2))
                    mm.then_inc(y_made, 1)

                turn(0)
                with pe.Fori(0, NE // 2) as pair:
                    for s in range(2):
                        e = 2 * pair + s
                        pe.wait_ge(weights_split, 4 * e + 4)
                        pe.sem_inc(gate7p, 1)
                        first = pe.value_load(bounds[0:1, ds(e + 1, 1)], min_val=0, max_val=SGS)
                        end = pe.value_load(bounds[0:1, ds(e + 2, 1)], min_val=0, max_val=SGS)
                        with pe.Fori(first, end) as g:
                            layer1(g, s)
                            layer2(g, s)

            @block.scalar
            def _(act):
                def round_x(g):
                    act.wait_ge(xe_made, DC * g + DC)
                    act.sem_inc(gate7a, 1)
                    act.activation(x_hi[:, :, :], xe[:, :, :], ACT.Copy).then_inc(x_rounded, 1)

                round_x(0)
                act.activation(warm[:, :], b1_cols[:, 0:1], ACT.Gelu)
                n = groups(act)
                with act.Fori(0, n) as g:
                    e = expert(act, g)
                    act.wait_ge(y_made, g + 1)
                    act.sem_inc(gate7a, 1)
                    for b in range(BANKS):
                        act.wait_ge(h_made, BANKS * g + (b + 1))
                        act.sem_inc(gate7a, 1)
                        for j in (2 * b, 2 * b + 1):
                            act.activation(h[:, j, :], h_ps[:, j, :], ACT.Gelu,
                                           bias=b1_cols[:, ds(e * KC + j, 1)]).then_inc(gelu_made, 1)
                        act.wait_ge(gelu_made, KC * g + (2 * b + 2))
                        act.sem_inc(gate7a, 1)
                        act.activation(h_hi[:, 2 * b:2 * b + 2, :], h[:, 2 * b:2 * b + 2, :], ACT.Copy) \
                            .then_inc(h_rounded, 1)
                    round_x(g + 1)

            @block.vector
            def _(dve):
                dve.sem_inc(y_taken, 1)

                def norm_x(g, e):
                    dve.wait_ge(x_turned, g + 1)
                    for c in range(DC):
                        dve.tensor_scalar(xe[:, c, :], xt_ps[:, c, :], gains[:, ds(e * DC + c, 1)],
                                          offs[:, ds(e * DC + c, 1)], ALU.mult, ALU.add).then_inc(xe_made, 1)

                def split_x(g):
                    dve.wait_ge(x_rounded, g + 1)
                    dve.tensor_tensor(x_lo[:, :, :], xe[:, :, :], x_hi[:, :, :].bitcast(F32), ALU.subtract) \
                        .then_inc(x_split, 1)

                norm_x(0, expert(dve, 0))
                split_x(0)
                n = groups(dve)
                with dve.Fori(0, n) as g:
                    following = expert(dve, g + 1)
                    for b in range(BANKS):
                        if b == 2:
                            norm_x(g + 1, following)
                        dve.wait_ge(h_rounded, BANKS * g + (b + 1))
                        dve.tensor_tensor(h_lo[:, 2 * b:2 * b + 2, :], h[:, 2 * b:2 * b + 2, :],
                                          h_hi[:, 2 * b:2 * b + 2, :].bitcast(F32), ALU.subtract) \
                            .then_inc(h_split, 1)
                    split_x(g + 1)
                    e = expert(dve, g)
                    dve.wait_ge(y_stored, 16 * g + 16)
                    dve.wait_ge(y_made, g + 2)
                    dve.tensor_tensor(y[:, :, :], y_ps[:, :, 0:D],
                                      b2_rows[:, ds(e * D, D)].unsqueeze(1).to_broadcast([P, 2, D]), ALU.add) \
                        .then_inc(y_taken, 1)

        next_phase()

        raw_room.close()
        with ExitStack() as s8:
            yg = s8.enter_context(nc.sbuf_tensor("yg", [P, 7, 2, D], F32))
            o = s8.enter_context(nc.sbuf_tensor("o", [P, 7, D], F32))
            half_o = s8.enter_context(nc.sbuf_tensor("half_o", [P, 7, D], F32))
            slot_g = s8.enter_context(nc.sbuf_tensor("slot_g", [P, 7, 2], I32))
            slots_ready = [named(f"slots_ready{k}") for k in range(7)]
            y_back = [[named(f"y_back{k}{j}") for j in range(2)] for k in range(7)]
            halved = [named(f"halved{k}") for k in range(7)]
            o_made = [named(f"o_made{k}") for k in range(7)]
            o_stored = [named(f"o_stored{k}") for k in range(7)]
            gate8a = named("gate8a")
            gate8p = named("gate8p")
            block = s8.enter_context(nc.Block())

            @block.scalar
            def _(act):
                def fix_slots(t, s, n):
                    for k in range(2):
                        slot_free(act, y_back[s][k], n, 16)
                    act.sem_inc(gate8a, 1)
                    act.activation(slot_g[:, s, :], slot_i[:, ds(t, 1), :].rearrange("p a k -> p (a k)"), ACT.Copy) \
                        .then_inc(slots_ready[s], 1)

                over_sevens(act, fix_slots)

            @block.gpsimd
            def _(pool):
                def gather(t, s, n):
                    slot_free(pool, o_made[s], n)
                    pool.sem_inc(gate8p, 1)
                    pool.wait_ge(slots_ready[s], n + 1)
                    pool.sem_inc(gate8p, 1)
                    for k in range(2):
                        pool.indirect_dma_start(yg[:, s, k, :], None, slot_y,
                                                bass.IndirectOffsetOnAxis(ap=slot_g[:, s, k:k + 1], axis=0)) \
                            .then_inc(y_back[s][k], 16)

                over_sevens(pool, gather)

            @block.vector
            def _(dve):
                def combine(t, s, n):
                    slot_free(dve, o_stored[s], n, 16)
                    for k, (src_t, dst_t, made) in enumerate(((qx[:, ds(t * D, D)], half_o[:, s, :], halved[s]),
                                                              (half_o[:, s, :], o[:, s, :], o_made[s]))):
                        dve.wait_ge(y_back[s][k], 16 * n + 16)
                        dve.scalar_tensor_tensor(out=dst_t, in0=yg[:, s, k, :],
                                                 scalar=w_top[:, ds(t, 1), k:k + 1].rearrange("p a k -> p (a k)"),
                                                 in1=src_t, op0=ALU.mult, op1=ALU.add).then_inc(made, 1)
                        if k == 0:
                            dve.wait_ge(halved[s], n + 1)

                over_sevens(dve, combine)

            @block.sync
            def _(sp):
                def store(t, s, n):
                    sp.wait_ge(o_made[s], n + 1)
                    sp.dma_start(out[ds(t * P, P), :], o[:, s, :]).then_inc(o_stored[s], 16)

                over_sevens(sp, store)
                for s in range(7):
                    sp.wait_ge(o_stored[s], 16 * (NT // 7))


def kernel(x, src, dst, edge_attr_64, edge_weight, L0_gnn_ln_g, L0_gnn_ln_b, L0_gnn_Wq, L0_gnn_bq, L0_gnn_Wk,
           L0_gnn_bk, L0_gnn_Wv, L0_gnn_bv, L0_gnn_Wo, L0_gnn_bo, L0_gnn_Wdk, L0_gnn_bdk, L0_gnn_Wdv, L0_gnn_bdv,
           L0_ffn_Wr, L0_ffn_br, L0_ffn_ln_g, L0_ffn_ln_b, L0_ffn_W1, L0_ffn_b1, L0_ffn_W2, L0_ffn_b2):
    import numpy as np
    import concourse.bacc as bacc
    from concourse.bass_utils import run_bass_kernel_spmd

    def padded(v, rows, fill=0):
        v = np.asarray(v)
        return np.concatenate([v, np.full((rows - v.shape[0],) + v.shape[1:], fill, v.dtype)])

    def columns(v):
        v = np.asarray(v)
        return np.moveaxis(v.reshape(v.shape[:-1] + (DC, P)), -1, 0)

    edges = ET * P
    arrays = {
        "x": padded(x, NT * P),
        "src": padded(src, edges).reshape(ET, P),
        "dst": padded(dst, edges, N - 1).reshape(ET, P),
        "edge_weight": padded(edge_weight, edges, CUT).reshape(ET, P),
        "edge_attr_t": np.tile(padded(edge_attr_64, edges + P).reshape(ET + 1, P, R).transpose(0, 2, 1), (1, 2, 1)),
        "wqkv_t": np.concatenate([np.asarray(w).T for w in (L0_gnn_Wk, L0_gnn_Wv, L0_gnn_Wq)], 1),
        "bqkv": np.concatenate([np.asarray(b) for b in (L0_gnn_bk, L0_gnn_bv, L0_gnn_bq)])[None],
        "gnn_g": columns(L0_gnn_ln_g),
        "gnn_b": columns(L0_gnn_ln_b),
        "wd_t": np.tile(np.concatenate([np.asarray(L0_gnn_Wdk).T, np.asarray(L0_gnn_Wdv).T], 1), (2, 1)),
        "bd": np.tile(np.concatenate([np.asarray(L0_gnn_bdk), np.asarray(L0_gnn_bdv)])[None], (2, 1)),
        "wo_t": np.asarray(L0_gnn_Wo).T,
        "bo": np.asarray(L0_gnn_bo)[None],
        "wr": L0_ffn_Wr,
        "br": np.asarray(L0_ffn_br)[None],
        "ffn_g": columns(L0_ffn_ln_g).reshape(P, NE * DC),
        "ffn_b": columns(L0_ffn_ln_b).reshape(P, NE * DC),
        "w1": L0_ffn_W1,
        "b1": np.asarray(L0_ffn_b1).reshape(NE, KC, P).transpose(2, 0, 1).reshape(P, NE * KC),
        "w2": L0_ffn_W2,
        "b2": np.asarray(L0_ffn_b2).reshape(1, NE * D),
        "part_sel": np.array([[0, 1], [1, -1]], np.float32),
    }
    arrays = {f"in_{name}": np.ascontiguousarray(v) for name, v in arrays.items()}
    nc = bacc.Bacc("TRN2", target_bir_lowering=False, num_devices=1)
    access = {name[3:]: nc.dram_tensor(name, v.shape, mybir.dt.from_np(v.dtype), kind="ExternalInput").ap()
              for name, v in arrays.items()}
    out = nc.dram_tensor("out_x", (NT * P, D), F32, kind="ExternalOutput").ap()
    build_program(nc, access, out)
    result = run_bass_kernel_spmd(nc, [arrays], core_ids=[0])
    return result.results[0]["out_x"][:N]
```
